# Optimizing a Trainium2 kernel written in Bass

```python
import numpy as np
import jax
import jax.numpy as jnp

def _softmax(x, axis=-1):
    return jax.nn.softmax(x, axis=axis)
def _gelu(x):
    return jax.nn.gelu(x, approximate=True)
def _silu(x):
    return jax.nn.silu(x)
def _sigmoid(x):
    return jax.nn.sigmoid(x)
def _layernorm(x, axis=-1, eps=1e-5):
    m = jnp.mean(x, axis=axis, keepdims=True)
    v = jnp.var(x, axis=axis, keepdims=True)
    return (x - m) / jnp.sqrt(v + eps)
def _scatter_add(tgt, idx, src, axis=0):
    return tgt.at[idx].add(src)
def _segment_sum(src, seg, n):
    return jax.ops.segment_sum(src, seg, n)

kernel_name = 'mk_adj_resnorm_d4_adj_128_732a51'

def setup_inputs(seed: int = 0):
    np.random.seed(seed)
    _w = jnp.asarray
    def _rec_inputs():
        import jax
        import jax.numpy as jnp
        _gk = jax.random.key(seed)
        x = -9.806e-05 + 1 * jax.random.normal(jax.random.fold_in(_gk, 1), (8192, 128), jnp.float32)
        _a = jax.random.bernoulli(jax.random.fold_in(_gk, 2), 0.00390625, (8192, 8192))
        _a = jnp.logical_or(_a, jnp.swapaxes(_a, -1, -2))
        _a = jnp.logical_or(_a, jnp.eye(8192, dtype=bool))
        adj = _a.astype(jnp.int32)
        return x, adj
    x, adj = _rec_inputs()
    def _L0_gnn_setup():
        import jax, jax.numpy as jnp
        import numpy as np
        N, IN_DIM, OUT_DIM, H = (4096, 128, 128, 4)
        HEAD_DIM = OUT_DIM // H
        NEG_SLOPE = 0.2
        key = jax.random.key(seed)
        k1, k2, k3, k4, k5 = jax.random.split(key, 5)
        x = jax.random.normal(k1, (N, IN_DIM), dtype=jnp.float32)
        adj = jax.random.randint(k2, (N, N), 0, 2, dtype=jnp.int32)
        W = jax.random.normal(k3, (OUT_DIM, IN_DIM), dtype=jnp.float32) * (1.0 / np.sqrt(IN_DIM))
        attn_src = jax.random.normal(k4, (1, H, HEAD_DIM), dtype=jnp.float32) * 0.1
        attn_dst = jax.random.normal(k5, (1, H, HEAD_DIM), dtype=jnp.float32) * 0.1
        return {'x': x, 'adj': adj, 'W': W, 'attn_src': attn_src, 'attn_dst': attn_dst}
    _L0_gnn_all = _L0_gnn_setup()
    _L0_gnn_in = {k: v for k, v in _L0_gnn_all.items() if k in ('W', 'attn_src', 'attn_dst', )}
    del _L0_gnn_all

    def _L1_gnn_setup():
        import jax, jax.numpy as jnp
        import numpy as np
        from jax import lax
        N = 8192
        D = 128
        CHUNK = 128
        key = jax.random.key(seed)
        k1, k2 = jax.random.split(key)
        x = jax.random.normal(k1, (N, D), dtype=jnp.float32)
        adj = jax.random.randint(k2, (N, N), 0, 2, dtype=jnp.int32)
        return {'x': x, 'adj': adj}
    _L1_gnn_all = _L1_gnn_setup()
    _L1_gnn_in = {k: v for k, v in _L1_gnn_all.items() if k in ()}
    del _L1_gnn_all

    def _L2_gnn_setup():
        import jax, jax.numpy as jnp
        import numpy as np
        N, D = (8192, 128)
        key = jax.random.key(seed)
        k1, k2, k3 = jax.random.split(key, 3)
        adj = jax.random.randint(k1, (N, N), 0, 2, dtype=jnp.int32)
        emb = jax.random.normal(k2, (N, D), dtype=jnp.float32)
        attn = jax.random.normal(k3, (2 * D, 1), dtype=jnp.float32)
        return {'adj': adj, 'emb': emb, 'attn': attn}
    _L2_gnn_all = _L2_gnn_setup()
    _L2_gnn_in = {k: v for k, v in _L2_gnn_all.items() if k in ('attn', )}
    del _L2_gnn_all

    def _L3_gnn_setup():
        import jax, jax.numpy as jnp
        import numpy as np
        N = 8192
        IN = 128
        OUT = 128
        THR = 0.0001
        ALPHA = 0.2
        NEG = -1000000000.0
        key = jax.random.key(seed)
        k1, k2, k3, k4 = jax.random.split(key, 4)
        inp = jax.random.normal(k1, (N, IN), jnp.float32)
        W = jax.random.normal(k2, (IN, OUT), jnp.float32) * (1.414 * np.sqrt(2.0 / (IN + OUT)))
        a = jax.random.normal(k3, (2 * OUT, 1), jnp.float32) * (1.414 * np.sqrt(2.0 / (2 * OUT + 1)))
        adj = jax.random.randint(k4, (N, N), 0, 2, jnp.int32)
        return {'input': inp, 'W': W, 'a': a, 'adj': adj, 'M': N}
    _L3_gnn_all = _L3_gnn_setup()
    _L3_gnn_in = {k: v for k, v in _L3_gnn_all.items() if k in ('W', 'a', )}
    del _L3_gnn_all

    return {
        "x": x,
        "adj": adj,
        "L0_gnn_W": _L0_gnn_in["W"],
        "L0_gnn_attn_src": _L0_gnn_in["attn_src"],
        "L0_gnn_attn_dst": _L0_gnn_in["attn_dst"],
        "L2_gnn_attn": _L2_gnn_in["attn"],
        "L3_gnn_W": _L3_gnn_in["W"],
        "L3_gnn_a": _L3_gnn_in["a"],
    }

def reference(x, adj, L0_gnn_W, L0_gnn_attn_src, L0_gnn_attn_dst, L2_gnn_attn, L3_gnn_W, L3_gnn_a):
    import jax
    import jax.numpy as jnp
    def _L0_gnn_ref(x, adj, W, attn_src, attn_dst):
        import jax, jax.numpy as jnp
        import numpy as np
        N, IN_DIM, OUT_DIM, H = (4096, 128, 128, 4)
        HEAD_DIM = OUT_DIM // H
        NEG_SLOPE = 0.2
        n = x.shape[0]
        h = (x @ W.T).reshape(n, H, HEAD_DIM)
        e_src = jnp.sum(h * attn_src, axis=-1)
        e_dst = jnp.sum(h * attn_dst, axis=-1)
        e = e_src[:, None, :] + e_dst[None, :, :]
        e = jax.nn.leaky_relu(e, negative_slope=NEG_SLOPE)
        e = jnp.where((adj == 0)[:, :, None], -jnp.inf, e)
        alpha = jax.nn.softmax(e, axis=1)
        out = jnp.einsum('ijh,jhd->ihd', alpha, h)
        return out.reshape(n, -1)

    def _L1_gnn_ref(x, adj):
        import jax, jax.numpy as jnp
        import numpy as np
        from jax import lax
        N = 8192
        D = 128
        CHUNK = 128
        n, d = x.shape
        neg = jnp.finfo(x.dtype).min
        adj_chunks = adj.reshape(n // CHUNK, CHUNK, n)

        def step(carry, a):
            mask = a != 0
            masked = jnp.where(mask[:, :, None], x[None, :, :], neg)
            m = jnp.max(masked, axis=1)
            has_nbr = jnp.any(mask, axis=1)
            out = jnp.where(has_nbr[:, None], m, jnp.zeros((), x.dtype))
            return (carry, out)
        _, out = lax.scan(step, None, adj_chunks)
        return out.reshape(n, d)

    def _L2_gnn_ref(adj, emb, attn):
        import jax, jax.numpy as jnp
        import numpy as np
        N, D = (8192, 128)
        d = emb.shape[1]
        s_i = emb @ attn[:d]
        s_j = emb @ attn[d:]
        e = jax.nn.leaky_relu(s_i + s_j.T, negative_slope=0.2)
        neg_inf = jnp.float32(-1000000000.0)
        e = e + jnp.where(adj > 0, jnp.float32(0.0), neg_inf)
        alpha = jax.nn.softmax(e, axis=1)
        return alpha @ emb

    def _L3_gnn_ref(input, W, a, adj, M):
        import jax, jax.numpy as jnp
        import numpy as np
        N = 8192
        IN = 128
        OUT = 128
        THR = 0.0001
        ALPHA = 0.2
        NEG = -1000000000.0
        h = input @ W
        a_src = a[:OUT, 0]
        a_dst = a[OUT:, 0]
        e = jax.nn.leaky_relu((h[:M] @ a_src)[:, None] + (h @ a_dst)[None, :], negative_slope=ALPHA)
        valid = (adj[:M] > 0) & (h.sum(axis=1) != 0)[None, :]
        att = jax.nn.softmax(jnp.where(valid, e, NEG), axis=1)
        att = jnp.where(valid, att, 0.0)
        L = valid.sum(axis=1).astype(h.dtype)
        top = att.max(axis=1)
        attention = jnp.where(att >= THR, att, 0.0) * L[:, None]
        attention = jnp.where((top > THR)[:, None], attention, 0.0)
        h_prime = attention @ h
        return jax.nn.elu(h[:M] + h_prime)

    x = _layernorm(x + _L0_gnn_ref(x, adj, L0_gnn_W, L0_gnn_attn_src, L0_gnn_attn_dst), axis=-1)
    x = _layernorm(x + _L1_gnn_ref(x, adj), axis=-1)
    x = _layernorm(x + _L2_gnn_ref(adj, x, L2_gnn_attn), axis=-1)
    x = _layernorm(x + _L3_gnn_ref(x, L3_gnn_W, L3_gnn_a, adj, 8192), axis=-1)
    return x


_drawn_inputs = setup_inputs


def setup_inputs(seed=0):
    import zlib

    import numpy as np

    out = dict(_drawn_inputs(seed))
    spreads = {}
    factors = {}
    for name, (base, spread) in spreads.items():
        noise = np.random.default_rng([zlib.crc32(name.encode()), seed]).standard_normal(out[name].shape)
        drawn = base * np.exp(spread * noise) if base else spread * noise
        out[name] = jnp.asarray(drawn.astype(out[name].dtype))
    for name, factor in factors.items():
        out[name] = (out[name] * factor).astype(out[name].dtype)
    return out
```

```python
from contextlib import ExitStack

import concourse.bass as bass
import numpy as np
from concourse import mybir

F32 = mybir.dt.float32
BF16 = mybir.dt.bfloat16
I32 = mybir.dt.int32
ALU = mybir.AluOpType
ACT = mybir.ActivationFunctionType
AX = mybir.AxisListType
RMAX = bass.bass_isa.ReduceOp.max

P = 128
HEADS = 4
HD = P // HEADS
HW = HD + 1
BITS = 6
PATS = 1 << BITS
SPAN = 2 * BITS
NQ = -(-P // SPAN)
SUB = 512
CT = 8
CW = CT * P
SLOPE = 0.2
EPS = 1e-5
THR = 1e-4
NEG = -(2.0 ** 100)


def span_starts():
    return [min(q * SPAN, P - SPAN) for q in range(NQ)]


def constants():
    ident = np.eye(P, dtype=np.float32)
    sel = np.zeros((P, NQ, BITS, P), np.float32)
    ham = np.zeros((P, NQ, P), np.float32)
    bits = np.zeros((P, 1 + BITS), np.float32)
    for p in range(P):
        group, pattern = divmod(p, PATS)
        bits[p, 0] = 1 - bin(pattern).count("1")
        for k in range(BITS):
            on = pattern >> k & 1
            bits[p, 1 + k] = 0.0 if on else NEG
            for q, start in enumerate(span_starts()):
                row = start + group * BITS + k
                sel[row, q, k, p] = on
                ham[row, q, p] = 1.0 if on else -1.0
    return {
        "c_ident": ident,
        "c_sel": sel.reshape(P, -1),
        "c_ham": ham.reshape(P, -1),
        "c_bits": bits,
    }


def build(nc, x, adj, W0, src0, dst0, attn2, W3, a3, c_ident, c_sel, c_ham, c_bits, out):
    N = x.shape[0]
    T = N // P
    NC = N // CW
    HB = T // 2
    GB = min(8, HB)
    NG = HB // GB
    U0W = 3 * HEADS * HW

    scratch = {}

    def dram(name, shape, dt):
        scratch[name] = nc.dram_tensor(name, shape, dt)
        return scratch[name].ap()

    maskT = dram("maskT", [T, P, T, P], BF16)
    negn = dram("negn", [T, P, N], BF16)
    x_1 = dram("x_1", [P, T, P], F32)
    x_2 = dram("x_2", [P, T, P], F32)
    x_3 = dram("x_3", [P, T, P], F32)
    sums = dram("sums", [T, P, U0W], F32)
    ab0 = dram("ab0", [P, 2, T, HEADS], F32)
    rhs0 = dram("rhs0", [P, T, 3, 2 * HEADS * HW], BF16)
    rows = dram("rows", [8, N], F32)
    table = dram("table", [T, P, NQ, 3, P], BF16)
    best_d = dram("best_d", [P, 2, N], F32)
    h_3 = dram("h_3", [P, T, P], F32)
    d0_cols = dram("d0_cols", [P, T, HEADS], F32)
    cols = dram("cols", [P, 5, T], F32)

    def tiles(a):
        return a.rearrange("(t p) c -> p t c", p=P)

    phases = [0]

    def phase(body):
        phases[0] += 1
        tag = f"p{phases[0]}_"
        sems = []

        def sem(name):
            sems.append(nc.alloc_semaphore(tag + name))
            return sems[-1]

        with ExitStack() as ctx:
            body(
                lambda name, shape, dt: ctx.enter_context(nc.sbuf_tensor(tag + name, shape, dt)),
                lambda name, shape, dt: ctx.enter_context(nc.psum_tensor(tag + name, shape, dt)),
                sem,
                lambda: ctx.enter_context(nc.Block()),
            )
        nc.clear_and_free_semaphores(sems)
        nc.all_engine_barrier()

    def chain(eng, sem):
        n = [0]

        def link(ins):
            n[0] += 1
            ins.then_inc(sem, 1)
            eng.wait_ge(sem, n[0])

        return link

    def adjacency(sb, ps, sem, block):
        ident = sb("a_ident", [P, P], F32)
        identb = sb("a_identb", [P, P], BF16)
        raw = sb("a_raw", [P, 2, N // 2], I32)
        mask = sb("a_mask", [P, 2, N // 2], BF16)
        neg = sb("a_neg", [P, 2, N // 2], BF16)
        maskt = sb("a_maskt", [P, 2, HB, P], BF16)
        bank = ps("a_bank", [P, 2, NG, 2 * SUB], BF16)
        ident_in, ident_ok = sem("a_ident_in"), sem("a_ident_ok")
        raw_in = [sem("a_raw_in0"), sem("a_raw_in1")]
        cast_done = [sem("a_cast0"), sem("a_cast1")]
        neg_done = [sem("a_neg0"), sem("a_neg1")]
        neg_stored = [sem("a_nst0"), sem("a_nst1")]
        transposed = [sem("a_tr0"), sem("a_tr1")]
        copied = [sem("a_cp0"), sem("a_cp1")]
        mask_stored = [sem("a_mst0"), sem("a_mst1")]
        blk = block()
        adj_t = adj.rearrange("(t p) n -> t p n", p=P)

        @blk.sync
        def _(sp):
            sp.dma_start(ident[:], c_ident).then_inc(ident_in, 16)
            for hf in range(2):
                sp.dma_start(raw[:, hf], adj_t[0, :, hf * (N // 2):(hf + 1) * (N // 2)]).then_inc(raw_in[hf], 16)

            def load(t):
                for hf in range(2):
                    sp.wait_ge(cast_done[hf], t)
                    sp.wait_ge(neg_done[hf], t)
                    sp.dma_start(raw[:, hf], adj_t[bass.ds(t, 1), :, hf * (N // 2):(hf + 1) * (N // 2)]
                                 .rearrange("a p n -> p (a n)")).then_inc(raw_in[hf], 16)

            def store(t):
                for hf in range(2):
                    sp.wait_ge(neg_done[hf], t + 1)
                    sp.dma_start(negn[bass.ds(t, 1), :, hf * (N // 2):(hf + 1) * (N // 2)]
                                 .rearrange("a p n -> p (a n)"), neg[:, hf]).then_inc(neg_stored[hf], 16)
                for hf in range(2):
                    sp.wait_ge(copied[hf], t * NG + NG)
                    sp.dma_start(maskT[bass.ds(t, 1), :, hf * HB:(hf + 1) * HB, :]
                                 .rearrange("a p b c -> p (a b c)"),
                                 maskt[:, hf].rearrange("p b c -> p (b c)")).then_inc(mask_stored[hf], 16)

            with sp.Fori(1, T) as t:
                load(t)
                store(t - 1)
            store(T - 1)
            for hf in range(2):
                sp.wait_ge(neg_stored[hf], 16 * T)
                sp.wait_ge(mask_stored[hf], 16 * T)

        @blk.vector
        def _(dve):
            dve.wait_ge(ident_in, 16)
            nc.vector.tensor_copy(identb[:], ident[:]).then_inc(ident_ok, 1)
            for first in (True, False):
                def step(t, first=first):
                    for hf in range(2):
                        dve.wait_ge(raw_in[hf], t * 16 + 16)
                        if not first:
                            dve.wait_ge(transposed[hf], t * NG)
                        nc.vector.tensor_copy(mask[:, hf], raw[:, hf]).then_inc(cast_done[hf], 1)
                    if not first:
                        dve.wait_ge(mask_stored[0], t * 16)
                    for g in range(NG):
                        dve.wait_ge(transposed[0], t * NG + g + 1)
                        nc.vector.tensor_copy(maskt[:, 0, g * GB:(g + 1) * GB],
                                              bank[:, 0, g, :GB * P].rearrange("p (b c) -> p b c", c=P)).then_inc(copied[0], 1)
                if first:
                    step(0)
                else:
                    with dve.Fori(1, T) as t:
                        step(t)

        @blk.scalar
        def _(act):
            for first in (True, False):
                def step(t, first=first):
                    for hf in range(2):
                        act.wait_ge(raw_in[hf], t * 16 + 16)
                        if not first:
                            act.wait_ge(neg_stored[hf], t * 16)
                        nc.scalar.activation(neg[:, hf], raw[:, hf], ACT.Copy, bias=NEG,
                                             scale=-NEG).then_inc(neg_done[hf], 1)
                    if not first:
                        act.wait_ge(mask_stored[1], t * 16)
                    for g in range(NG):
                        act.wait_ge(transposed[1], t * NG + g + 1)
                        nc.scalar.copy(maskt[:, 1, g * GB:(g + 1) * GB],
                                       bank[:, 1, g, :GB * P].rearrange("p (b c) -> p b c", c=P)).then_inc(copied[1], 1)
                if first:
                    step(0)
                else:
                    with act.Fori(1, T) as t:
                        step(t)

        @blk.tensor
        def _(pe):
            pe.wait_ge(ident_ok, 1)
            for first in (True, False):
                def step(t, first=first):
                    for hf in range(2):
                        pe.wait_ge(cast_done[hf], t + 1)
                        if not first:
                            pe.wait_ge(copied[hf], t * NG)
                        for g in range(NG):
                            for b in range(GB):
                                c = (g * GB + b) * P
                                last = nc.tensor.transpose(bank[:, hf, g, b * P:(b + 1) * P],
                                                           mask[:, hf, c:c + P], identb[:])
                            last.then_inc(transposed[hf], 1)
                if first:
                    step(0)
                else:
                    with pe.Fori(1, T) as t:
                        step(t)

    phase(adjacency)

    def project(blk, sem, ps, sb, tag, xt_src, weights, width, h, ready_x, ready_w):
        xT = sb(tag + "_xT", [P, 2, P], F32)
        pT = ps(tag + "_pT", [P, 2, SUB], F32)
        pH = ps(tag + "_pH", [P, 2, SUB], F32)
        xT_ready, pT_ready, pH_ready, h_ready = (sem(tag + n) for n in ("_xTr", "_pTr", "_pHr", "_hr"))

        def tensor(pe):
            for sem_, val in (ready_x, ready_w):
                pe.wait_ge(sem_, val)
            for i in range(T // 2):
                for b in range(2):
                    if i:
                        pe.wait_ge(xT_ready, i * 2 - 1 + b)
                    nc.tensor.transpose(pT[:, b, :P], xt_src(i * 2 + b), ident_of[tag][:]).then_inc(pT_ready, 1)
                for b in range(2):
                    pe.wait_ge(xT_ready, i * 2 + b + 1)
                    if i:
                        pe.wait_ge(h_ready, i * 2 - 1 + b)
                    nc.tensor.matmul(pH[:, b, :width], xT[:, b], weights[:, :width], start=True,
                                     stop=True).then_inc(pH_ready, 1)

        def scalar(act):
            for n in range(T):
                act.wait_ge(pT_ready, n + 1)
                if n >= 2:
                    act.wait_ge(pH_ready, n - 1)
                nc.scalar.copy(xT[:, n % 2], pT[:, n % 2, :P]).then_inc(xT_ready, 1)

        def vector(dve):
            with dve.Fori(0, T // 2) as i:
                for b in range(2):
                    dve.wait_ge(pH_ready, i * 2 + b + 1)
                    nc.vector.tensor_copy(h[:, bass.ds(i * 2 + b, 1)].rearrange("p a c -> p (a c)"),
                                          pH[:, b, :width]).then_inc(h_ready, 1)
            dve.wait_ge(h_ready, T)

        return tensor, scalar, vector

    ident_of = {}

    def operands0(sb, ps, sem, block):
        ident = ident_of["o"] = sb("o_ident", [P, P], F32)
        X = sb("o_X", [P, T, P], F32)
        Wn = sb("o_Wn", [P, P], F32)
        sd = sb("o_sd", [P, 2], F32)
        heads = sb("o_heads", [P, 2 * HEADS], F32)
        Wx = sb("o_Wx", [P, P + 2 * HEADS], F32)
        h = sb("o_h", [P, T, P + 2 * HEADS], F32)
        top = sb("o_top", [P, HEADS], F32)
        c = sb("o_c", [P, HEADS], F32)
        z = sb("o_z", [P, T, 2, HEADS], F32)
        e = sb("o_e", [P, 4, T, HEADS], F32)
        negs = sb("o_negs", [P, HEADS, T], F32)
        negsT = sb("o_negsT", [P, HEADS, P], F32)
        QT = T // 4 if T >= 32 else T // 2
        f = sb("o_f", [P, QT, HEADS, 2, HW], F32)
        g = sb("o_g", [P, QT, HEADS * 2 * HW], F32)
        r3 = sb("o_r3", [P, QT, 3, HEADS * 2 * HW], BF16)
        pW = ps("o_pW", [P, 2, SUB], F32)
        pS = ps("o_pS", [P, SUB], F32)
        loaded, w_ok, heads_ok, w_mm, top_ok, c_ok = (sem("o_" + n) for n in
                                                      ("loaded", "w_ok", "heads_ok", "w_mm", "top_ok", "c_ok"))
        dcol = sb("o_dcol", [P, T, HEADS], F32)
        dcol_ok = sem("o_dcol_ok")
        dch, z_ok, e_ok, negs_ok, negs_tr, negs_cp, rows_st, r_ok, r_st, e_st = (
            sem("o_" + n) for n in ("dch", "z_ok", "e_ok", "negs_ok", "negs_tr", "negs_cp", "rows_st",
                                    "r_ok", "r_st", "e_st"))
        blk = block()
        tensor, scalar, vector = project(blk, sem, ps, sb, "o", lambda t: X[:, t], Wx, P + 2 * HEADS, h, (loaded, 16 * 5), (w_ok, 1))
        TH = min(P, HEADS * T)
        NTR = HEADS * T // TH

        @blk.sync
        def _(sp):
            sp.dma_start(X[:], tiles(x)).then_inc(loaded, 16)
            sp.dma_start(ident[:], c_ident).then_inc(loaded, 16)
            sp.dma_start(Wn[:], W0).then_inc(loaded, 16)
            sp.dma_start(sd[:, 0:1], src0.rearrange("a h d -> (h d) a")).then_inc(loaded, 16)
            sp.dma_start(sd[:, 1:2], dst0.rearrange("a h d -> (h d) a")).then_inc(loaded, 16)
            for n in range(T // QT):
                sp.wait_ge(r_ok, n + 1)
                sp.dma_start(rhs0[:, n * QT:(n + 1) * QT], r3[:]).then_inc(r_st, 16)
            sp.wait_ge(dcol_ok, 1)
            sp.wait_ge(e_ok, 4)
            sp.dma_start(ab0, e[:, 0:2]).then_inc(e_st, 16)
            sp.dma_start(d0_cols, dcol[:]).then_inc(e_st, 16)
            sp.wait_ge(negs_cp, NTR)
            rr = rows[0:HEADS].rearrange("h (t p) -> (h t) p", p=P)
            for n in range(NTR):
                sp.dma_start(rr[n * TH:(n + 1) * TH], negsT[:TH, n]).then_inc(rows_st, 16)
            sp.wait_ge(rows_st, 16 * NTR)
            sp.wait_ge(e_st, 32)
            sp.wait_ge(r_st, 16 * (T // QT))

        @blk.gpsimd
        def _(pool):
            pool.wait_ge(top_ok, 1)
            nc.gpsimd.partition_all_reduce(c[:], top[:], P, RMAX).then_inc(c_ok, 1)

        @blk.scalar
        def _(act):
            scalar(act)
            act.wait_ge(z_ok, 1)
            nc.scalar.activation(e[:, 0], z[:, :, 0], ACT.Exp).then_inc(e_ok, 1)
            act.wait_ge(z_ok, 2)
            nc.scalar.activation(e[:, 1], z[:, :, 1], ACT.Exp).then_inc(e_ok, 1)
            act.wait_ge(z_ok, 3)
            nc.scalar.activation(e[:, 2], z[:, :, 0], ACT.Exp).then_inc(e_ok, 1)
            nc.scalar.activation(e[:, 3], z[:, :, 0], ACT.Exp, scale=SLOPE).then_inc(e_ok, 1)

        @blk.vector
        def _(dve):
            link = chain(dve, dch)
            link(nc.vector.memset(heads[:], 0.0))
            dve.wait_ge(loaded, 16 * 5)
            for k in range(2):
                for hd in range(HEADS):
                    q = slice(hd * HD, (hd + 1) * HD)
                    link(nc.vector.tensor_copy(heads[q, k * HEADS + hd:k * HEADS + hd + 1], sd[q, k:k + 1]))
            dve.sem_inc(heads_ok, 1)
            dve.wait_ge(w_mm, 1)
            link(nc.vector.tensor_copy(Wx[:, :P], pW[:, 0, :P]))
            nc.vector.tensor_copy(Wx[:, P:], pW[:, 1, :2 * HEADS]).then_inc(w_ok, 1)
            vector(dve)
            s, d = h[:, :, P:P + HEADS], h[:, :, P + HEADS:]
            nc.vector.tensor_reduce(top[:], d.rearrange("p t h -> p h t"), AX.X, ALU.max).then_inc(top_ok, 1)
            nc.vector.tensor_scalar(negs[:], s.rearrange("p t h -> p h t"), -1.0, None, ALU.mult).then_inc(negs_ok, 1)
            nc.vector.tensor_copy(dcol[:], d).then_inc(dcol_ok, 1)
            dve.wait_ge(c_ok, 1)
            cb = c[:].unsqueeze(1).broadcast_to([P, T, HEADS])
            link(nc.vector.tensor_tensor(z[:, :, 1], s, cb, ALU.add))
            nc.vector.tensor_scalar(z[:, :, 0], z[:, :, 1], 1 - SLOPE, 0.0, ALU.mult, ALU.min).then_inc(z_ok, 1)
            dve.wait_ge(z_ok, 1)
            nc.vector.tensor_scalar(z[:, :, 1], z[:, :, 1], SLOPE - 1, 0.0, ALU.mult, ALU.min).then_inc(z_ok, 1)
            dve.wait_ge(e_ok, 1)
            nc.vector.tensor_tensor(z[:, :, 0], d, cb, ALU.subtract).then_inc(z_ok, 1)
            for n in range(NTR):
                dve.wait_ge(negs_tr, NTR)
                nc.vector.tensor_copy(negsT[:TH, n], pS[:TH, n * P:(n + 1) * P]).then_inc(negs_cp, 1)
            dve.wait_ge(e_ok, 4)
            for n in range(T // QT):
                ts_ = slice(n * QT, (n + 1) * QT)
                for hd in range(HEADS):
                    for k in range(2):
                        w = e[:, 2 + k, ts_, hd:hd + 1]
                        link(nc.vector.tensor_tensor(f[:, :, hd, k, :HD], h[:, ts_, hd * HD:(hd + 1) * HD],
                                                     w.broadcast_to([P, QT, HD]), ALU.mult))
                        link(nc.vector.tensor_copy(f[:, :, hd, k, HD:], w))
                ff = f[:].rearrange("p t h k c -> p t (h k c)")
                if n:
                    dve.wait_ge(r_st, 16 * n)
                link(nc.vector.tensor_copy(r3[:, :, 0], ff))
                link(nc.vector.tensor_tensor(g[:], ff, r3[:, :, 0], ALU.subtract))
                link(nc.vector.tensor_copy(r3[:, :, 1], g[:]))
                link(nc.vector.tensor_tensor(r3[:, :, 2], g[:], r3[:, :, 1], ALU.subtract))
                dve.sem_inc(r_ok, 1)

        @blk.tensor
        def _(pe):
            pe.wait_ge(loaded, 16 * 5)
            pe.wait_ge(heads_ok, 1)
            nc.tensor.transpose(pW[:, 0, :P], Wn[:], ident[:])
            nc.tensor.matmul(pW[:, 1, :2 * HEADS], Wn[:], heads[:], start=True, stop=True).then_inc(w_mm, 1)
            tensor(pe)
            pe.wait_ge(negs_ok, 1)
            nf = negs[:].rearrange("p h t -> p (h t)")
            for n in range(NTR):
                nc.tensor.transpose(pS[:TH, n * P:(n + 1) * P], nf[:, n * TH:(n + 1) * TH],
                                    ident[:]).then_inc(negs_tr, 1)

    phase(operands0)

    def sums0(sb, ps, sem, block):
        W2 = 2 * HEADS * HW
        R = sb("s_R", [P, T, 3, HEADS, 2, HW], BF16)
        hd_cols = sb("s_d", [P, T, HEADS], F32)
        negs = sb("s_negs", [P, HEADS, CW], F32)
        mask = sb("s_mask", [P, 2, CT, 2, P], BF16)
        m1 = sb("s_m1", [P, 2, HEADS, CW], BF16)
        zero = sb("s_zero", [P, SUB], BF16)
        st = sb("s_st", [P, CT, U0W], F32)
        acc = ps("s_acc", [P, CT, SUB], F32)
        loaded, zero_ok, negs_in, chunk_cmp = (sem("s_" + n) for n in ("loaded", "zero_ok", "negs_in", "chunk_cmp"))
        mask_in = [sem("s_mi0"), sem("s_mi1")]
        mask_used = [sem("s_mu0"), sem("s_mu1")]
        m1_ready, m1_used, acc_done, acc_copied, st_out = (sem("s_" + n) for n in
                                                          ("m1r", "m1u", "accd", "accc", "sto"))
        blk = block()
        NP = T // 4

        @blk.sync
        def _(sp):
            sp.dma_start(R[:], rhs0.rearrange("p t k (h u c) -> p t k h u c", h=HEADS, u=2)).then_inc(loaded, 16)
            sp.dma_start(hd_cols[:], d0_cols).then_inc(loaded, 16)
            with sp.Fori(0, NC) as ch:
                sp.wait_ge(chunk_cmp, ch + 1)
                sp.dma_start(negs[:], rows[0:HEADS, bass.ds(ch * CW, CW)].partition_broadcast(P)).then_inc(negs_in, 16)
                with sp.Fori(0, NP) as i:
                    for b in range(2):
                        sp.wait_ge(mask_used[b], ch * NP + i + 1)
                        for t in range(CT):
                            sp.dma_start(mask[:, b, t], maskT[bass.ds(ch * CT + t, 1), :, bass.ds(i * 4 + b * 2, 2), :]
                                         .rearrange("a p b c -> p (a b) c")).then_inc(mask_in[b], 16)

        @blk.vector
        def _(dve):
            nc.vector.memset(zero[:], 0.0).then_inc(zero_ok, 1)
            dve.sem_inc(chunk_cmp, 1)
            dve.wait_ge(loaded, 32)
            with dve.Fori(0, NC) as ch:
                with dve.Fori(0, NP) as i:
                    dve.wait_ge(negs_in, ch * 16 + 16)
                    for b in range(2):
                        dve.wait_ge(mask_in[b], (ch * NP + i + 1) * (16 * CT))
                        for k in range(2):
                            dve.wait_ge(m1_used, (ch * NP + i) * 4 + b * 2 + k + 1)
                            for hd in range(HEADS):
                                last = nc.vector.scalar_tensor_tensor(
                                    m1[:, k, hd].rearrange("p (t c) -> p t c", c=P),
                                    negs[:, hd].rearrange("p (t c) -> p t c", c=P),
                                    hd_cols[:, bass.ds(i * 4 + b * 2 + k, 1), hd:hd + 1].rearrange("p a c -> p (a c)"),
                                    mask[:, b, :, k], ALU.is_lt, ALU.mult)
                            last.then_inc(m1_ready, 1)
                dve.wait_ge(m1_ready, (ch + 1) * T)
                dve.sem_inc(chunk_cmp, 1)

        @blk.tensor
        def _(pe):
            pe.sem_inc(m1_used, 2)
            for b in range(2):
                pe.sem_inc(mask_used[b], 1)
            pe.wait_ge(zero_ok, 1)
            pe.wait_ge(loaded, 32)
            with pe.Fori(0, NC) as ch:
                for t in range(CT):
                    pe.wait_ge(acc_copied, ch * CT + t + 1)
                    nc.tensor.matmul(acc[:, t, :U0W], zero[:, :P], zero[:, :U0W], start=True, stop=False)
                with pe.Fori(0, NP) as i:
                    for b in range(2):
                        for k in range(2):
                            pe.wait_ge(m1_ready, (ch * NP + i) * 4 + b * 2 + k + 1)
                            j = i * 4 + b * 2 + k
                            for t in range(CT):
                                for part in range(3):
                                    nc.tensor.matmul(
                                        acc[:, t, W2:U0W].rearrange("p (h c) -> p h c", c=HW), mask[:, b, t, k],
                                        R[:, bass.ds(j, 1), part, :, 1].rearrange("p a h c -> p (a h) c"),
                                        start=False, stop=False, skip_group_check=True)
                                for hd in range(HEADS):
                                    for part in range(3):
                                        last = nc.tensor.matmul(
                                            acc[:, t, hd * 2 * HW:(hd + 1) * 2 * HW],
                                            m1[:, k, hd, t * P:(t + 1) * P],
                                            R[:, bass.ds(j, 1), part, hd].rearrange("p a u c -> p (a u c)"),
                                            start=False, stop=False, skip_group_check=True)
                            last.then_inc(m1_used, 1)
                        pe.wait_ge(m1_used, (ch * NP + i) * 4 + b * 2 + 4)
                        pe.sem_inc(mask_used[b], 1)
                for t in range(CT):
                    nc.tensor.matmul(acc[:, t, :U0W], zero[:, :P], zero[:, :U0W], start=False,
                                     stop=True).then_inc(acc_done, 1)

        @blk.scalar
        def _(act):
            act.sem_inc(acc_copied, CT)
            act.sem_inc(st_out, 16)
            with act.Fori(0, NC) as ch:
                act.wait_ge(st_out, ch * 16 + 16)
                for t in range(CT):
                    act.wait_ge(acc_done, ch * CT + t + 1)
                    nc.scalar.copy(st[:, t], acc[:, t, :U0W]).then_inc(acc_copied, 1)
                act.wait_ge(acc_copied, (ch + 2) * CT)
                act.dma_start(sums[bass.ds(ch * CT, CT)].rearrange("t p c -> p t c"), st[:]).then_inc(st_out, 16)
            act.wait_ge(st_out, 16 * NC + 16)

    phase(sums0)

    def normalise(dve, link, X, tmp, stat, var_ok, std_ok):
        wide = lambda a: a.unsqueeze(2).broadcast_to([P, T, P])
        link(nc.vector.tensor_reduce(stat[:, 0], X[:], AX.X, ALU.add))
        link(nc.vector.tensor_scalar(stat[:, 0], stat[:, 0], 1.0 / P, None, ALU.mult))
        link(nc.vector.tensor_tensor(X[:], X[:], wide(stat[:, 0]), ALU.subtract))
        link(nc.vector.tensor_tensor(tmp[:], X[:], X[:], ALU.mult))
        link(nc.vector.tensor_reduce(stat[:, 1], tmp[:], AX.X, ALU.add))
        nc.vector.tensor_scalar(stat[:, 1], stat[:, 1], 1.0 / P, EPS, ALU.mult, ALU.add).then_inc(var_ok, 1)
        dve.wait_ge(std_ok, 1)
        link(nc.vector.reciprocal(stat[:, 0], stat[:, 2]))
        link(nc.vector.tensor_tensor(X[:], X[:], wide(stat[:, 0]), ALU.mult))

    def root(act, stat, var_ok, std_ok):
        act.wait_ge(var_ok, 1)
        nc.scalar.activation(stat[:, 2], stat[:, 1], ACT.Sqrt).then_inc(std_ok, 1)

    def finish0(sb, ps, sem, block):
        X, tmp, stat = sb("f_X", [P, T, P], F32), sb("f_tmp", [P, T, P], F32), sb("f_stat", [P, 3, T], F32)
        U = sb("f_U", [P, T, U0W], F32)
        ab = sb("f_ab", [P, 2, T, HEADS], F32)
        loaded, dch, var_ok, std_ok, x_ok, x_st = (sem("f_" + n) for n in
                                                   ("loaded", "dch", "var_ok", "std_ok", "x_ok", "x_st"))
        blk = block()

        @blk.sync
        def _(sp):
            sp.dma_start(U[:], sums[:, :, :U0W].rearrange("t p c -> p t c")).then_inc(loaded, 16)
            sp.dma_start(ab[:], ab0).then_inc(loaded, 16)
            sp.dma_start(X[:], tiles(x)).then_inc(loaded, 16)
            sp.wait_ge(x_ok, 1)
            sp.dma_start(x_1, X[:]).then_inc(x_st, 16)
            sp.wait_ge(x_st, 16)

        @blk.scalar
        def _(act):
            root(act, stat, var_ok, std_ok)

        @blk.vector
        def _(dve):
            link = chain(dve, dch)
            dve.wait_ge(loaded, 48)
            for hd in range(HEADS):
                u = U[:, :, hd * 2 * HW:hd * 2 * HW + HW]
                v = U[:, :, hd * 2 * HW + HW:(hd + 1) * 2 * HW]
                w = U[:, :, 2 * HEADS * HW + hd * HW:2 * HEADS * HW + (hd + 1) * HW]
                link(nc.vector.tensor_tensor(w, w, v, ALU.subtract))
                link(nc.vector.tensor_tensor(w, w, ab[:, 1, :, hd:hd + 1].broadcast_to([P, T, HW]), ALU.mult))
                link(nc.vector.tensor_tensor(u, u, ab[:, 0, :, hd:hd + 1].broadcast_to([P, T, HW]), ALU.mult))
                link(nc.vector.tensor_tensor(u, u, w, ALU.add))
                link(nc.vector.reciprocal(w[:, :, HD:], u[:, :, HD:]))
                link(nc.vector.tensor_tensor(u[:, :, :HD], u[:, :, :HD], w[:, :, HD:].broadcast_to([P, T, HD]),
                                             ALU.mult))
                xs = X[:, :, hd * HD:(hd + 1) * HD]
                link(nc.vector.tensor_tensor(xs, xs, u[:, :, :HD], ALU.add))
            normalise(dve, link, X, tmp, stat, var_ok, std_ok)
            dve.sem_inc(x_ok, 1)

    phase(finish0)

    def tables1(sb, ps, sem, block):
        X = sb("t_X", [P, T, P], F32)
        parts = sb("t_parts", [P, 3, T, P], BF16)
        selw = sb("t_selw", [P, NQ * BITS * P], F32)
        sel = sb("t_sel", [P, NQ, BITS, P], BF16)
        bits = sb("t_bits", [P, 1 + BITS], F32)
        best = sb("t_best", [P, 4, P], F32)
        rest = sb("t_rest", [P, 4, P], F32)
        split = sb("t_split", [P, 2, 4, 3, P], BF16)
        rowsum = ps("t_rows", [P, BITS, SUB], F32)
        loaded, dch, parts_ok, mm_ready, mm_used, rest_ok, split_ok = (
            sem("t_" + n) for n in ("loaded", "dch", "parts_ok", "mm_ready", "mm_used", "rest_ok", "split_ok"))
        stored = [sem("t_st0"), sem("t_st1")]
        uses = [(NQ + 1) // 2, NQ // 2]
        blk = block()

        @blk.sync
        def _(sp):
            sp.dma_start(X[:], x_1).then_inc(loaded, 16)
            sp.dma_start(selw[:], c_sel).then_inc(loaded, 16)
            sp.dma_start(bits[:], c_bits).then_inc(loaded, 16)
            for b in range(2):
                sp.sem_inc(stored[b], 16)
            with sp.Fori(0, T // 4) as cb:
                for q in range(NQ):
                    sp.wait_ge(split_ok, cb * NQ + q + 1)
                    sp.dma_start(table[bass.ds(cb * 4, 4), :, q].rearrange("t p k c -> p t k c"),
                                 split[:, q % 2]).then_inc(stored[q % 2], 16)
            for b in range(2):
                sp.wait_ge(stored[b], 16 * (T // 4 * uses[b] + 1))

        @blk.vector
        def _(dve):
            link = chain(dve, dch)
            dve.sem_inc(mm_used, BITS)
            dve.wait_ge(loaded, 48)
            nc.vector.tensor_copy(sel[:].rearrange("p q k c -> p (q k c)"), selw[:])
            link(nc.vector.tensor_copy(parts[:, 0], X[:]))
            link(nc.vector.tensor_tensor(X[:], X[:], parts[:, 0], ALU.subtract))
            link(nc.vector.tensor_copy(parts[:, 1], X[:]))
            nc.vector.tensor_tensor(parts[:, 2], X[:], parts[:, 1], ALU.subtract).then_inc(parts_ok, 1)
            with dve.Fori(0, T // 4) as cb:
                for q in range(NQ):
                    for k in range(BITS):
                        n = (cb * NQ + q) * BITS + k
                        dve.wait_ge(mm_ready, n + 1)
                        got = rowsum[:, k].rearrange("p (t c) -> p t c", c=P)
                        if k == 0:
                            nc.vector.tensor_scalar(best[:], got, bits[:, 1:2], None, ALU.add).then_inc(mm_used, 1)
                        else:
                            dve.wait_ge(mm_used, n + BITS)
                            nc.vector.scalar_tensor_tensor(best[:], got, bits[:, 1 + k:2 + k], best[:],
                                                           ALU.add, ALU.max).then_inc(mm_used, 1)
                    dve.wait_ge(mm_used, (cb * NQ + q + 2) * BITS)
                    dve.wait_ge(stored[q % 2], (cb * uses[q % 2] + q // 2 + 1) * 16)
                    m = (cb * NQ + q) * 3
                    nc.vector.tensor_copy(split[:, q % 2, :, 0], best[:]).then_inc(rest_ok, 1)
                    dve.wait_ge(rest_ok, m + 1)
                    nc.vector.tensor_tensor(rest[:], best[:], split[:, q % 2, :, 0], ALU.subtract).then_inc(rest_ok, 1)
                    dve.wait_ge(rest_ok, m + 2)
                    nc.vector.tensor_copy(split[:, q % 2, :, 1], rest[:]).then_inc(rest_ok, 1)
                    dve.wait_ge(rest_ok, m + 3)
                    nc.vector.tensor_tensor(split[:, q % 2, :, 2], rest[:], split[:, q % 2, :, 1],
                                            ALU.subtract).then_inc(split_ok, 1)

        @blk.tensor
        def _(pe):
            pe.wait_ge(parts_ok, 1)
            with pe.Fori(0, T // 4) as cb:
                for q in range(NQ):
                    for k in range(BITS):
                        pe.wait_ge(mm_used, (cb * NQ + q) * BITS + k + 1)
                        for part in range(3):
                            last = nc.tensor.matmul(rowsum[:, k].rearrange("p (t c) -> p t c", c=P),
                                                    sel[:, q, k], parts[:, part, bass.ds(cb * 4, 4)],
                                                    start=part == 0, stop=part == 2)
                        last.then_inc(mm_ready, 1)

    phase(tables1)

    def maxima1(sb, ps, sem, block):
        UW = 2 * SUB
        NU = N // UW
        UNITS = 2 * NQ * NU
        hamw = sb("m_hamw", [P, NQ * P], F32)
        ham = sb("m_ham", [P, NQ, P], BF16)
        bits = sb("m_bits", [P, 1 + BITS], F32)
        best = sb("m_best", [P, 2, N], F32)
        mask = sb("m_mask", [P, 2, T, P], BF16)
        tab = sb("m_tab", [P, 2, NQ, 3, P], BF16)
        hot = sb("m_hot", [P, 2, UW], BF16)
        dist = ps("m_dist", [P, 2, 2, SUB], F32)
        rowv = ps("m_row", [P, 2, 2, SUB], F32)
        loaded, ham_ok, best_ok, dist_ready, hot_ready, hot_used, row_ready, row_used, best_st = (
            sem("m_" + n) for n in ("loaded", "ham_ok", "best_ok", "dist_ready", "hot_ready", "hot_used",
                                    "row_ready", "row_used", "best_st"))
        block_in = [sem("m_in0"), sem("m_in1")]
        block_used = [sem("m_us0"), sem("m_us1")]
        blk = block()
        order = [(b, q, u) for b in range(2) for q in range(NQ) for u in range(NU)]

        @blk.sync
        def _(sp):
            sp.dma_start(hamw[:], c_ham).then_inc(loaded, 16)
            sp.dma_start(bits[:], c_bits).then_inc(loaded, 16)
            with sp.Fori(0, T // 2) as i:
                for b in range(2):
                    sp.wait_ge(block_used[b], i + 1)
                    sp.dma_start(mask[:, b], maskT[:, :, bass.ds(i * 2 + b, 1), :]
                                 .rearrange("t p a c -> p t (a c)")).then_inc(block_in[b], 16)
                    sp.dma_start(tab[:, b], table[bass.ds(i * 2 + b, 1)]
                                 .rearrange("a p q k c -> p (a q) k c")).then_inc(block_in[b], 16)
            sp.wait_ge(row_used, T * UNITS + 2)
            sp.dma_start(best_d, best[:]).then_inc(best_st, 16)
            sp.wait_ge(best_st, 16)

        @blk.tensor
        def _(pe):
            pe.sem_inc(hot_used, 2)
            for b in range(2):
                pe.sem_inc(block_used[b], 1)
            pe.wait_ge(ham_ok, 1)
            with pe.Fori(0, T // 2) as i:
                def distance(n):
                    b, q, u = order[n]
                    if q == 0 and u == 0:
                        pe.wait_ge(block_in[b], i * 32 + 32)
                    pe.wait_ge(hot_ready, i * UNITS + n + 1)
                    for s in range(2):
                        last = nc.tensor.matmul(
                            dist[:, n % 2, s].rearrange("p (t c) -> p t c", c=P), ham[:, q],
                            mask[:, b, (2 * u + s) * 4:(2 * u + s + 1) * 4], start=True, stop=True)
                    last.then_inc(dist_ready, 1)

                distance(0)
                for n, (b, q, u) in enumerate(order):
                    if n + 1 < len(order):
                        distance(n + 1)
                    pe.wait_ge(hot_ready, i * UNITS + n + 3)
                    for s in range(2):
                        pe.wait_ge(row_used, (i * UNITS + n) * 2 + s + 1)
                        for part in range(3):
                            for g in range(2):
                                half = slice(g * PATS, (g + 1) * PATS)
                                last = nc.tensor.matmul(rowv[:, s, g], tab[half, b, q, part],
                                                        hot[half, n % 2, s * SUB:(s + 1) * SUB],
                                                        start=part == 0, stop=part == 2)
                                if part == 2:
                                    last.then_inc(row_ready, 1)
                    pe.wait_ge(row_ready, (i * UNITS + n + 1) * 4)
                    pe.sem_inc(hot_used, 1)
                    if q == NQ - 1 and u == NU - 1:
                        pe.sem_inc(block_used[b], 1)

        @blk.scalar
        def _(act):
            act.wait_ge(loaded, 32)
            act.sem_inc(hot_ready, 2)
            with act.Fori(0, T // 2) as i:
                for n in range(UNITS):
                    act.wait_ge(dist_ready, i * UNITS + n + 1)
                    act.wait_ge(hot_used, i * UNITS + n + 1)
                    nc.scalar.activation(hot[:, n % 2].rearrange("p (s c) -> p s c", s=2), dist[:, n % 2], ACT.Relu,
                                         bias=bits[:, 0:1]).then_inc(hot_ready, 1)

        @blk.vector
        def _(dve):
            dve.wait_ge(loaded, 32)
            nc.vector.tensor_copy(ham[:].rearrange("p q c -> p (q c)"), hamw[:]).then_inc(ham_ok, 1)
            nc.vector.memset(best[:], NEG).then_inc(best_ok, 1)
            dve.wait_ge(best_ok, 1)
            dve.sem_inc(row_used, 2)
            with dve.Fori(0, T // 2) as i:
                for n, (b, q, u) in enumerate(order):
                    for s in range(2):
                        dve.wait_ge(row_ready, ((i * UNITS + n) * 2 + s + 1) * 2)
                        dve.wait_ge(row_used, (i * UNITS + n) * 2 + s + 1)
                        c = (u * 2 + s) * SUB
                        nc.vector.tensor_tensor(best[:, :, c:c + SUB], rowv[:, s], best[:, :, c:c + SUB],
                                                ALU.max).then_inc(row_used, 1)

    phase(maxima1)

    def write_rows(pe_in, ident, sb, ps, sem, tag, count):
        flat = sb(tag + "_flat", [P, count, P], F32)
        pF = ps(tag + "_pF", [P, count, SUB], F32)
        tr, cp, st = sem(tag + "_rtr"), sem(tag + "_rcp"), sem(tag + "_rst")

        def tensor(pe):
            for n in range(count):
                nc.tensor.transpose(pF[:T, n, :P], pe_in(n), ident[:]).then_inc(tr, 1)

        def scalar(act):
            for n in range(count):
                act.wait_ge(tr, n + 1)
                nc.scalar.copy(flat[:T, n], pF[:T, n, :P]).then_inc(cp, 1)

        def sync(sp, first_row):
            for n in range(count):
                sp.wait_ge(cp, n + 1)
                sp.dma_start(rows[first_row + n].rearrange("(t p) -> t p", p=P), flat[:T, n]).then_inc(st, 16)
            sp.wait_ge(st, 16 * count)

        return tensor, scalar, sync

    def finish1(sb, ps, sem, block):
        X, tmp, stat = sb("g_X", [P, T, P], F32), sb("g_tmp", [P, T, P], F32), sb("g_stat", [P, 3, T], F32)
        ident = sb("g_ident", [P, P], F32)
        best = sb("g_best", [P, 2, N], F32)
        at = sb("g_at", [P, 2, P], F32)
        sc = sb("g_sc", [P, 5, T], F32)
        y = ps("g_y", [P, 4, SUB], F32)
        loaded, dch, var_ok, std_ok, x_ok, x_st, best_ok, tr, tr_used, sc_ok = (
            sem("g_" + n) for n in ("loaded", "dch", "var_ok", "std_ok", "x_ok", "x_st", "best_ok", "tr", "tr_used",
                                    "sc_ok"))
        rt, ra, rs = write_rows(lambda n: sc[:, 1], ident, sb, ps, sem, "g", 1)
        blk = block()

        @blk.sync
        def _(sp):
            sp.dma_start(best[:], best_d).then_inc(loaded, 16)
            sp.dma_start(ident[:], c_ident).then_inc(loaded, 16)
            sp.dma_start(X[:], x_1).then_inc(loaded, 16)
            sp.dma_start(at[:], attn2.rearrange("(k c) a -> a k c", k=2).partition_broadcast(P)
                         .rearrange("q a k c -> q (a k) c")).then_inc(loaded, 16)
            sp.wait_ge(x_ok, 1)
            sp.dma_start(x_2, X[:]).then_inc(x_st, 16)
            sp.wait_ge(sc_ok, 1)
            sp.dma_start(cols[:, :4], sc[:, :4]).then_inc(x_st, 16)
            rs(sp, 4)
            sp.wait_ge(x_st, 32)

        @blk.scalar
        def _(act):
            root(act, stat, var_ok, std_ok)
            ra(act)

        @blk.tensor
        def _(pe):
            pe.wait_ge(loaded, 64)
            pe.wait_ge(best_ok, 1)
            for t in range(T):
                if t >= 4:
                    pe.wait_ge(tr_used, t - 3)
                nc.tensor.transpose(y[:, t % 4, :P], best[:, 0, t * P:(t + 1) * P], ident[:]).then_inc(tr, 1)
            pe.wait_ge(sc_ok, 1)
            rt(pe)

        @blk.vector
        def _(dve):
            link = chain(dve, dch)
            dve.wait_ge(loaded, 64)
            link(nc.vector.tensor_tensor(best[:, 0], best[:, 0], best[:, 1], ALU.max))
            link(nc.vector.scalar_tensor_tensor(best[:, 0], best[:, 0], NEG / 2, best[:, 0], ALU.is_gt, ALU.mult))
            dve.sem_inc(best_ok, 1)
            for t in range(T):
                dve.wait_ge(tr, t + 1)
                nc.vector.tensor_tensor(X[:, t], y[:, t % 4, :P], X[:, t], ALU.add).then_inc(tr_used, 1)
            dve.wait_ge(tr_used, T)
            normalise(dve, link, X, tmp, stat, var_ok, std_ok)
            dve.sem_inc(x_ok, 1)
            for k in range(2):
                link(nc.vector.tensor_tensor(tmp[:], X[:], at[:, k].unsqueeze(1).broadcast_to([P, T, P]), ALU.mult))
                link(nc.vector.tensor_reduce(sc[:, k], tmp[:], AX.X, ALU.add))
            link(nc.vector.tensor_scalar(sc[:, 2], sc[:, 1], SLOPE, None, ALU.mult))
            link(nc.vector.memset(sc[:, 3], 1.0))
            dve.sem_inc(sc_ok, 1)

    phase(finish1)

    def guard(tag, with_sum):
        def body(sb, ps, sem, block):
            ident = sb("ident", [P, P], F32)
            sc = sb("sc", [P, 5, T], F32)
            dall = sb("dall", [P, N], F32)
            neg = sb("neg", [P, 2, N], BF16)
            v = sb("v", [P, 2, N], F32)
            dn = sb("dn", [P, T], F32)
            zt = sb("zt", [P, 2, T], F32)
            m = sb("m", [P, T], F32)
            nm = sb("nm", [P, T], F32)
            tot = sb("tot", [P, T], F32)
            gate = sb("gate", [P, T], F32)
            s12 = sb("s12", [P, 2, T], F32)
            tick = sb("tick", [P, 1], F32)
            dmax = sb("dmax", [P, 2], F32)
            dn_ok, low_ready, tot_ok = sem("dn_ok"), sem("low_ready"), sem("tot_ok")
            ones = sb("ones", [P, 1], F32)
            total = sb("total", [P, 2], F32)
            s02 = sb("s02", [P, T], F32)
            low = sb("low", [P, N if with_sum else 1], F32)
            (loaded, dch, ident_ok, v_ready, v_used, nm_ready, e_ready, p_ready, ln_in, ln_ok, s_ok, gate_st,
             step) = (sem(n) for n in ("loaded", "dch", "ident_ok", "v_ready", "v_used", "nm_ready", "e_ready",
                                       "p_ready", "ln_in", "ln_ok", "s_ok", "gate_st", "step"))
            neg_in = [sem("neg_in0"), sem("neg_in1")]
            neg_used = [sem("neg_used0"), sem("neg_used1")]
            rt, ra, rs = write_rows(lambda n: s12[:, n], ident, sb, ps, sem, "w", 2)
            blk = block()

            @blk.sync
            def _(sp):
                sp.dma_start(ident[:], c_ident).then_inc(loaded, 16)
                sp.dma_start(sc[:, :4], cols[:, :4]).then_inc(loaded, 16)
                sp.dma_start(dall[:], rows[4].partition_broadcast(P)).then_inc(loaded, 16)
                with sp.Fori(0, T // 2) as i:
                    for b in range(2):
                        sp.wait_ge(neg_used[b], i + 1)
                        sp.dma_start(neg[:, b], negn[bass.ds(i * 2 + b, 1)].rearrange("a p n -> p (a n)")
                                     ).then_inc(neg_in[b], 16)
                rs(sp, 5)
                if with_sum:
                    sp.dma_start(cols[:, 4], gate[:]).then_inc(gate_st, 16)
                    sp.wait_ge(gate_st, 16)

            @blk.vector
            def _(dve):
                link = chain(dve, dch)
                for b in range(2):
                    dve.sem_inc(neg_used[b], 1)
                dve.wait_ge(loaded, 48)

                def largest(t, i, b):
                    one = bass.ds(t, 1)
                    dve.wait_ge(neg_in[b], i * 16 + 16)
                    if with_sum:
                        dve.wait_ge(v_used, t + 1)
                    nc.vector.memset(tick[:], 0.0)
                    nc.vector.tensor_tensor_reduce(out=v[:, b], in0=dall[:], in1=neg[:, b], scale=1.0,
                                                   scalar=4 * NEG, op0=ALU.add, op1=ALU.max,
                                                   accum_out=dmax[:, b:b + 1]).then_inc(neg_used[b], 1)
                    dve.wait_ge(neg_used[b], i + 2)
                    nc.vector.tensor_copy(dn[:, one], dmax[:, b:b + 1]).then_inc(dn_ok, 1)
                    if with_sum:
                        nc.vector.tensor_tensor(zt[:, 0, one], sc[:, 0, one], dmax[:, b:b + 1],
                                                ALU.add).then_inc(step, 1)
                        dve.wait_ge(step, t * 2 + 1)
                        nc.vector.tensor_scalar(zt[:, 1, one], zt[:, 0, one], SLOPE, None,
                                                ALU.mult).then_inc(step, 1)
                        dve.wait_ge(step, t * 2 + 2)
                        nc.vector.scalar_tensor_tensor(nm[:, one], zt[:, 0, one], zt[:, 1, one], ones[:], ALU.max,
                                                       ALU.mult).then_inc(nm_ready, 1)

                def larger(t, b):
                    one = bass.ds(t, 1)
                    dve.wait_ge(low_ready, t + 1)
                    nc.vector.scalar_tensor_tensor(v[:, b], v[:, b], sc[:, 0, one], low[:], ALU.add,
                                                   ALU.max).then_inc(e_ready, 1)

                def steps(i, first):
                    for b in range(2):
                        largest(i * 2 + b, i, b)
                        if with_sum and not (first and b == 0):
                            larger(i * 2 + b - 1, 1 - b)

                if with_sum:
                    nc.vector.memset(ones[:], -1.0)
                    link(nc.vector.tensor_scalar(s02[:], sc[:, 0], SLOPE, None, ALU.mult))
                    dve.sem_inc(e_ready, 1)
                steps(0, True)
                with dve.Fori(1, T // 2) as i:
                    steps(i, False)
                if with_sum:
                    larger(T - 1, 1)
                dve.wait_ge(dn_ok, T)
                link(nc.vector.tensor_tensor(zt[:, 0], sc[:, 0], dn[:], ALU.add))
                link(nc.vector.tensor_scalar(zt[:, 1], zt[:, 0], SLOPE, None, ALU.mult))
                link(nc.vector.tensor_tensor(m[:], zt[:, 0], zt[:, 1], ALU.max))
                if with_sum:
                    dve.wait_ge(ln_ok, 1)
                    link(nc.vector.tensor_tensor(m[:], m[:], tot[:], ALU.add))
                link(nc.vector.tensor_tensor(s12[:, 0], sc[:, 0], m[:], ALU.subtract))
                link(nc.vector.scalar_tensor_tensor(s12[:, 1], sc[:, 0], SLOPE, m[:], ALU.mult, ALU.subtract))
                dve.sem_inc(s_ok, 1)

            @blk.tensor
            def _(pe):
                pe.wait_ge(loaded, 48)
                pe.wait_ge(s_ok, 1)
                rt(pe)

            @blk.scalar
            def _(act):
                if with_sum:
                    act.sem_inc(v_used, 2)

                    def lower(t, b):
                        one = bass.ds(t, 1)
                        act.wait_ge(nm_ready, t + 1)
                        act.wait_ge(e_ready, t + 1)
                        nc.scalar.activation(low[:], v[:, b], ACT.Identity, bias=s02[:, one],
                                             scale=SLOPE).then_inc(low_ready, 1)

                    def exps(t, b):
                        act.wait_ge(e_ready, t + 2)
                        nc.scalar.activation(v[:, b], v[:, b], ACT.Exp, bias=nm[:, bass.ds(t, 1)],
                                             accum_out=total[:, b:b + 1]).then_inc(v_used, 1)
                        act.wait_ge(v_used, t + 3)
                        nc.scalar.copy(tot[:, bass.ds(t, 1)], total[:, b:b + 1]).then_inc(tot_ok, 1)

                    def steps(i, first):
                        for b in range(2):
                            lower(i * 2 + b, b)
                            if not (first and b == 0):
                                exps(i * 2 + b - 1, 1 - b)

                    steps(0, True)
                    with act.Fori(1, T // 2) as i:
                        steps(i, False)
                    exps(T - 1, 1)
                    act.wait_ge(tot_ok, T)
                    act.wait_ge(v_used, T + 2)
                    nc.scalar.activation(tot[:], tot[:], ACT.Ln).then_inc(ln_in, 1)
                    act.wait_ge(ln_in, 1)
                    nc.scalar.activation(gate[:], tot[:], ACT.Exp, scale=-1.0).then_inc(ln_ok, 1)
                    act.wait_ge(ln_ok, 1)
                ra(act)

        phase(body)

    def attend(tag, values, width, threshold):
        def body(sb, ps, sem, block):
            NP = T // 4
            vals = sb("vals", [P, T, P], F32)
            rhs = sb("rhs", [P, T, P + 1], F32)
            sc = sb("sc", [P, 5, T], F32)
            s12 = sb("s12", [P, 2, CW], F32)
            mask = sb("mask", [P, 2, CT, 2, P], BF16)
            low = sb("low", [P, 2, CW], F32)
            arg = sb("arg", [P, 2, CW], F32)
            prob = sb("prob", [P, 2, CW], F32)
            wts = sb("wts", [P, 2, CW], F32)
            kept = sb("kept", [P, 2, CW], F32)
            maskv = sb("maskv", [P, T, 1], BF16)
            zero = sb("zero", [P, SUB], BF16)
            st = sb("st", [P, CT, P + 1], F32)
            acc = ps("acc", [P, CT, SUB], F32)
            loaded, rhs_ok, s_in, s_used, low_ready, arg_ready, prob_ready, w_ready, k_ready, k_used = (
                sem(n) for n in ("loaded", "rhs_ok", "s_in", "s_used", "low_ready", "arg_ready", "prob_ready",
                                 "w_ready", "k_ready", "k_used"))
            acc_done, acc_copied, st_out = sem("acc_done"), sem("acc_copied"), sem("st_out")
            mask_in = [sem("mask_in0"), sem("mask_in1")]
            mask_used = [sem("mask_used0"), sem("mask_used1")]
            blk = block()
            units = [(b, k) for b in range(2) for k in range(2)]

            @blk.sync
            def _(sp):
                sp.dma_start(vals[:], values).then_inc(loaded, 16)
                sp.dma_start(sc[:, :4], cols[:, :4]).then_inc(loaded, 16)
                with sp.Fori(0, NC) as ch:
                    sp.wait_ge(s_used, ch + 1)
                    sp.dma_start(s12[:], rows[5:7, bass.ds(ch * CW, CW)].partition_broadcast(P)).then_inc(s_in, 16)
                    with sp.Fori(0, NP) as i:
                        for b in range(2):
                            sp.wait_ge(mask_used[b], ch * NP + i + 1)
                            for t in range(CT):
                                sp.dma_start(mask[:, b, t], maskT[bass.ds(ch * CT + t, 1), :,
                                                                  bass.ds(i * 4 + b * 2, 2), :]
                                             .rearrange("a p b c -> p (a b) c")).then_inc(mask_in[b], 16)

            def chunks(eng, before, first_step, second_step, after):
                with eng.Fori(0, NC) as ch:
                    before(ch)

                    def steps(i, first):
                        for u in range(4):
                            n = (ch * NP + i) * 4 + u
                            first_step(n, i * 4 + u, u)
                            if not (first and u == 0):
                                second_step(n - 1, (u - 1) % 4)
                    steps(0, True)
                    with eng.Fori(1, NP) as i:
                        steps(i, False)
                    second_step((ch + 1) * T - 1, 3)
                    after(ch)

            @blk.scalar
            def _(act):
                act.sem_inc(acc_copied, CT)
                act.sem_inc(st_out, 16)
                act.sem_inc(prob_ready, 2)
                act.wait_ge(loaded, 32)

                def lower(n, j, u):
                    act.wait_ge(arg_ready, n + 1)
                    nc.scalar.activation(low[:, u % 2], s12[:, 1], ACT.Identity,
                                         bias=sc[:, 2, bass.ds(j, 1)]).then_inc(low_ready, 1)

                def exps(n, u):
                    act.wait_ge(arg_ready, n + 3)
                    act.wait_ge(w_ready, n + 1)
                    nc.scalar.activation(prob[:, u % 2], arg[:, u % 2], ACT.Exp).then_inc(prob_ready, 1)

                def copy_out(ch):
                    act.wait_ge(st_out, ch * 16 + 16)
                    for t in range(CT):
                        act.wait_ge(acc_done, ch * CT + t + 1)
                        nc.scalar.copy(st[:, t], acc[:, t, :P + 1]).then_inc(acc_copied, 1)
                    act.wait_ge(acc_copied, (ch + 2) * CT)
                    act.dma_start(sums[bass.ds(ch * CT, CT), :, :P + 1].rearrange("t p c -> p t c"),
                                  st[:]).then_inc(st_out, 16)

                chunks(act, lambda ch: act.wait_ge(s_in, ch * 16 + 16), lower, exps, copy_out)
                act.wait_ge(st_out, 16 * NC + 16)

            @blk.vector
            def _(dve):
                dve.wait_ge(loaded, 32)
                nc.vector.memset(zero[:], 0.0)
                nc.vector.tensor_copy(rhs[:, :, :P], vals[:])
                nc.vector.tensor_copy(maskv[:], sc[:, 3].unsqueeze(2))
                nc.vector.memset(rhs[:, :, P:], 1.0).then_inc(rhs_ok, 1)
                dve.sem_inc(s_used, 1)
                dve.sem_inc(arg_ready, 2)
                dve.sem_inc(w_ready, 2)

                def larger(n, j, u):
                    dve.wait_ge(low_ready, n + 1)
                    dve.wait_ge(prob_ready, n + 1)
                    nc.vector.scalar_tensor_tensor(arg[:, u % 2], s12[:, 0],
                                                   sc[:, 1, bass.ds(j, 1)], low[:, u % 2],
                                                   ALU.add, ALU.max).then_inc(arg_ready, 1)

                def masked(n, u):
                    b, k = units[u]
                    dve.wait_ge(prob_ready, n + 3)
                    if u % 2 == 0:
                        dve.wait_ge(mask_in[b], (n - u + 4) * (4 * CT))
                    dve.wait_ge(k_used, n + 1)
                    out_, ready = (wts, w_ready)
                    nc.vector.scalar_tensor_tensor(out_[:, u % 2].rearrange("p (t c) -> p t c", c=P),
                                                   prob[:, u % 2].rearrange("p (t c) -> p t c", c=P), 2.0,
                                                   mask[:, b, :, k], ALU.min, ALU.mult).then_inc(w_ready, 1)
                    if threshold is not None:
                        dve.wait_ge(w_ready, n + 3)
                        nc.vector.scalar_tensor_tensor(kept[:, u % 2], wts[:, u % 2], threshold, wts[:, u % 2],
                                                       ALU.is_ge, ALU.mult).then_inc(k_ready, 1)

                def done(ch):
                    dve.sem_inc(s_used, 1)

                chunks(dve, lambda ch: dve.wait_ge(s_in, ch * 16 + 16), larger, masked, done)

            @blk.tensor
            def _(pe):
                pe.sem_inc(k_used, 2)
                for b in range(2):
                    pe.sem_inc(mask_used[b], 1)
                pe.wait_ge(rhs_ok, 1)
                src = wts if threshold is None else kept
                with pe.Fori(0, NC) as ch:
                    for t in range(CT):
                        pe.wait_ge(acc_copied, ch * CT + t + 1)
                        nc.tensor.matmul(acc[:, t, :P + 1], zero[:, :P], zero[:, :P + 1], start=True, stop=False)
                    with pe.Fori(0, NP) as i:
                        for u, (b, k) in enumerate(units):
                            n = (ch * NP + i) * 4 + u
                            if threshold is None:
                                pe.wait_ge(w_ready, n + 3)
                            else:
                                pe.wait_ge(k_ready, n + 1)
                            for t in range(CT):
                                if threshold is not None:
                                    nc.tensor.matmul(acc[:, t, P:P + 1], mask[:, b, t, k],
                                                     maskv[:, bass.ds(i * 4 + u, 1)].rearrange("p a c -> p (a c)"),
                                                     start=False, stop=False, skip_group_check=True)
                                last = nc.tensor.matmul(
                                    acc[:, t, :width], src[:, u % 2, t * P:(t + 1) * P],
                                    rhs[:, bass.ds(i * 4 + u, 1), :width].rearrange("p a c -> p (a c)"),
                                    start=False, stop=False, skip_group_check=True)
                            last.then_inc(k_used, 1)
                            if k == 1:
                                pe.wait_ge(k_used, n + 3)
                                pe.sem_inc(mask_used[b], 1)
                    for t in range(CT):
                        nc.tensor.matmul(acc[:, t, :P + 1], zero[:, :P], zero[:, :P + 1], start=False,
                                         stop=True).then_inc(acc_done, 1)

        phase(body)

    guard("g2", False)
    attend("t2", x_2, P + 1, None)

    def finish2(sb, ps, sem, block):
        ident = ident_of["h"] = sb("h_ident", [P, P], F32)
        X, tmp, stat = sb("h_X", [P, T, P], F32), sb("h_tmp", [P, T, P], F32), sb("h_stat", [P, 3, T], F32)
        U = sb("h_U", [P, T, P + 1], F32)
        W = sb("h_W", [P, P], F32)
        h = sb("h_h", [P, T, P], F32)
        at = sb("h_at", [P, 2, P], F32)
        sc = sb("h_sc", [P, 5, T], F32)
        loaded, dch, var_ok, std_ok, x_ok, x_st, sc_ok = (
            sem("h_" + n) for n in ("loaded", "dch", "var_ok", "std_ok", "x_ok", "x_st", "sc_ok"))
        rt, ra, rs = write_rows(lambda n: sc[:, 1], ident, sb, ps, sem, "h", 1)
        tensor, scalar, vector = project(None, sem, ps, sb, "h", lambda t: X[:, t], W, P, h, (loaded, 80), (x_ok, 1))
        blk = block()

        @blk.sync
        def _(sp):
            sp.dma_start(U[:], sums[:, :, :P + 1].rearrange("t p c -> p t c")).then_inc(loaded, 16)
            sp.dma_start(ident[:], c_ident).then_inc(loaded, 16)
            sp.dma_start(X[:], x_2).then_inc(loaded, 16)
            sp.dma_start(W[:], W3).then_inc(loaded, 16)
            sp.dma_start(at[:], a3.rearrange("(k c) a -> a k c", k=2).partition_broadcast(P)
                         .rearrange("q a k c -> q (a k) c")).then_inc(loaded, 16)
            sp.wait_ge(x_ok, 1)
            sp.dma_start(x_3, X[:]).then_inc(x_st, 16)
            sp.wait_ge(sc_ok, 1)
            sp.dma_start(cols[:, :4], sc[:, :4]).then_inc(x_st, 16)
            sp.dma_start(h_3, h[:]).then_inc(x_st, 16)
            rs(sp, 4)
            sp.wait_ge(x_st, 48)

        @blk.scalar
        def _(act):
            root(act, stat, var_ok, std_ok)
            scalar(act)
            ra(act)

        @blk.tensor
        def _(pe):
            tensor(pe)
            pe.wait_ge(sc_ok, 1)
            rt(pe)

        @blk.vector
        def _(dve):
            link = chain(dve, dch)
            dve.wait_ge(loaded, 80)
            link(nc.vector.reciprocal(stat[:, 0], U[:, :, P]))
            link(nc.vector.tensor_tensor(tmp[:], U[:, :, :P], stat[:, 0].unsqueeze(2).broadcast_to([P, T, P]),
                                         ALU.mult))
            link(nc.vector.tensor_tensor(X[:], X[:], tmp[:], ALU.add))
            normalise(dve, link, X, tmp, stat, var_ok, std_ok)
            dve.sem_inc(x_ok, 1)
            vector(dve)
            for k in range(2):
                link(nc.vector.tensor_tensor(tmp[:], h[:], at[:, k].unsqueeze(1).broadcast_to([P, T, P]), ALU.mult))
                link(nc.vector.tensor_reduce(sc[:, k], tmp[:], AX.X, ALU.add))
            link(nc.vector.tensor_reduce(stat[:, 0], h[:], AX.X, ALU.add))
            link(nc.vector.tensor_scalar(sc[:, 3], stat[:, 0], 0.0, None, ALU.not_equal))
            link(nc.vector.tensor_scalar(stat[:, 1], sc[:, 3], 1.0, -NEG, ALU.subtract, ALU.mult))
            link(nc.vector.tensor_tensor(sc[:, 1], sc[:, 1], stat[:, 1], ALU.add))
            link(nc.vector.tensor_scalar(sc[:, 2], sc[:, 1], SLOPE, None, ALU.mult))
            dve.sem_inc(sc_ok, 1)

    phase(finish2)
    guard("g3", True)
    attend("t3", h_3, P, THR)

    def finish3(sb, ps, sem, block):
        X, tmp, stat = sb("X", [P, T, P], F32), sb("tmp", [P, T, P], F32), sb("stat", [P, 3, T], F32)
        U = sb("U", [P, T, P + 1], F32)
        h = sb("h", [P, T, P], F32)
        sc = sb("sc", [P, 5, T], F32)
        loaded, dch, var_ok, std_ok, x_ok, x_st, low_ok, exp_ok = (
            sem(n) for n in ("loaded", "dch", "var_ok", "std_ok", "x_ok", "x_st", "low_ok", "exp_ok"))
        blk = block()

        @blk.sync
        def _(sp):
            sp.dma_start(U[:], sums[:, :, :P + 1].rearrange("t p c -> p t c")).then_inc(loaded, 16)
            sp.dma_start(X[:], x_3).then_inc(loaded, 16)
            sp.dma_start(h[:], h_3).then_inc(loaded, 16)
            sp.dma_start(sc[:, :5], cols[:, :5]).then_inc(loaded, 16)
            sp.wait_ge(x_ok, 1)
            sp.dma_start(tiles(out), X[:]).then_inc(x_st, 16)
            sp.wait_ge(x_st, 16)

        @blk.scalar
        def _(act):
            act.wait_ge(low_ok, 1)
            nc.scalar.activation(tmp[:], tmp[:], ACT.Exp).then_inc(exp_ok, 1)
            root(act, stat, var_ok, std_ok)

        @blk.vector
        def _(dve):
            link = chain(dve, dch)
            dve.wait_ge(loaded, 64)
            link(nc.vector.scalar_tensor_tensor(stat[:, 0], sc[:, 4], THR, U[:, :, P], ALU.is_gt, ALU.mult))
            link(nc.vector.tensor_tensor(U[:, :, :P], U[:, :, :P], stat[:, 0].unsqueeze(2).broadcast_to([P, T, P]),
                                         ALU.mult))
            link(nc.vector.tensor_tensor(h[:], h[:], U[:, :, :P], ALU.add))
            link(nc.vector.tensor_scalar(tmp[:], h[:], 0.0, None, ALU.min))
            dve.sem_inc(low_ok, 1)
            link(nc.vector.tensor_scalar(h[:], h[:], 0.0, -1.0, ALU.max, ALU.add))
            link(nc.vector.tensor_tensor(X[:], X[:], h[:], ALU.add))
            dve.wait_ge(exp_ok, 1)
            link(nc.vector.tensor_tensor(X[:], X[:], tmp[:], ALU.add))
            normalise(dve, link, X, tmp, stat, var_ok, std_ok)
            dve.sem_inc(x_ok, 1)

    phase(finish3)


_INS = ["x", "adj", "L0_gnn_W", "L0_gnn_attn_src", "L0_gnn_attn_dst", "L2_gnn_attn", "L3_gnn_W", "L3_gnn_a"]


def kernel(**inputs):
    import concourse.bacc as bacc
    from concourse.bass_utils import run_bass_kernel_spmd

    nc = bacc.Bacc("TRN2", target_bir_lowering=False, num_devices=1)
    arrays, args = {}, []
    for name, a in [(n, inputs[n]) for n in _INS] + sorted(constants().items()):
        a = np.ascontiguousarray(a)
        arrays[f"in_{name}"] = a
        args.append(nc.dram_tensor(f"in_{name}", a.shape, mybir.dt.from_np(a.dtype), kind="ExternalInput").ap())
    n = inputs["x"].shape[0]
    out = nc.dram_tensor("out", (n, P), F32, kind="ExternalOutput").ap()
    by_name = dict(zip(_INS + sorted(constants()), args))
    build(nc, *(by_name[k] for k in _INS), by_name["c_ident"], by_name["c_sel"], by_name["c_ham"],
          by_name["c_bits"], out)
    r = run_bass_kernel_spmd(nc, [arrays], core_ids=[0])
    return r.results[0]["out"]
```

```python
from contextlib import ExitStack

import concourse.bass as bass
import numpy as np
from concourse import mybir

F32 = mybir.dt.float32
BF16 = mybir.dt.bfloat16
I32 = mybir.dt.int32
ALU = mybir.AluOpType
ACT = mybir.ActivationFunctionType
AX = mybir.AxisListType
RMAX = bass.bass_isa.ReduceOp.max

P = 128
HEADS = 4
HD = P // HEADS
HW = HD + 1
SUB = 512
CT = 8
CW = CT * P
SLOPE = 0.2
EPS = 1e-5
THR = 1e-4
NEG = -(2.0 ** 100)


def constants():
    ident = np.eye(P, dtype=np.float32)
    prefix = np.triu(np.ones((P, P), np.float32), 1) + 0.5 * ident
    prefix[:, P - 1] = 1.0
    prefix[P - 1] = 0.0
    half = np.zeros((P, 1), np.float32)
    half[P - 1] = 0.5
    turn = np.arange(P, dtype=np.float32) + 0.5
    slot = np.stack([np.full((P, P), -1.0, np.float32), np.tile(turn, (P, 1))], 1)
    slot[P - 1, 0] = turn
    return {"c_half": half, "c_ident": ident, "c_prefix": prefix, "c_slot": slot.reshape(P, -1)}


def build(nc, x, adj, W0, src0, dst0, attn2, W3, a3, c_half, c_ident, c_prefix, c_slot, out):
    N = x.shape[0]
    T = N // P
    NC = N // CW
    NBLK = T + 2
    HB = T // 2
    GB = min(8, HB)
    NG = HB // GB
    U0W = 3 * HEADS * HW

    scratch = {}

    def dram(name, shape, dt):
        scratch[name] = nc.dram_tensor(name, shape, dt)
        return scratch[name].ap()

    maskT = dram("maskT", [T, P, T, P], BF16)
    negn = dram("negn", [T, P, N], BF16)
    x_1 = dram("x_1", [P, T, P], F32)
    x_2 = dram("x_2", [P, T, P], F32)
    x_3 = dram("x_3", [P, T, P], F32)
    sums = dram("sums", [T, P, U0W], F32)
    ab0 = dram("ab0", [P, 2, T, HEADS], F32)
    rhs0 = dram("rhs0", [P, T, 3, 2 * HEADS * HW], BF16)
    rows = dram("rows", [8, N], F32)
    parts_d = dram("parts_d", [P, 3, NBLK, P], BF16)
    first_d = dram("first_d", [2, NBLK + 1], I32)
    best_d = dram("best_d", [P, N], F32)
    h_3 = dram("h_3", [P, T, P], F32)
    d0_cols = dram("d0_cols", [P, T, HEADS], F32)
    cols = dram("cols", [P, 5, T], F32)

    def tiles(a):
        return a.rearrange("(t p) c -> p t c", p=P)

    phases = [0]

    def phase(body):
        phases[0] += 1
        tag = f"p{phases[0]}_"
        sems = []

        def sem(name):
            sems.append(nc.alloc_semaphore(tag + name))
            return sems[-1]

        with ExitStack() as ctx:
            body(
                lambda name, shape, dt: ctx.enter_context(nc.sbuf_tensor(tag + name, shape, dt)),
                lambda name, shape, dt: ctx.enter_context(nc.psum_tensor(tag + name, shape, dt)),
                sem,
                lambda: ctx.enter_context(nc.Block()),
            )
        nc.clear_and_free_semaphores(sems)
        nc.all_engine_barrier()

    def chain(eng, sem):
        n = [0]

        def link(ins):
            n[0] += 1
            ins.then_inc(sem, 1)
            eng.wait_ge(sem, n[0])

        return link

    def adjacency(sb, ps, sem, block):
        ident = sb("a_ident", [P, P], F32)
        identb = sb("a_identb", [P, P], BF16)
        raw = sb("a_raw", [P, 2, N // 2], I32)
        mask = sb("a_mask", [P, 2, N // 2], BF16)
        neg = sb("a_neg", [P, 2, N // 2], BF16)
        maskt = sb("a_maskt", [P, 2, HB, P], BF16)
        bank = ps("a_bank", [P, 2, NG, 2 * SUB], BF16)
        full = sb("a_full", [P, NBLK], F32)
        here = sb("a_here", [P, T + 2], F32)
        zeros = sb("a_zeros", [P, NBLK], F32)
        first = sb("a_first", [P, NBLK + 1], F32)
        firsti = sb("a_firsti", [P, 2, NBLK + 1], I32)
        tally, dch, full_ok, all_ok, first_ok, first_st = (
            sem("a_" + n) for n in ("tally", "dch", "full_ok", "all_ok", "first_ok", "first_st"))
        ident_in, ident_ok = sem("a_ident_in"), sem("a_ident_ok")
        raw_in = [sem("a_raw_in0"), sem("a_raw_in1")]
        cast_done = [sem("a_cast0"), sem("a_cast1")]
        neg_done = [sem("a_neg0"), sem("a_neg1")]
        neg_stored = [sem("a_nst0"), sem("a_nst1")]
        transposed = [sem("a_tr0"), sem("a_tr1")]
        copied = [sem("a_cp0"), sem("a_cp1")]
        mask_stored = [sem("a_mst0"), sem("a_mst1")]
        blk = block()
        adj_t = adj.rearrange("(t p) n -> t p n", p=P)

        @blk.sync
        def _(sp):
            sp.dma_start(ident[:], c_ident).then_inc(ident_in, 16)
            for hf in range(2):
                sp.dma_start(raw[:, hf], adj_t[0, :, hf * (N // 2):(hf + 1) * (N // 2)]).then_inc(raw_in[hf], 16)

            def load(t):
                for hf in range(2):
                    sp.wait_ge(cast_done[hf], t)
                    sp.wait_ge(neg_done[hf], t)
                    sp.dma_start(raw[:, hf], adj_t[bass.ds(t, 1), :, hf * (N // 2):(hf + 1) * (N // 2)]
                                 .rearrange("a p n -> p (a n)")).then_inc(raw_in[hf], 16)

            def store(t):
                for hf in range(2):
                    sp.wait_ge(neg_done[hf], t + 1)
                    sp.dma_start(negn[bass.ds(t, 1), :, hf * (N // 2):(hf + 1) * (N // 2)]
                                 .rearrange("a p n -> p (a n)"), neg[:, hf]).then_inc(neg_stored[hf], 16)
                for hf in range(2):
                    sp.wait_ge(copied[hf], t * NG + NG)
                    sp.dma_start(maskT[bass.ds(t, 1), :, hf * HB:(hf + 1) * HB, :]
                                 .rearrange("a p b c -> p (a b c)"),
                                 maskt[:, hf].rearrange("p b c -> p (b c)")).then_inc(mask_stored[hf], 16)

            with sp.Fori(1, T) as t:
                load(t)
                store(t - 1)
            store(T - 1)
            sp.wait_ge(first_ok, 1)
            sp.dma_start(first_d.rearrange("(a k) n -> a k n", a=1), firsti[0:1]).then_inc(first_st, 16)
            sp.wait_ge(first_st, 16)
            for hf in range(2):
                sp.wait_ge(neg_stored[hf], 16 * T)
                sp.wait_ge(mask_stored[hf], 16 * T)

        @blk.gpsimd
        def _(pool):
            pool.wait_ge(full_ok, 1)
            nc.gpsimd.partition_all_reduce(first[:, 1:], full[:], P, RMAX).then_inc(all_ok, 1)

        @blk.vector
        def _(dve):
            dve.wait_ge(ident_in, 16)
            link = chain(dve, dch)
            nc.vector.tensor_copy(identb[:], ident[:]).then_inc(ident_ok, 1)
            nc.vector.memset(zeros[:], 0.0)
            link(nc.vector.memset(full[:], 0.0))
            for initial in (True, False):
                def step(t, first=initial):
                    for hf in range(2):
                        dve.wait_ge(raw_in[hf], t * 16 + 16)
                        if not first:
                            dve.wait_ge(transposed[hf], t * NG)
                        nc.vector.tensor_copy(mask[:, hf], raw[:, hf]).then_inc(cast_done[hf], 1)
                        dve.wait_ge(cast_done[hf], t + 1)
                        m = mask[:, hf].rearrange("p (b c) -> p b c", c=P)
                        nc.vector.tensor_reduce(here[:, hf * HB:(hf + 1) * HB], m[:, :, :P - 1], AX.X, ALU.add)
                        nc.vector.tensor_reduce(here[:, T + hf:T + hf + 1], m[:, :, P - 1], AX.X,
                                                ALU.add).then_inc(tally, 1)
                    dve.wait_ge(tally, t * 4 + 2)
                    nc.vector.tensor_tensor(here[:, T:T + 1], here[:, T:T + 1], here[:, T + 1:], ALU.add).then_inc(
                        tally, 1)
                    dve.wait_ge(tally, t * 4 + 3)
                    nc.vector.tensor_tensor(full[:, :T + 1], full[:, :T + 1], here[:, :T + 1],
                                            ALU.max).then_inc(tally, 1)
                    if not first:
                        dve.wait_ge(mask_stored[0], t * 16)
                    for g in range(NG):
                        dve.wait_ge(transposed[0], t * NG + g + 1)
                        nc.vector.tensor_copy(maskt[:, 0, g * GB:(g + 1) * GB],
                                              bank[:, 0, g, :GB * P].rearrange("p (b c) -> p b c", c=P)).then_inc(copied[0], 1)
                if initial:
                    step(0)
                else:
                    with dve.Fori(1, T) as t:
                        step(t)
            dve.wait_ge(tally, T * 4)
            link(nc.vector.tensor_scalar(full[:], full[:], 1.0, None, ALU.max))
            dve.sem_inc(full_ok, 1)
            dve.wait_ge(all_ok, 1)
            link(nc.vector.tensor_tensor_scan(full[:], first[:, 1:], zeros[:], 0.0, ALU.add, ALU.add))
            link(nc.vector.memset(firsti[:], 0))
            link(nc.vector.tensor_copy(firsti[:, 1, :NBLK], first[:, 1:]))
            link(nc.vector.tensor_copy(firsti[:, 0, 1:], full[:]))
            dve.sem_inc(first_ok, 1)

        @blk.scalar
        def _(act):
            for first in (True, False):
                def step(t, first=first):
                    for hf in range(2):
                        act.wait_ge(raw_in[hf], t * 16 + 16)
                        if not first:
                            act.wait_ge(neg_stored[hf], t * 16)
                        nc.scalar.activation(neg[:, hf], raw[:, hf], ACT.Copy, bias=NEG,
                                             scale=-NEG).then_inc(neg_done[hf], 1)
                    if not first:
                        act.wait_ge(mask_stored[1], t * 16)
                    for g in range(NG):
                        act.wait_ge(transposed[1], t * NG + g + 1)
                        nc.scalar.copy(maskt[:, 1, g * GB:(g + 1) * GB],
                                       bank[:, 1, g, :GB * P].rearrange("p (b c) -> p b c", c=P)).then_inc(copied[1], 1)
                if first:
                    step(0)
                else:
                    with act.Fori(1, T) as t:
                        step(t)

        @blk.tensor
        def _(pe):
            pe.wait_ge(ident_ok, 1)
            for first in (True, False):
                def step(t, first=first):
                    for hf in range(2):
                        pe.wait_ge(cast_done[hf], t + 1)
                        if not first:
                            pe.wait_ge(copied[hf], t * NG)
                        for g in range(NG):
                            for b in range(GB):
                                c = (g * GB + b) * P
                                last = nc.tensor.transpose(bank[:, hf, g, b * P:(b + 1) * P],
                                                           mask[:, hf, c:c + P], identb[:])
                            last.then_inc(transposed[hf], 1)
                if first:
                    step(0)
                else:
                    with pe.Fori(1, T) as t:
                        step(t)

    phase(adjacency)

    def project(blk, sem, ps, sb, tag, xt_src, weights, width, h, ready_x, ready_w):
        xT = sb(tag + "_xT", [P, 2, P], F32)
        pT = ps(tag + "_pT", [P, 2, SUB], F32)
        pH = ps(tag + "_pH", [P, 2, SUB], F32)
        xT_ready, pT_ready, pH_ready, h_ready = (sem(tag + n) for n in ("_xTr", "_pTr", "_pHr", "_hr"))

        def tensor(pe):
            for sem_, val in (ready_x, ready_w):
                pe.wait_ge(sem_, val)
            for i in range(T // 2):
                for b in range(2):
                    if i:
                        pe.wait_ge(xT_ready, i * 2 - 1 + b)
                    nc.tensor.transpose(pT[:, b, :P], xt_src(i * 2 + b), ident_of[tag][:]).then_inc(pT_ready, 1)
                for b in range(2):
                    pe.wait_ge(xT_ready, i * 2 + b + 1)
                    if i:
                        pe.wait_ge(h_ready, i * 2 - 1 + b)
                    nc.tensor.matmul(pH[:, b, :width], xT[:, b], weights[:, :width], start=True,
                                     stop=True).then_inc(pH_ready, 1)

        def scalar(act):
            for n in range(T):
                act.wait_ge(pT_ready, n + 1)
                if n >= 2:
                    act.wait_ge(pH_ready, n - 1)
                nc.scalar.copy(xT[:, n % 2], pT[:, n % 2, :P]).then_inc(xT_ready, 1)

        def vector(dve):
            with dve.Fori(0, T // 2) as i:
                for b in range(2):
                    dve.wait_ge(pH_ready, i * 2 + b + 1)
                    nc.vector.tensor_copy(h[:, bass.ds(i * 2 + b, 1)].rearrange("p a c -> p (a c)"),
                                          pH[:, b, :width]).then_inc(h_ready, 1)
            dve.wait_ge(h_ready, T)

        return tensor, scalar, vector

    ident_of = {}

    def operands0(sb, ps, sem, block):
        ident = ident_of["o"] = sb("o_ident", [P, P], F32)
        X = sb("o_X", [P, T, P], F32)
        Wn = sb("o_Wn", [P, P], F32)
        sd = sb("o_sd", [P, 2], F32)
        heads = sb("o_heads", [P, 2 * HEADS], F32)
        Wx = sb("o_Wx", [P, P + 2 * HEADS], F32)
        h = sb("o_h", [P, T, P + 2 * HEADS], F32)
        top = sb("o_top", [P, HEADS], F32)
        c = sb("o_c", [P, HEADS], F32)
        z = sb("o_z", [P, T, 2, HEADS], F32)
        e = sb("o_e", [P, 4, T, HEADS], F32)
        negs = sb("o_negs", [P, HEADS, T], F32)
        negsT = sb("o_negsT", [P, HEADS, P], F32)
        QT = T // 4 if T >= 32 else T // 2
        f = sb("o_f", [P, QT, HEADS, 2, HW], F32)
        g = sb("o_g", [P, QT, HEADS * 2 * HW], F32)
        r3 = sb("o_r3", [P, QT, 3, HEADS * 2 * HW], BF16)
        pW = ps("o_pW", [P, 2, SUB], F32)
        pS = ps("o_pS", [P, SUB], F32)
        loaded, w_ok, heads_ok, w_mm, top_ok, c_ok = (sem("o_" + n) for n in
                                                      ("loaded", "w_ok", "heads_ok", "w_mm", "top_ok", "c_ok"))
        dcol = sb("o_dcol", [P, T, HEADS], F32)
        dcol_ok = sem("o_dcol_ok")
        dch, z_ok, e_ok, negs_ok, negs_tr, negs_cp, rows_st, r_ok, r_st, e_st = (
            sem("o_" + n) for n in ("dch", "z_ok", "e_ok", "negs_ok", "negs_tr", "negs_cp", "rows_st",
                                    "r_ok", "r_st", "e_st"))
        blk = block()
        tensor, scalar, vector = project(blk, sem, ps, sb, "o", lambda t: X[:, t], Wx, P + 2 * HEADS, h, (loaded, 16 * 5), (w_ok, 1))
        TH = min(P, HEADS * T)
        NTR = HEADS * T // TH

        @blk.sync
        def _(sp):
            sp.dma_start(X[:], tiles(x)).then_inc(loaded, 16)
            sp.dma_start(ident[:], c_ident).then_inc(loaded, 16)
            sp.dma_start(Wn[:], W0).then_inc(loaded, 16)
            sp.dma_start(sd[:, 0:1], src0.rearrange("a h d -> (h d) a")).then_inc(loaded, 16)
            sp.dma_start(sd[:, 1:2], dst0.rearrange("a h d -> (h d) a")).then_inc(loaded, 16)
            for n in range(T // QT):
                sp.wait_ge(r_ok, n + 1)
                sp.dma_start(rhs0[:, n * QT:(n + 1) * QT], r3[:]).then_inc(r_st, 16)
            sp.wait_ge(dcol_ok, 1)
            sp.wait_ge(e_ok, 4)
            sp.dma_start(ab0, e[:, 0:2]).then_inc(e_st, 16)
            sp.dma_start(d0_cols, dcol[:]).then_inc(e_st, 16)
            sp.wait_ge(negs_cp, NTR)
            rr = rows[0:HEADS].rearrange("h (t p) -> (h t) p", p=P)
            for n in range(NTR):
                sp.dma_start(rr[n * TH:(n + 1) * TH], negsT[:TH, n]).then_inc(rows_st, 16)
            sp.wait_ge(rows_st, 16 * NTR)
            sp.wait_ge(e_st, 32)
            sp.wait_ge(r_st, 16 * (T // QT))

        @blk.gpsimd
        def _(pool):
            pool.wait_ge(top_ok, 1)
            nc.gpsimd.partition_all_reduce(c[:], top[:], P, RMAX).then_inc(c_ok, 1)

        @blk.scalar
        def _(act):
            scalar(act)
            act.wait_ge(z_ok, 1)
            nc.scalar.activation(e[:, 0], z[:, :, 0], ACT.Exp).then_inc(e_ok, 1)
            act.wait_ge(z_ok, 2)
            nc.scalar.activation(e[:, 1], z[:, :, 1], ACT.Exp).then_inc(e_ok, 1)
            act.wait_ge(z_ok, 3)
            nc.scalar.activation(e[:, 2], z[:, :, 0], ACT.Exp).then_inc(e_ok, 1)
            nc.scalar.activation(e[:, 3], z[:, :, 0], ACT.Exp, scale=SLOPE).then_inc(e_ok, 1)

        @blk.vector
        def _(dve):
            link = chain(dve, dch)
            link(nc.vector.memset(heads[:], 0.0))
            dve.wait_ge(loaded, 16 * 5)
            for k in range(2):
                for hd in range(HEADS):
                    q = slice(hd * HD, (hd + 1) * HD)
                    link(nc.vector.tensor_copy(heads[q, k * HEADS + hd:k * HEADS + hd + 1], sd[q, k:k + 1]))
            dve.sem_inc(heads_ok, 1)
            dve.wait_ge(w_mm, 1)
            link(nc.vector.tensor_copy(Wx[:, :P], pW[:, 0, :P]))
            nc.vector.tensor_copy(Wx[:, P:], pW[:, 1, :2 * HEADS]).then_inc(w_ok, 1)
            vector(dve)
            s, d = h[:, :, P:P + HEADS], h[:, :, P + HEADS:]
            nc.vector.tensor_reduce(top[:], d.rearrange("p t h -> p h t"), AX.X, ALU.max).then_inc(top_ok, 1)
            nc.vector.tensor_scalar(negs[:], s.rearrange("p t h -> p h t"), -1.0, None, ALU.mult).then_inc(negs_ok, 1)
            nc.vector.tensor_copy(dcol[:], d).then_inc(dcol_ok, 1)
            dve.wait_ge(c_ok, 1)
            cb = c[:].unsqueeze(1).broadcast_to([P, T, HEADS])
            link(nc.vector.tensor_tensor(z[:, :, 1], s, cb, ALU.add))
            nc.vector.tensor_scalar(z[:, :, 0], z[:, :, 1], 1 - SLOPE, 0.0, ALU.mult, ALU.min).then_inc(z_ok, 1)
            dve.wait_ge(z_ok, 1)
            nc.vector.tensor_scalar(z[:, :, 1], z[:, :, 1], SLOPE - 1, 0.0, ALU.mult, ALU.min).then_inc(z_ok, 1)
            dve.wait_ge(e_ok, 1)
            nc.vector.tensor_tensor(z[:, :, 0], d, cb, ALU.subtract).then_inc(z_ok, 1)
            for n in range(NTR):
                dve.wait_ge(negs_tr, NTR)
                nc.vector.tensor_copy(negsT[:TH, n], pS[:TH, n * P:(n + 1) * P]).then_inc(negs_cp, 1)
            dve.wait_ge(e_ok, 4)
            for n in range(T // QT):
                ts_ = slice(n * QT, (n + 1) * QT)
                for hd in range(HEADS):
                    for k in range(2):
                        w = e[:, 2 + k, ts_, hd:hd + 1]
                        link(nc.vector.tensor_tensor(f[:, :, hd, k, :HD], h[:, ts_, hd * HD:(hd + 1) * HD],
                                                     w.broadcast_to([P, QT, HD]), ALU.mult))
                        link(nc.vector.tensor_copy(f[:, :, hd, k, HD:], w))
                ff = f[:].rearrange("p t h k c -> p t (h k c)")
                if n:
                    dve.wait_ge(r_st, 16 * n)
                link(nc.vector.tensor_copy(r3[:, :, 0], ff))
                link(nc.vector.tensor_tensor(g[:], ff, r3[:, :, 0], ALU.subtract))
                link(nc.vector.tensor_copy(r3[:, :, 1], g[:]))
                link(nc.vector.tensor_tensor(r3[:, :, 2], g[:], r3[:, :, 1], ALU.subtract))
                dve.sem_inc(r_ok, 1)

        @blk.tensor
        def _(pe):
            pe.wait_ge(loaded, 16 * 5)
            pe.wait_ge(heads_ok, 1)
            nc.tensor.transpose(pW[:, 0, :P], Wn[:], ident[:])
            nc.tensor.matmul(pW[:, 1, :2 * HEADS], Wn[:], heads[:], start=True, stop=True).then_inc(w_mm, 1)
            tensor(pe)
            pe.wait_ge(negs_ok, 1)
            nf = negs[:].rearrange("p h t -> p (h t)")
            for n in range(NTR):
                nc.tensor.transpose(pS[:TH, n * P:(n + 1) * P], nf[:, n * TH:(n + 1) * TH],
                                    ident[:]).then_inc(negs_tr, 1)

    phase(operands0)

    def sums0(sb, ps, sem, block):
        W2 = 2 * HEADS * HW
        R = sb("s_R", [P, T, 3, HEADS, 2, HW], BF16)
        hd_cols = sb("s_d", [P, T, HEADS], F32)
        negs = sb("s_negs", [P, HEADS, CW], F32)
        mask = sb("s_mask", [P, 2, CT, 2, P], BF16)
        m1 = sb("s_m1", [P, 2, HEADS, CW], BF16)
        zero = sb("s_zero", [P, SUB], BF16)
        st = sb("s_st", [P, CT, U0W], F32)
        acc = ps("s_acc", [P, CT, SUB], F32)
        loaded, zero_ok, negs_in, chunk_cmp = (sem("s_" + n) for n in ("loaded", "zero_ok", "negs_in", "chunk_cmp"))
        mask_in = [sem("s_mi0"), sem("s_mi1")]
        mask_used = [sem("s_mu0"), sem("s_mu1")]
        m1_ready, m1_used, acc_done, acc_copied, st_out = (sem("s_" + n) for n in
                                                          ("m1r", "m1u", "accd", "accc", "sto"))
        blk = block()
        NP = T // 4

        @blk.sync
        def _(sp):
            sp.dma_start(R[:], rhs0.rearrange("p t k (h u c) -> p t k h u c", h=HEADS, u=2)).then_inc(loaded, 16)
            sp.dma_start(hd_cols[:], d0_cols).then_inc(loaded, 16)
            with sp.Fori(0, NC) as ch:
                sp.wait_ge(chunk_cmp, ch + 1)
                sp.dma_start(negs[:], rows[0:HEADS, bass.ds(ch * CW, CW)].partition_broadcast(P)).then_inc(negs_in, 16)
                with sp.Fori(0, NP) as i:
                    for b in range(2):
                        sp.wait_ge(mask_used[b], ch * NP + i + 1)
                        for t in range(CT):
                            sp.dma_start(mask[:, b, t], maskT[bass.ds(ch * CT + t, 1), :, bass.ds(i * 4 + b * 2, 2), :]
                                         .rearrange("a p b c -> p (a b) c")).then_inc(mask_in[b], 16)

        @blk.vector
        def _(dve):
            nc.vector.memset(zero[:], 0.0).then_inc(zero_ok, 1)
            dve.sem_inc(chunk_cmp, 1)
            dve.wait_ge(loaded, 32)
            with dve.Fori(0, NC) as ch:
                with dve.Fori(0, NP) as i:
                    dve.wait_ge(negs_in, ch * 16 + 16)
                    for b in range(2):
                        dve.wait_ge(mask_in[b], (ch * NP + i + 1) * (16 * CT))
                        for k in range(2):
                            dve.wait_ge(m1_used, (ch * NP + i) * 4 + b * 2 + k + 1)
                            for hd in range(HEADS):
                                last = nc.vector.scalar_tensor_tensor(
                                    m1[:, k, hd].rearrange("p (t c) -> p t c", c=P),
                                    negs[:, hd].rearrange("p (t c) -> p t c", c=P),
                                    hd_cols[:, bass.ds(i * 4 + b * 2 + k, 1), hd:hd + 1].rearrange("p a c -> p (a c)"),
                                    mask[:, b, :, k], ALU.is_lt, ALU.mult)
                            last.then_inc(m1_ready, 1)
                dve.wait_ge(m1_ready, (ch + 1) * T)
                dve.sem_inc(chunk_cmp, 1)

        @blk.tensor
        def _(pe):
            pe.sem_inc(m1_used, 2)
            for b in range(2):
                pe.sem_inc(mask_used[b], 1)
            pe.wait_ge(zero_ok, 1)
            pe.wait_ge(loaded, 32)
            with pe.Fori(0, NC) as ch:
                for t in range(CT):
                    pe.wait_ge(acc_copied, ch * CT + t + 1)
                    nc.tensor.matmul(acc[:, t, :U0W], zero[:, :P], zero[:, :U0W], start=True, stop=False)
                with pe.Fori(0, NP) as i:
                    for b in range(2):
                        for k in range(2):
                            pe.wait_ge(m1_ready, (ch * NP + i) * 4 + b * 2 + k + 1)
                            j = i * 4 + b * 2 + k
                            for t in range(CT):
                                for part in range(3):
                                    nc.tensor.matmul(
                                        acc[:, t, W2:U0W].rearrange("p (h c) -> p h c", c=HW), mask[:, b, t, k],
                                        R[:, bass.ds(j, 1), part, :, 1].rearrange("p a h c -> p (a h) c"),
                                        start=False, stop=False, skip_group_check=True)
                                for hd in range(HEADS):
                                    for part in range(3):
                                        last = nc.tensor.matmul(
                                            acc[:, t, hd * 2 * HW:(hd + 1) * 2 * HW],
                                            m1[:, k, hd, t * P:(t + 1) * P],
                                            R[:, bass.ds(j, 1), part, hd].rearrange("p a u c -> p (a u c)"),
                                            start=False, stop=False, skip_group_check=True)
                            last.then_inc(m1_used, 1)
                        pe.wait_ge(m1_used, (ch * NP + i) * 4 + b * 2 + 4)
                        pe.sem_inc(mask_used[b], 1)
                for t in range(CT):
                    nc.tensor.matmul(acc[:, t, :U0W], zero[:, :P], zero[:, :U0W], start=False,
                                     stop=True).then_inc(acc_done, 1)

        @blk.scalar
        def _(act):
            act.sem_inc(acc_copied, CT)
            act.sem_inc(st_out, 16)
            with act.Fori(0, NC) as ch:
                act.wait_ge(st_out, ch * 16 + 16)
                for t in range(CT):
                    act.wait_ge(acc_done, ch * CT + t + 1)
                    nc.scalar.copy(st[:, t], acc[:, t, :U0W]).then_inc(acc_copied, 1)
                act.wait_ge(acc_copied, (ch + 2) * CT)
                act.dma_start(sums[bass.ds(ch * CT, CT)].rearrange("t p c -> p t c"), st[:]).then_inc(st_out, 16)
            act.wait_ge(st_out, 16 * NC + 16)

    phase(sums0)

    def normalise(dve, link, X, tmp, stat, var_ok, std_ok):
        wide = lambda a: a.unsqueeze(2).broadcast_to([P, T, P])
        link(nc.vector.tensor_reduce(stat[:, 0], X[:], AX.X, ALU.add))
        link(nc.vector.tensor_scalar(stat[:, 0], stat[:, 0], 1.0 / P, None, ALU.mult))
        link(nc.vector.tensor_tensor(X[:], X[:], wide(stat[:, 0]), ALU.subtract))
        link(nc.vector.tensor_tensor(tmp[:], X[:], X[:], ALU.mult))
        link(nc.vector.tensor_reduce(stat[:, 1], tmp[:], AX.X, ALU.add))
        nc.vector.tensor_scalar(stat[:, 1], stat[:, 1], 1.0 / P, EPS, ALU.mult, ALU.add).then_inc(var_ok, 1)
        dve.wait_ge(std_ok, 1)
        link(nc.vector.reciprocal(stat[:, 0], stat[:, 2]))
        link(nc.vector.tensor_tensor(X[:], X[:], wide(stat[:, 0]), ALU.mult))

    def root(act, stat, var_ok, std_ok):
        act.wait_ge(var_ok, 1)
        nc.scalar.activation(stat[:, 2], stat[:, 1], ACT.Sqrt).then_inc(std_ok, 1)

    def finish0(sb, ps, sem, block):
        X, tmp, stat = sb("f_X", [P, T, P], F32), sb("f_tmp", [P, T, P], F32), sb("f_stat", [P, 3, T], F32)
        U = sb("f_U", [P, T, U0W], F32)
        ab = sb("f_ab", [P, 2, T, HEADS], F32)
        loaded, dch, var_ok, std_ok, x_ok, x_st = (sem("f_" + n) for n in
                                                   ("loaded", "dch", "var_ok", "std_ok", "x_ok", "x_st"))
        blk = block()

        @blk.sync
        def _(sp):
            sp.dma_start(U[:], sums[:, :, :U0W].rearrange("t p c -> p t c")).then_inc(loaded, 16)
            sp.dma_start(ab[:], ab0).then_inc(loaded, 16)
            sp.dma_start(X[:], tiles(x)).then_inc(loaded, 16)
            sp.wait_ge(x_ok, 1)
            sp.dma_start(x_1, X[:]).then_inc(x_st, 16)
            sp.wait_ge(x_st, 16)

        @blk.scalar
        def _(act):
            root(act, stat, var_ok, std_ok)

        @blk.vector
        def _(dve):
            link = chain(dve, dch)
            dve.wait_ge(loaded, 48)
            for hd in range(HEADS):
                u = U[:, :, hd * 2 * HW:hd * 2 * HW + HW]
                v = U[:, :, hd * 2 * HW + HW:(hd + 1) * 2 * HW]
                w = U[:, :, 2 * HEADS * HW + hd * HW:2 * HEADS * HW + (hd + 1) * HW]
                link(nc.vector.tensor_tensor(w, w, v, ALU.subtract))
                link(nc.vector.tensor_tensor(w, w, ab[:, 1, :, hd:hd + 1].broadcast_to([P, T, HW]), ALU.mult))
                link(nc.vector.tensor_tensor(u, u, ab[:, 0, :, hd:hd + 1].broadcast_to([P, T, HW]), ALU.mult))
                link(nc.vector.tensor_tensor(u, u, w, ALU.add))
                link(nc.vector.reciprocal(w[:, :, HD:], u[:, :, HD:]))
                link(nc.vector.tensor_tensor(u[:, :, :HD], u[:, :, :HD], w[:, :, HD:].broadcast_to([P, T, HD]),
                                             ALU.mult))
                xs = X[:, :, hd * HD:(hd + 1) * HD]
                link(nc.vector.tensor_tensor(xs, xs, u[:, :, :HD], ALU.add))
            normalise(dve, link, X, tmp, stat, var_ok, std_ok)
            dve.sem_inc(x_ok, 1)

    phase(finish0)

    def parts1(sb, ps, sem, block):
        xe = sb("xe", [P, NBLK, P], F32)
        none = sb("none", [1, NBLK * P], F32)
        parts = sb("parts", [P, 3, NBLK, P], BF16)
        zeroed, loaded, dch, parts_ok, stored = (sem(n) for n in ("zeroed", "loaded", "dch", "parts_ok", "stored"))
        blk = block()

        @blk.sync
        def _(sp):
            sp.wait_ge(zeroed, 2)
            sp.dma_start(xe[:P - 1, :T], x_1[:P - 1]).then_inc(loaded, 16)
            sp.dma_start(xe[:T, T], x_1[P - 1]).then_inc(loaded, 16)
            sp.dma_start(xe[P - 1:], none[:]).then_inc(loaded, 16)
            sp.wait_ge(parts_ok, 1)
            sp.dma_start(parts_d, parts[:]).then_inc(stored, 16)
            sp.wait_ge(stored, 16)

        @blk.vector
        def _(dve):
            link = chain(dve, dch)
            nc.vector.memset(none[:], NEG).then_inc(zeroed, 1)
            nc.vector.memset(xe[:], 0.0).then_inc(zeroed, 1)
            dve.wait_ge(loaded, 48)
            link(nc.vector.tensor_copy(parts[:, 0], xe[:]))
            link(nc.vector.tensor_tensor(xe[:], xe[:], parts[:, 0], ALU.subtract))
            link(nc.vector.tensor_copy(parts[:, 1], xe[:]))
            link(nc.vector.tensor_tensor(parts[:, 2], xe[:], parts[:, 1], ALU.subtract))
            dve.sem_inc(parts_ok, 1)

    phase(parts1)

    def maxima1(sb, ps, sem, block):
        UW = 2 * SUB
        NU = N // UW
        GWU = 2 if NU >= 4 else 1
        NGR = NU // GWU
        AHEAD = 2 * GWU
        STEP = min(NU, 2)
        prew = sb("prew", [P, P], F32)
        pre = sb("pre", [P, P], BF16)
        half = sb("half", [P, 1], F32)
        slot = sb("slot", [P, 2, P], F32)
        first = sb("first", [1, 2, NBLK + 1], I32)
        best = sb("best", [P, N], F32)
        mask = sb("mask", [P, 2, T, P], BF16)
        nothing = sb("nothing", [P, T, P], BF16)
        order = sb("order", [P, 2, N], BF16)
        parts = sb("parts", [P, 3, NBLK, P], BF16)
        hot = sb("hot", [P, 2, GWU * UW], BF16)
        count = ps("count", [P, 2, 2, SUB], F32)
        rowv = ps("rowv", [P, 2, 2, SUB], F32)
        (loaded, pre_ok, best_ok, zero_ok, count_ready, order_ready, block_done, hot_ready, row_ready, row_used,
         best_st) = (sem(n) for n in ("loaded", "pre_ok", "best_ok", "zero_ok", "count_ready", "order_ready",
                                      "block_done", "hot_ready", "row_ready", "row_used", "best_st"))
        mask_in = [sem("mask_in0"), sem("mask_in1")]
        blk = block()

        @blk.sync
        def _(sp):
            sp.dma_start(prew[:], c_prefix).then_inc(loaded, 16)
            sp.dma_start(half[:], c_half).then_inc(loaded, 16)
            sp.dma_start(slot[:].rearrange("p k n -> p (k n)"), c_slot).then_inc(loaded, 16)
            sp.dma_start(first[:], first_d.rearrange("(a k) n -> a k n", a=1)).then_inc(loaded, 16)
            sp.dma_start(parts[:], parts_d).then_inc(loaded, 16)
            for b in range(2):
                sp.dma_start(mask[:, b], maskT[:, :, b, :].rearrange("t p c -> p t c")).then_inc(mask_in[b], 16)
                sp.sem_inc(mask_in[b], 16)
            with sp.Fori(1, T // 2) as i:
                for b in range(2):
                    sp.wait_ge(count_ready, (i * 2 + b - 1) * NU)
                    sp.dma_start(mask[:, b], maskT[:, :, bass.ds(i * 2 + b, 1), :]
                                 .rearrange("t p a c -> p t (a c)")).then_inc(mask_in[b], 32)
            sp.wait_ge(zero_ok, 1)
            sp.wait_ge(count_ready, (T - 1) * NU)
            sp.dma_start(mask[:T, 0], maskT[:, P - 1].rearrange("t b c -> b t c")).then_inc(mask_in[0], 16)
            sp.dma_start(mask[T:, 0], nothing[T:]).then_inc(mask_in[0], 16)
            sp.wait_ge(count_ready, T * NU)
            sp.dma_start(mask[:, 1], nothing[:]).then_inc(mask_in[1], 32)
            sp.wait_ge(count_ready, (T + 1) * NU)
            sp.dma_start(mask[:, 0], nothing[:]).then_inc(mask_in[0], 32)
            sp.wait_ge(block_done, NBLK + 1)
            sp.dma_start(best_d, best[:]).then_inc(best_st, 16)
            sp.wait_ge(best_st, 16)

        @blk.tensor
        def _(pe):
            def counts(b, k):
                for u in range(NU):
                    pe.wait_ge(order_ready, b * NU + u + 1)
                    for s in range(2):
                        t = (2 * u + s) * 4
                        last = nc.tensor.matmul(count[:, u % 2, s].rearrange("p (t c) -> p t c", c=P) if NU > 1 else
                                                count[:, 0, s].rearrange("p (t c) -> p t c", c=P),
                                                pre[:], mask[:, k, t:t + 4], start=True, stop=True)
                    last.then_inc(count_ready, 1)

            pe.wait_ge(pre_ok, 1)
            pe.sem_inc(row_ready, AHEAD)
            pe.wait_ge(mask_in[0], 32)
            counts(0, 0)
            with pe.Fori(0, NBLK // 2) as i:
                for k in range(2):
                    b = i * 2 + k
                    pe.wait_ge(mask_in[1 - k], (i + 1 + k) * 32)
                    counts(b + 1, 1 - k)
                    lo = pe.value_load(first[0:1, 0, bass.ds(b, 1)], min_val=0, max_val=NBLK * P)
                    hi = pe.value_load(first[0:1, 0, bass.ds(b + 1, 1)], min_val=1, max_val=NBLK * P)
                    with pe.Fori(lo, hi) as n:
                        for u in range(NU):
                            g, r = divmod(u, GWU)
                            if r == 0:
                                pe.wait_ge(hot_ready, n * NGR + g + 1)
                            pe.wait_ge(row_used, n * NU + u + 1)
                            for part in range(3):
                                for s in range(2):
                                    c = (r * 2 + s) * SUB
                                    last = nc.tensor.matmul(
                                        rowv[:, u % 2, s],
                                        parts[:, part, bass.ds(b, 1)].rearrange("p a c -> p (a c)"),
                                        hot[:, g % 2, c:c + SUB], start=part == 0, stop=part == 2)
                            last.then_inc(row_ready, 1)

        @blk.scalar
        def _(act):
            def orders(b, k):
                for u in range(NU):
                    act.wait_ge(count_ready, b * NU + u + 1)
                    nc.scalar.activation(order[:, k, u * UW:(u + 1) * UW].rearrange("p (s c) -> p s c", s=2),
                                         count[:, u % 2], ACT.Identity, bias=half[:]).then_inc(order_ready, 1)

            act.sem_inc(order_ready, 2)
            act.wait_ge(loaded, 80)
            orders(0, 0)
            with act.Fori(0, NBLK // 2) as i:
                for k in range(2):
                    act.wait_ge(block_done, i * 2 + k + 1)
                    orders(i * 2 + k + 1, 1 - k)

        @blk.vector
        def _(dve):
            dve.wait_ge(loaded, 80)
            nc.vector.memset(nothing[:], 0.0).then_inc(zero_ok, 1)
            nc.vector.tensor_copy(pre[:], prew[:]).then_inc(pre_ok, 1)
            nc.vector.memset(best[:], NEG).then_inc(best_ok, 1)
            dve.wait_ge(best_ok, 1)
            dve.sem_inc(row_used, 2)
            dve.sem_inc(block_done, 1)
            with dve.Fori(0, NBLK // 2) as i:
                for k in range(2):
                    b = i * 2 + k
                    lo = dve.value_load(first[0:1, 0, bass.ds(b, 1)], min_val=0, max_val=NBLK * P)
                    turns = dve.value_load(first[0:1, 1, bass.ds(b, 1)], min_val=1, max_val=P)
                    with dve.Fori(0, turns) as turn:
                        n = lo + turn

                        def pick(g):
                            w = GWU * UW
                            dve.wait_ge(order_ready, (b + 1) * NU + 2)
                            dve.wait_ge(row_ready, (n * NGR + g + 1) * GWU)
                            nc.vector.tensor_scalar(hot[:, g % 2], order[:, k, g * w:(g + 1) * w],
                                                    slot[:, 0, bass.ds(turn, 1)], slot[:, 1, bass.ds(turn, 1)],
                                                    ALU.max, ALU.is_equal).then_inc(hot_ready, 1)

                        def take(u):
                            dve.wait_ge(row_ready, n * NU + u + 1 + AHEAD)
                            dve.wait_ge(row_used, n * NU + u + 3 - STEP)
                            cols_ = best[:, u * UW:(u + 1) * UW].rearrange("p (s c) -> p s c", s=2)
                            nc.vector.tensor_tensor(cols_, rowv[:, u % 2], cols_, ALU.max).then_inc(row_used, 1)

                        pick(0)
                        for g in range(NGR):
                            if g + 1 < NGR:
                                pick(g + 1)
                            for r in range(GWU):
                                take(g * GWU + r)
                    dve.wait_ge(row_used, (lo + turns) * NU + 2)
                    dve.sem_inc(block_done, 1)

    phase(maxima1)

    def write_rows(pe_in, ident, sb, ps, sem, tag, count):
        flat = sb(tag + "_flat", [P, count, P], F32)
        pF = ps(tag + "_pF", [P, count, SUB], F32)
        tr, cp, st = sem(tag + "_rtr"), sem(tag + "_rcp"), sem(tag + "_rst")

        def tensor(pe):
            for n in range(count):
                nc.tensor.transpose(pF[:T, n, :P], pe_in(n), ident[:]).then_inc(tr, 1)

        def scalar(act):
            for n in range(count):
                act.wait_ge(tr, n + 1)
                nc.scalar.copy(flat[:T, n], pF[:T, n, :P]).then_inc(cp, 1)

        def sync(sp, first_row):
            for n in range(count):
                sp.wait_ge(cp, n + 1)
                sp.dma_start(rows[first_row + n].rearrange("(t p) -> t p", p=P), flat[:T, n]).then_inc(st, 16)
            sp.wait_ge(st, 16 * count)

        return tensor, scalar, sync

    def finish1(sb, ps, sem, block):
        X, tmp, stat = sb("g_X", [P, T, P], F32), sb("g_tmp", [P, T, P], F32), sb("g_stat", [P, 3, T], F32)
        ident = sb("g_ident", [P, P], F32)
        best = sb("g_best", [P, N], F32)
        at = sb("g_at", [P, 2, P], F32)
        sc = sb("g_sc", [P, 5, T], F32)
        y = ps("g_y", [P, 4, SUB], F32)
        loaded, dch, var_ok, std_ok, x_ok, x_st, best_ok, tr, tr_used, sc_ok = (
            sem("g_" + n) for n in ("loaded", "dch", "var_ok", "std_ok", "x_ok", "x_st", "best_ok", "tr", "tr_used",
                                    "sc_ok"))
        rt, ra, rs = write_rows(lambda n: sc[:, 1], ident, sb, ps, sem, "g", 1)
        blk = block()

        @blk.sync
        def _(sp):
            sp.dma_start(best[:], best_d).then_inc(loaded, 16)
            sp.dma_start(ident[:], c_ident).then_inc(loaded, 16)
            sp.dma_start(X[:], x_1).then_inc(loaded, 16)
            sp.dma_start(at[:], attn2.rearrange("(k c) a -> a k c", k=2).partition_broadcast(P)
                         .rearrange("q a k c -> q (a k) c")).then_inc(loaded, 16)
            sp.wait_ge(x_ok, 1)
            sp.dma_start(x_2, X[:]).then_inc(x_st, 16)
            sp.wait_ge(sc_ok, 1)
            sp.dma_start(cols[:, :4], sc[:, :4]).then_inc(x_st, 16)
            rs(sp, 4)
            sp.wait_ge(x_st, 32)

        @blk.scalar
        def _(act):
            root(act, stat, var_ok, std_ok)
            ra(act)

        @blk.tensor
        def _(pe):
            pe.wait_ge(loaded, 64)
            pe.wait_ge(best_ok, 1)
            for t in range(T):
                if t >= 4:
                    pe.wait_ge(tr_used, t - 3)
                nc.tensor.transpose(y[:, t % 4, :P], best[:, t * P:(t + 1) * P], ident[:]).then_inc(tr, 1)
            pe.wait_ge(sc_ok, 1)
            rt(pe)

        @blk.vector
        def _(dve):
            link = chain(dve, dch)
            dve.wait_ge(loaded, 64)
            link(nc.vector.scalar_tensor_tensor(best[:], best[:], NEG / 2, best[:], ALU.is_gt, ALU.mult))
            dve.sem_inc(best_ok, 1)
            for t in range(T):
                dve.wait_ge(tr, t + 1)
                nc.vector.tensor_tensor(X[:, t], y[:, t % 4, :P], X[:, t], ALU.add).then_inc(tr_used, 1)
            dve.wait_ge(tr_used, T)
            normalise(dve, link, X, tmp, stat, var_ok, std_ok)
            dve.sem_inc(x_ok, 1)
            for k in range(2):
                link(nc.vector.tensor_tensor(tmp[:], X[:], at[:, k].unsqueeze(1).broadcast_to([P, T, P]), ALU.mult))
                link(nc.vector.tensor_reduce(sc[:, k], tmp[:], AX.X, ALU.add))
            link(nc.vector.tensor_scalar(sc[:, 2], sc[:, 1], SLOPE, None, ALU.mult))
            link(nc.vector.memset(sc[:, 3], 1.0))
            dve.sem_inc(sc_ok, 1)

    phase(finish1)

    def guard(tag, with_sum):
        def body(sb, ps, sem, block):
            ident = sb("ident", [P, P], F32)
            sc = sb("sc", [P, 5, T], F32)
            dall = sb("dall", [P, N], F32)
            neg = sb("neg", [P, 2, N], BF16)
            v = sb("v", [P, 2, N], F32)
            dn = sb("dn", [P, T], F32)
            zt = sb("zt", [P, 2, T], F32)
            m = sb("m", [P, T], F32)
            nm = sb("nm", [P, T], F32)
            tot = sb("tot", [P, T], F32)
            gate = sb("gate", [P, T], F32)
            s12 = sb("s12", [P, 2, T], F32)
            tick = sb("tick", [P, 1], F32)
            dmax = sb("dmax", [P, 2], F32)
            dn_ok, low_ready, tot_ok = sem("dn_ok"), sem("low_ready"), sem("tot_ok")
            ones = sb("ones", [P, 1], F32)
            total = sb("total", [P, 2], F32)
            s02 = sb("s02", [P, T], F32)
            low = sb("low", [P, N if with_sum else 1], F32)
            (loaded, dch, ident_ok, v_ready, v_used, nm_ready, e_ready, p_ready, ln_in, ln_ok, s_ok, gate_st,
             step) = (sem(n) for n in ("loaded", "dch", "ident_ok", "v_ready", "v_used", "nm_ready", "e_ready",
                                       "p_ready", "ln_in", "ln_ok", "s_ok", "gate_st", "step"))
            neg_in = [sem("neg_in0"), sem("neg_in1")]
            neg_used = [sem("neg_used0"), sem("neg_used1")]
            rt, ra, rs = write_rows(lambda n: s12[:, n], ident, sb, ps, sem, "w", 2)
            blk = block()

            @blk.sync
            def _(sp):
                sp.dma_start(ident[:], c_ident).then_inc(loaded, 16)
                sp.dma_start(sc[:, :4], cols[:, :4]).then_inc(loaded, 16)
                sp.dma_start(dall[:], rows[4].partition_broadcast(P)).then_inc(loaded, 16)
                with sp.Fori(0, T // 2) as i:
                    for b in range(2):
                        sp.wait_ge(neg_used[b], i + 1)
                        sp.dma_start(neg[:, b], negn[bass.ds(i * 2 + b, 1)].rearrange("a p n -> p (a n)")
                                     ).then_inc(neg_in[b], 16)
                rs(sp, 5)
                if with_sum:
                    sp.dma_start(cols[:, 4], gate[:]).then_inc(gate_st, 16)
                    sp.wait_ge(gate_st, 16)

            @blk.vector
            def _(dve):
                link = chain(dve, dch)
                for b in range(2):
                    dve.sem_inc(neg_used[b], 1)
                dve.wait_ge(loaded, 48)

                def largest(t, i, b):
                    one = bass.ds(t, 1)
                    dve.wait_ge(neg_in[b], i * 16 + 16)
                    if with_sum:
                        dve.wait_ge(v_used, t + 1)
                    nc.vector.memset(tick[:], 0.0)
                    nc.vector.tensor_tensor_reduce(out=v[:, b], in0=dall[:], in1=neg[:, b], scale=1.0,
                                                   scalar=4 * NEG, op0=ALU.add, op1=ALU.max,
                                                   accum_out=dmax[:, b:b + 1]).then_inc(neg_used[b], 1)
                    dve.wait_ge(neg_used[b], i + 2)
                    nc.vector.tensor_copy(dn[:, one], dmax[:, b:b + 1]).then_inc(dn_ok, 1)
                    if with_sum:
                        nc.vector.tensor_tensor(zt[:, 0, one], sc[:, 0, one], dmax[:, b:b + 1],
                                                ALU.add).then_inc(step, 1)
                        dve.wait_ge(step, t * 2 + 1)
                        nc.vector.tensor_scalar(zt[:, 1, one], zt[:, 0, one], SLOPE, None,
                                                ALU.mult).then_inc(step, 1)
                        dve.wait_ge(step, t * 2 + 2)
                        nc.vector.scalar_tensor_tensor(nm[:, one], zt[:, 0, one], zt[:, 1, one], ones[:], ALU.max,
                                                       ALU.mult).then_inc(nm_ready, 1)

                def larger(t, b):
                    one = bass.ds(t, 1)
                    dve.wait_ge(low_ready, t + 1)
                    nc.vector.scalar_tensor_tensor(v[:, b], v[:, b], sc[:, 0, one], low[:], ALU.add,
                                                   ALU.max).then_inc(e_ready, 1)

                def steps(i, first):
                    for b in range(2):
                        largest(i * 2 + b, i, b)
                        if with_sum and not (first and b == 0):
                            larger(i * 2 + b - 1, 1 - b)

                if with_sum:
                    nc.vector.memset(ones[:], -1.0)
                    link(nc.vector.tensor_scalar(s02[:], sc[:, 0], SLOPE, None, ALU.mult))
                    dve.sem_inc(e_ready, 1)
                steps(0, True)
                with dve.Fori(1, T // 2) as i:
                    steps(i, False)
                if with_sum:
                    larger(T - 1, 1)
                dve.wait_ge(dn_ok, T)
                link(nc.vector.tensor_tensor(zt[:, 0], sc[:, 0], dn[:], ALU.add))
                link(nc.vector.tensor_scalar(zt[:, 1], zt[:, 0], SLOPE, None, ALU.mult))
                link(nc.vector.tensor_tensor(m[:], zt[:, 0], zt[:, 1], ALU.max))
                if with_sum:
                    dve.wait_ge(ln_ok, 1)
                    link(nc.vector.tensor_tensor(m[:], m[:], tot[:], ALU.add))
                link(nc.vector.tensor_tensor(s12[:, 0], sc[:, 0], m[:], ALU.subtract))
                link(nc.vector.scalar_tensor_tensor(s12[:, 1], sc[:, 0], SLOPE, m[:], ALU.mult, ALU.subtract))
                dve.sem_inc(s_ok, 1)

            @blk.tensor
            def _(pe):
                pe.wait_ge(loaded, 48)
                pe.wait_ge(s_ok, 1)
                rt(pe)

            @blk.scalar
            def _(act):
                if with_sum:
                    act.sem_inc(v_used, 2)

                    def lower(t, b):
                        one = bass.ds(t, 1)
                        act.wait_ge(nm_ready, t + 1)
                        act.wait_ge(e_ready, t + 1)
                        nc.scalar.activation(low[:], v[:, b], ACT.Identity, bias=s02[:, one],
                                             scale=SLOPE).then_inc(low_ready, 1)

                    def exps(t, b):
                        act.wait_ge(e_ready, t + 2)
                        nc.scalar.activation(v[:, b], v[:, b], ACT.Exp, bias=nm[:, bass.ds(t, 1)],
                                             accum_out=total[:, b:b + 1]).then_inc(v_used, 1)
                        act.wait_ge(v_used, t + 3)
                        nc.scalar.copy(tot[:, bass.ds(t, 1)], total[:, b:b + 1]).then_inc(tot_ok, 1)

                    def steps(i, first):
                        for b in range(2):
                            lower(i * 2 + b, b)
                            if not (first and b == 0):
                                exps(i * 2 + b - 1, 1 - b)

                    steps(0, True)
                    with act.Fori(1, T // 2) as i:
                        steps(i, False)
                    exps(T - 1, 1)
                    act.wait_ge(tot_ok, T)
                    act.wait_ge(v_used, T + 2)
                    nc.scalar.activation(tot[:], tot[:], ACT.Ln).then_inc(ln_in, 1)
                    act.wait_ge(ln_in, 1)
                    nc.scalar.activation(gate[:], tot[:], ACT.Exp, scale=-1.0).then_inc(ln_ok, 1)
                    act.wait_ge(ln_ok, 1)
                ra(act)

        phase(body)

    def attend(tag, values, width, threshold):
        def body(sb, ps, sem, block):
            NP = T // 4
            vals = sb("vals", [P, T, P], F32)
            rhs = sb("rhs", [P, T, P + 1], F32)
            sc = sb("sc", [P, 5, T], F32)
            s12 = sb("s12", [P, 2, CW], F32)
            mask = sb("mask", [P, 2, CT, 2, P], BF16)
            low = sb("low", [P, 2, CW], F32)
            arg = sb("arg", [P, 2, CW], F32)
            prob = sb("prob", [P, 2, CW], F32)
            wts = sb("wts", [P, 2, CW], F32)
            kept = sb("kept", [P, 2, CW], F32)
            maskv = sb("maskv", [P, T, 1], BF16)
            zero = sb("zero", [P, SUB], BF16)
            st = sb("st", [P, CT, P + 1], F32)
            acc = ps("acc", [P, CT, SUB], F32)
            loaded, rhs_ok, s_in, s_used, low_ready, arg_ready, prob_ready, w_ready, k_ready, k_used = (
                sem(n) for n in ("loaded", "rhs_ok", "s_in", "s_used", "low_ready", "arg_ready", "prob_ready",
                                 "w_ready", "k_ready", "k_used"))
            acc_done, acc_copied, st_out = sem("acc_done"), sem("acc_copied"), sem("st_out")
            mask_in = [sem("mask_in0"), sem("mask_in1")]
            mask_used = [sem("mask_used0"), sem("mask_used1")]
            blk = block()
            units = [(b, k) for b in range(2) for k in range(2)]

            @blk.sync
            def _(sp):
                sp.dma_start(vals[:], values).then_inc(loaded, 16)
                sp.dma_start(sc[:, :4], cols[:, :4]).then_inc(loaded, 16)
                with sp.Fori(0, NC) as ch:
                    sp.wait_ge(s_used, ch + 1)
                    sp.dma_start(s12[:], rows[5:7, bass.ds(ch * CW, CW)].partition_broadcast(P)).then_inc(s_in, 16)
                    with sp.Fori(0, NP) as i:
                        for b in range(2):
                            sp.wait_ge(mask_used[b], ch * NP + i + 1)
                            for t in range(CT):
                                sp.dma_start(mask[:, b, t], maskT[bass.ds(ch * CT + t, 1), :,
                                                                  bass.ds(i * 4 + b * 2, 2), :]
                                             .rearrange("a p b c -> p (a b) c")).then_inc(mask_in[b], 16)

            def chunks(eng, before, first_step, second_step, after):
                with eng.Fori(0, NC) as ch:
                    before(ch)

                    def steps(i, first):
                        for u in range(4):
                            n = (ch * NP + i) * 4 + u
                            first_step(n, i * 4 + u, u)
                            if not (first and u == 0):
                                second_step(n - 1, (u - 1) % 4)
                    steps(0, True)
                    with eng.Fori(1, NP) as i:
                        steps(i, False)
                    second_step((ch + 1) * T - 1, 3)
                    after(ch)

            @blk.scalar
            def _(act):
                act.sem_inc(acc_copied, CT)
                act.sem_inc(st_out, 16)
                act.sem_inc(prob_ready, 2)
                act.wait_ge(loaded, 32)

                def lower(n, j, u):
                    act.wait_ge(arg_ready, n + 1)
                    nc.scalar.activation(low[:, u % 2], s12[:, 1], ACT.Identity,
                                         bias=sc[:, 2, bass.ds(j, 1)]).then_inc(low_ready, 1)

                def exps(n, u):
                    act.wait_ge(arg_ready, n + 3)
                    act.wait_ge(w_ready, n + 1)
                    nc.scalar.activation(prob[:, u % 2], arg[:, u % 2], ACT.Exp).then_inc(prob_ready, 1)

                def copy_out(ch):
                    act.wait_ge(st_out, ch * 16 + 16)
                    for t in range(CT):
                        act.wait_ge(acc_done, ch * CT + t + 1)
                        nc.scalar.copy(st[:, t], acc[:, t, :P + 1]).then_inc(acc_copied, 1)
                    act.wait_ge(acc_copied, (ch + 2) * CT)
                    act.dma_start(sums[bass.ds(ch * CT, CT), :, :P + 1].rearrange("t p c -> p t c"),
                                  st[:]).then_inc(st_out, 16)

                chunks(act, lambda ch: act.wait_ge(s_in, ch * 16 + 16), lower, exps, copy_out)
                act.wait_ge(st_out, 16 * NC + 16)

            @blk.vector
            def _(dve):
                dve.wait_ge(loaded, 32)
                nc.vector.memset(zero[:], 0.0)
                nc.vector.tensor_copy(rhs[:, :, :P], vals[:])
                nc.vector.tensor_copy(maskv[:], sc[:, 3].unsqueeze(2))
                nc.vector.memset(rhs[:, :, P:], 1.0).then_inc(rhs_ok, 1)
                dve.sem_inc(s_used, 1)
                dve.sem_inc(arg_ready, 2)
                dve.sem_inc(w_ready, 2)

                def larger(n, j, u):
                    dve.wait_ge(low_ready, n + 1)
                    dve.wait_ge(prob_ready, n + 1)
                    nc.vector.scalar_tensor_tensor(arg[:, u % 2], s12[:, 0],
                                                   sc[:, 1, bass.ds(j, 1)], low[:, u % 2],
                                                   ALU.add, ALU.max).then_inc(arg_ready, 1)

                def masked(n, u):
                    b, k = units[u]
                    dve.wait_ge(prob_ready, n + 3)
                    if u % 2 == 0:
                        dve.wait_ge(mask_in[b], (n - u + 4) * (4 * CT))
                    dve.wait_ge(k_used, n + 1)
                    out_, ready = (wts, w_ready)
                    nc.vector.scalar_tensor_tensor(out_[:, u % 2].rearrange("p (t c) -> p t c", c=P),
                                                   prob[:, u % 2].rearrange("p (t c) -> p t c", c=P), 2.0,
                                                   mask[:, b, :, k], ALU.min, ALU.mult).then_inc(w_ready, 1)
                    if threshold is not None:
                        dve.wait_ge(w_ready, n + 3)
                        nc.vector.scalar_tensor_tensor(kept[:, u % 2], wts[:, u % 2], threshold, wts[:, u % 2],
                                                       ALU.is_ge, ALU.mult).then_inc(k_ready, 1)

                def done(ch):
                    dve.sem_inc(s_used, 1)

                chunks(dve, lambda ch: dve.wait_ge(s_in, ch * 16 + 16), larger, masked, done)

            @blk.tensor
            def _(pe):
                pe.sem_inc(k_used, 2)
                for b in range(2):
                    pe.sem_inc(mask_used[b], 1)
                pe.wait_ge(rhs_ok, 1)
                src = wts if threshold is None else kept
                with pe.Fori(0, NC) as ch:
                    for t in range(CT):
                        pe.wait_ge(acc_copied, ch * CT + t + 1)
                        nc.tensor.matmul(acc[:, t, :P + 1], zero[:, :P], zero[:, :P + 1], start=True, stop=False)
                    with pe.Fori(0, NP) as i:
                        for u, (b, k) in enumerate(units):
                            n = (ch * NP + i) * 4 + u
                            if threshold is None:
                                pe.wait_ge(w_ready, n + 3)
                            else:
                                pe.wait_ge(k_ready, n + 1)
                            for t in range(CT):
                                if threshold is not None:
                                    nc.tensor.matmul(acc[:, t, P:P + 1], mask[:, b, t, k],
                                                     maskv[:, bass.ds(i * 4 + u, 1)].rearrange("p a c -> p (a c)"),
                                                     start=False, stop=False, skip_group_check=True)
                                last = nc.tensor.matmul(
                                    acc[:, t, :width], src[:, u % 2, t * P:(t + 1) * P],
                                    rhs[:, bass.ds(i * 4 + u, 1), :width].rearrange("p a c -> p (a c)"),
                                    start=False, stop=False, skip_group_check=True)
                            last.then_inc(k_used, 1)
                            if k == 1:
                                pe.wait_ge(k_used, n + 3)
                                pe.sem_inc(mask_used[b], 1)
                    for t in range(CT):
                        nc.tensor.matmul(acc[:, t, :P + 1], zero[:, :P], zero[:, :P + 1], start=False,
                                         stop=True).then_inc(acc_done, 1)

        phase(body)

    guard("g2", False)
    attend("t2", x_2, P + 1, None)

    def finish2(sb, ps, sem, block):
        ident = ident_of["h"] = sb("h_ident", [P, P], F32)
        X, tmp, stat = sb("h_X", [P, T, P], F32), sb("h_tmp", [P, T, P], F32), sb("h_stat", [P, 3, T], F32)
        U = sb("h_U", [P, T, P + 1], F32)
        W = sb("h_W", [P, P], F32)
        h = sb("h_h", [P, T, P], F32)
        at = sb("h_at", [P, 2, P], F32)
        sc = sb("h_sc", [P, 5, T], F32)
        loaded, dch, var_ok, std_ok, x_ok, x_st, sc_ok = (
            sem("h_" + n) for n in ("loaded", "dch", "var_ok", "std_ok", "x_ok", "x_st", "sc_ok"))
        rt, ra, rs = write_rows(lambda n: sc[:, 1], ident, sb, ps, sem, "h", 1)
        tensor, scalar, vector = project(None, sem, ps, sb, "h", lambda t: X[:, t], W, P, h, (loaded, 80), (x_ok, 1))
        blk = block()

        @blk.sync
        def _(sp):
            sp.dma_start(U[:], sums[:, :, :P + 1].rearrange("t p c -> p t c")).then_inc(loaded, 16)
            sp.dma_start(ident[:], c_ident).then_inc(loaded, 16)
            sp.dma_start(X[:], x_2).then_inc(loaded, 16)
            sp.dma_start(W[:], W3).then_inc(loaded, 16)
            sp.dma_start(at[:], a3.rearrange("(k c) a -> a k c", k=2).partition_broadcast(P)
                         .rearrange("q a k c -> q (a k) c")).then_inc(loaded, 16)
            sp.wait_ge(x_ok, 1)
            sp.dma_start(x_3, X[:]).then_inc(x_st, 16)
            sp.wait_ge(sc_ok, 1)
            sp.dma_start(cols[:, :4], sc[:, :4]).then_inc(x_st, 16)
            sp.dma_start(h_3, h[:]).then_inc(x_st, 16)
            rs(sp, 4)
            sp.wait_ge(x_st, 48)

        @blk.scalar
        def _(act):
            root(act, stat, var_ok, std_ok)
            scalar(act)
            ra(act)

        @blk.tensor
        def _(pe):
            tensor(pe)
            pe.wait_ge(sc_ok, 1)
            rt(pe)

        @blk.vector
        def _(dve):
            link = chain(dve, dch)
            dve.wait_ge(loaded, 80)
            link(nc.vector.reciprocal(stat[:, 0], U[:, :, P]))
            link(nc.vector.tensor_tensor(tmp[:], U[:, :, :P], stat[:, 0].unsqueeze(2).broadcast_to([P, T, P]),
                                         ALU.mult))
            link(nc.vector.tensor_tensor(X[:], X[:], tmp[:], ALU.add))
            normalise(dve, link, X, tmp, stat, var_ok, std_ok)
            dve.sem_inc(x_ok, 1)
            vector(dve)
            for k in range(2):
                link(nc.vector.tensor_tensor(tmp[:], h[:], at[:, k].unsqueeze(1).broadcast_to([P, T, P]), ALU.mult))
                link(nc.vector.tensor_reduce(sc[:, k], tmp[:], AX.X, ALU.add))
            link(nc.vector.tensor_reduce(stat[:, 0], h[:], AX.X, ALU.add))
            link(nc.vector.tensor_scalar(sc[:, 3], stat[:, 0], 0.0, None, ALU.not_equal))
            link(nc.vector.tensor_scalar(stat[:, 1], sc[:, 3], 1.0, -NEG, ALU.subtract, ALU.mult))
            link(nc.vector.tensor_tensor(sc[:, 1], sc[:, 1], stat[:, 1], ALU.add))
            link(nc.vector.tensor_scalar(sc[:, 2], sc[:, 1], SLOPE, None, ALU.mult))
            dve.sem_inc(sc_ok, 1)

    phase(finish2)
    guard("g3", True)
    attend("t3", h_3, P, THR)

    def finish3(sb, ps, sem, block):
        X, tmp, stat = sb("X", [P, T, P], F32), sb("tmp", [P, T, P], F32), sb("stat", [P, 3, T], F32)
        U = sb("U", [P, T, P + 1], F32)
        h = sb("h", [P, T, P], F32)
        sc = sb("sc", [P, 5, T], F32)
        loaded, dch, var_ok, std_ok, x_ok, x_st, low_ok, exp_ok = (
            sem(n) for n in ("loaded", "dch", "var_ok", "std_ok", "x_ok", "x_st", "low_ok", "exp_ok"))
        blk = block()

        @blk.sync
        def _(sp):
            sp.dma_start(U[:], sums[:, :, :P + 1].rearrange("t p c -> p t c")).then_inc(loaded, 16)
            sp.dma_start(X[:], x_3).then_inc(loaded, 16)
            sp.dma_start(h[:], h_3).then_inc(loaded, 16)
            sp.dma_start(sc[:, :5], cols[:, :5]).then_inc(loaded, 16)
            sp.wait_ge(x_ok, 1)
            sp.dma_start(tiles(out), X[:]).then_inc(x_st, 16)
            sp.wait_ge(x_st, 16)

        @blk.scalar
        def _(act):
            act.wait_ge(low_ok, 1)
            nc.scalar.activation(tmp[:], tmp[:], ACT.Exp).then_inc(exp_ok, 1)
            root(act, stat, var_ok, std_ok)

        @blk.vector
        def _(dve):
            link = chain(dve, dch)
            dve.wait_ge(loaded, 64)
            link(nc.vector.scalar_tensor_tensor(stat[:, 0], sc[:, 4], THR, U[:, :, P], ALU.is_gt, ALU.mult))
            link(nc.vector.tensor_tensor(U[:, :, :P], U[:, :, :P], stat[:, 0].unsqueeze(2).broadcast_to([P, T, P]),
                                         ALU.mult))
            link(nc.vector.tensor_tensor(h[:], h[:], U[:, :, :P], ALU.add))
            link(nc.vector.tensor_scalar(tmp[:], h[:], 0.0, None, ALU.min))
            dve.sem_inc(low_ok, 1)
            link(nc.vector.tensor_scalar(h[:], h[:], 0.0, -1.0, ALU.max, ALU.add))
            link(nc.vector.tensor_tensor(X[:], X[:], h[:], ALU.add))
            dve.wait_ge(exp_ok, 1)
            link(nc.vector.tensor_tensor(X[:], X[:], tmp[:], ALU.add))
            normalise(dve, link, X, tmp, stat, var_ok, std_ok)
            dve.sem_inc(x_ok, 1)

    phase(finish3)


_INS = ["x", "adj", "L0_gnn_W", "L0_gnn_attn_src", "L0_gnn_attn_dst", "L2_gnn_attn", "L3_gnn_W", "L3_gnn_a"]


def kernel(**inputs):
    import concourse.bacc as bacc
    from concourse.bass_utils import run_bass_kernel_spmd

    nc = bacc.Bacc("TRN2", target_bir_lowering=False, num_devices=1)
    arrays, args = {}, []
    for name, a in [(n, inputs[n]) for n in _INS] + sorted(constants().items()):
        a = np.ascontiguousarray(a)
        arrays[f"in_{name}"] = a
        args.append(nc.dram_tensor(f"in_{name}", a.shape, mybir.dt.from_np(a.dtype), kind="ExternalInput").ap())
    n = inputs["x"].shape[0]
    out = nc.dram_tensor("out", (n, P), F32, kind="ExternalOutput").ap()
    by_name = dict(zip(_INS + sorted(constants()), args))
    build(nc, *(by_name[k] for k in _INS), by_name["c_half"], by_name["c_ident"],
          by_name["c_prefix"], by_name["c_slot"], out)
    r = run_bass_kernel_spmd(nc, [arrays], core_ids=[0])
    return r.results[0]["out"]
```

```python
from contextlib import ExitStack

import concourse.bass as bass
import numpy as np
from concourse import mybir

F32 = mybir.dt.float32
BF16 = mybir.dt.bfloat16
I32 = mybir.dt.int32
ALU = mybir.AluOpType
ACT = mybir.ActivationFunctionType
AX = mybir.AxisListType
RMAX = bass.bass_isa.ReduceOp.max

P = 128
HEADS = 4
HD = P // HEADS
HW = HD + 1
SUB = 512
CT = 8
CW = CT * P
SLOPE = 0.2
EPS = 1e-5
THR = 1e-4
NEG = -(2.0 ** 100)


def constants():
    ident = np.eye(P, dtype=np.float32)
    prefix = np.triu(np.ones((P, P), np.float32), 1) + 0.5 * ident
    prefix[:, P - 1] = 1.0
    prefix[P - 1] = 0.0
    half = np.zeros((P, 1), np.float32)
    half[P - 1] = 0.5
    turn = np.arange(P + 1, dtype=np.float32) + 0.5
    slot = np.stack([np.full((P, P + 1), -1.0, np.float32), np.tile(turn, (P, 1))], 1)
    slot[P - 1, 0] = turn
    return {"c_half": half, "c_ident": ident, "c_prefix": prefix, "c_slot": slot.reshape(P, -1)}


def build(nc, x, adj, W0, src0, dst0, attn2, W3, a3, c_half, c_ident, c_prefix, c_slot, out):
    N = x.shape[0]
    T = N // P
    NC = N // CW
    NBLK = T + 2
    HB = T // 2
    GB = 8 if HB % 8 == 0 else 4
    NG = HB // GB
    U0W = 3 * HEADS * HW

    scratch = {}

    def dram(name, shape, dt):
        scratch[name] = nc.dram_tensor(name, shape, dt)
        return scratch[name].ap()

    maskT = dram("maskT", [T, P, T, P], BF16)
    negn = dram("negn", [T, P, N], BF16)
    x_1 = dram("x_1", [P, T, P], F32)
    x_2 = dram("x_2", [P, T, P], F32)
    x_3 = dram("x_3", [P, T, P], F32)
    sums = dram("sums", [T, P, U0W], F32)
    ab0 = dram("ab0", [P, 2, T, HEADS], F32)
    rhs0 = dram("rhs0", [P, T, 3, 2 * HEADS * HW], BF16)
    rows = dram("rows", [8, N], F32)
    parts_d = dram("parts_d", [P, 3, NBLK, P], BF16)
    first_d = dram("first_d", [2, NBLK + 1], I32)
    best_d = dram("best_d", [P, N], F32)
    h_3 = dram("h_3", [P, T, P], F32)
    d0_cols = dram("d0_cols", [P, T, HEADS], F32)
    cols = dram("cols", [P, 5, T], F32)

    def tiles(a):
        return a.rearrange("(t p) c -> p t c", p=P)

    phases = [0]

    def phase(body):
        phases[0] += 1
        tag = f"p{phases[0]}_"
        sems = []

        def sem(name):
            sems.append(nc.alloc_semaphore(tag + name))
            return sems[-1]

        with ExitStack() as ctx:
            body(
                lambda name, shape, dt: ctx.enter_context(nc.sbuf_tensor(tag + name, shape, dt)),
                lambda name, shape, dt: ctx.enter_context(nc.psum_tensor(tag + name, shape, dt)),
                sem,
                lambda: ctx.enter_context(nc.Block()),
            )
        nc.clear_and_free_semaphores(sems)
        nc.all_engine_barrier()

    def chain(eng, sem):
        n = [0]

        def link(ins):
            n[0] += 1
            ins.then_inc(sem, 1)
            eng.wait_ge(sem, n[0])

        return link

    def adjacency(sb, ps, sem, block):
        ident = sb("a_ident", [P, P], F32)
        identb = sb("a_identb", [P, P], BF16)
        raw = sb("a_raw", [P, 2, N // 2], I32)
        mask = sb("a_mask", [P, 2, N // 2], BF16)
        neg = sb("a_neg", [P, 2, N // 2], BF16)
        maskt = sb("a_maskt", [P, 2, HB, P], BF16)
        bank = ps("a_bank", [P, 2, NG, 2 * SUB], BF16)
        full = sb("a_full", [P, NBLK], F32)
        here = sb("a_here", [P, T + 2], F32)
        zeros = sb("a_zeros", [P, NBLK], F32)
        first = sb("a_first", [P, NBLK + 1], F32)
        firsti = sb("a_firsti", [P, 2, NBLK + 1], I32)
        tally, dch, full_ok, all_ok, first_ok, first_st = (
            sem("a_" + n) for n in ("tally", "dch", "full_ok", "all_ok", "first_ok", "first_st"))
        ident_in, ident_ok = sem("a_ident_in"), sem("a_ident_ok")
        raw_in = [sem("a_raw_in0"), sem("a_raw_in1")]
        cast_done = [sem("a_cast0"), sem("a_cast1")]
        neg_done = [sem("a_neg0"), sem("a_neg1")]
        neg_stored = [sem("a_nst0"), sem("a_nst1")]
        transposed = [sem("a_tr0"), sem("a_tr1")]
        copied = [sem("a_cp0"), sem("a_cp1")]
        mask_stored = [sem("a_mst0"), sem("a_mst1")]
        blk = block()
        adj_t = adj.rearrange("(t p) n -> t p n", p=P)

        @blk.sync
        def _(sp):
            sp.dma_start(ident[:], c_ident).then_inc(ident_in, 16)
            for hf in range(2):
                sp.dma_start(raw[:, hf], adj_t[0, :, hf * (N // 2):(hf + 1) * (N // 2)]).then_inc(raw_in[hf], 16)

            def load(t):
                for hf in range(2):
                    sp.wait_ge(cast_done[hf], t)
                    sp.wait_ge(neg_done[hf], t)
                    sp.dma_start(raw[:, hf], adj_t[bass.ds(t, 1), :, hf * (N // 2):(hf + 1) * (N // 2)]
                                 .rearrange("a p n -> p (a n)")).then_inc(raw_in[hf], 16)

            def store(t):
                for hf in range(2):
                    sp.wait_ge(neg_done[hf], t + 1)
                    sp.dma_start(negn[bass.ds(t, 1), :, hf * (N // 2):(hf + 1) * (N // 2)]
                                 .rearrange("a p n -> p (a n)"), neg[:, hf]).then_inc(neg_stored[hf], 16)
                for hf in range(2):
                    sp.wait_ge(copied[hf], t * NG + NG)
                    sp.dma_start(maskT[bass.ds(t, 1), :, hf * HB:(hf + 1) * HB, :]
                                 .rearrange("a p b c -> p (a b c)"),
                                 maskt[:, hf].rearrange("p b c -> p (b c)")).then_inc(mask_stored[hf], 16)

            with sp.Fori(1, T) as t:
                load(t)
                store(t - 1)
            store(T - 1)
            sp.wait_ge(first_ok, 1)
            sp.dma_start(first_d.rearrange("(a k) n -> a k n", a=1), firsti[0:1]).then_inc(first_st, 16)
            sp.wait_ge(first_st, 16)
            for hf in range(2):
                sp.wait_ge(neg_stored[hf], 16 * T)
                sp.wait_ge(mask_stored[hf], 16 * T)

        @blk.gpsimd
        def _(pool):
            pool.wait_ge(full_ok, 1)
            nc.gpsimd.partition_all_reduce(first[:, 1:], full[:], P, RMAX).then_inc(all_ok, 1)

        @blk.vector
        def _(dve):
            dve.wait_ge(ident_in, 16)
            link = chain(dve, dch)
            nc.vector.tensor_copy(identb[:], ident[:]).then_inc(ident_ok, 1)
            nc.vector.memset(zeros[:], 0.0)
            link(nc.vector.memset(full[:], 0.0))
            for initial in (True, False):
                def step(t, first=initial):
                    for hf in range(2):
                        dve.wait_ge(raw_in[hf], t * 16 + 16)
                        if not first:
                            dve.wait_ge(transposed[hf], t * NG)
                        nc.vector.tensor_copy(mask[:, hf], raw[:, hf]).then_inc(cast_done[hf], 1)
                        dve.wait_ge(cast_done[hf], t + 1)
                        m = mask[:, hf].rearrange("p (b c) -> p b c", c=P)
                        nc.vector.tensor_reduce(here[:, hf * HB:(hf + 1) * HB], m[:, :, :P - 1], AX.X, ALU.add)
                        nc.vector.tensor_reduce(here[:, T + hf:T + hf + 1], m[:, :, P - 1], AX.X,
                                                ALU.add).then_inc(tally, 1)
                    dve.wait_ge(tally, t * 4 + 2)
                    nc.vector.tensor_tensor(here[:, T:T + 1], here[:, T:T + 1], here[:, T + 1:], ALU.add).then_inc(
                        tally, 1)
                    dve.wait_ge(tally, t * 4 + 3)
                    nc.vector.tensor_tensor(full[:, :T + 1], full[:, :T + 1], here[:, :T + 1],
                                            ALU.max).then_inc(tally, 1)
                    if not first:
                        dve.wait_ge(mask_stored[0], t * 16)
                    for g in range(NG):
                        dve.wait_ge(transposed[0], t * NG + g + 1)
                        nc.vector.tensor_copy(maskt[:, 0, g * GB:(g + 1) * GB],
                                              bank[:, 0, g, :GB * P].rearrange("p (b c) -> p b c", c=P)).then_inc(copied[0], 1)
                if initial:
                    step(0)
                else:
                    with dve.Fori(1, T) as t:
                        step(t)
            dve.wait_ge(tally, T * 4)
            link(nc.vector.tensor_scalar(full[:], full[:], 2.0, None, ALU.max))
            dve.sem_inc(full_ok, 1)
            dve.wait_ge(all_ok, 1)
            link(nc.vector.tensor_tensor_scan(full[:], first[:, 1:], zeros[:], 0.0, ALU.add, ALU.add))
            link(nc.vector.memset(firsti[:], 0))
            link(nc.vector.tensor_copy(firsti[:, 1, :NBLK], first[:, 1:]))
            link(nc.vector.tensor_copy(firsti[:, 0, 1:], full[:]))
            dve.sem_inc(first_ok, 1)

        @blk.scalar
        def _(act):
            for first in (True, False):
                def step(t, first=first):
                    for hf in range(2):
                        act.wait_ge(raw_in[hf], t * 16 + 16)
                        if not first:
                            act.wait_ge(neg_stored[hf], t * 16)
                        nc.scalar.activation(neg[:, hf], raw[:, hf], ACT.Copy, bias=NEG,
                                             scale=-NEG).then_inc(neg_done[hf], 1)
                    if not first:
                        act.wait_ge(mask_stored[1], t * 16)
                    for g in range(NG):
                        act.wait_ge(transposed[1], t * NG + g + 1)
                        nc.scalar.copy(maskt[:, 1, g * GB:(g + 1) * GB],
                                       bank[:, 1, g, :GB * P].rearrange("p (b c) -> p b c", c=P)).then_inc(copied[1], 1)
                if first:
                    step(0)
                else:
                    with act.Fori(1, T) as t:
                        step(t)

        @blk.tensor
        def _(pe):
            pe.wait_ge(ident_ok, 1)
            for first in (True, False):
                def step(t, first=first):
                    for hf in range(2):
                        pe.wait_ge(cast_done[hf], t + 1)
                        if not first:
                            pe.wait_ge(copied[hf], t * NG)
                        for g in range(NG):
                            for b in range(GB):
                                c = (g * GB + b) * P
                                last = nc.tensor.transpose(bank[:, hf, g, b * P:(b + 1) * P],
                                                           mask[:, hf, c:c + P], identb[:])
                            last.then_inc(transposed[hf], 1)
                if first:
                    step(0)
                else:
                    with pe.Fori(1, T) as t:
                        step(t)

    phase(adjacency)

    def project(blk, sem, ps, sb, tag, xt_src, weights, width, h, ready_x, ready_w):
        xT = sb(tag + "_xT", [P, 2, P], F32)
        pT = ps(tag + "_pT", [P, 2, SUB], F32)
        pH = ps(tag + "_pH", [P, 2, SUB], F32)
        xT_ready, pT_ready, pH_ready, h_ready = (sem(tag + n) for n in ("_xTr", "_pTr", "_pHr", "_hr"))

        def tensor(pe):
            for sem_, val in (ready_x, ready_w):
                pe.wait_ge(sem_, val)
            for i in range(T // 2):
                for b in range(2):
                    if i:
                        pe.wait_ge(xT_ready, i * 2 - 1 + b)
                    nc.tensor.transpose(pT[:, b, :P], xt_src(i * 2 + b), ident_of[tag][:]).then_inc(pT_ready, 1)
                for b in range(2):
                    pe.wait_ge(xT_ready, i * 2 + b + 1)
                    if i:
                        pe.wait_ge(h_ready, i * 2 - 1 + b)
                    nc.tensor.matmul(pH[:, b, :width], xT[:, b], weights[:, :width], start=True,
                                     stop=True).then_inc(pH_ready, 1)

        def scalar(act):
            for n in range(T):
                act.wait_ge(pT_ready, n + 1)
                if n >= 2:
                    act.wait_ge(pH_ready, n - 1)
                nc.scalar.copy(xT[:, n % 2], pT[:, n % 2, :P]).then_inc(xT_ready, 1)

        def vector(dve):
            with dve.Fori(0, T // 2) as i:
                for b in range(2):
                    dve.wait_ge(pH_ready, i * 2 + b + 1)
                    nc.vector.tensor_copy(h[:, bass.ds(i * 2 + b, 1)].rearrange("p a c -> p (a c)"),
                                          pH[:, b, :width]).then_inc(h_ready, 1)
            dve.wait_ge(h_ready, T)

        return tensor, scalar, vector

    ident_of = {}

    def operands0(sb, ps, sem, block):
        ident = ident_of["o"] = sb("o_ident", [P, P], F32)
        X = sb("o_X", [P, T, P], F32)
        Wn = sb("o_Wn", [P, P], F32)
        sd = sb("o_sd", [P, 2], F32)
        heads = sb("o_heads", [P, 2 * HEADS], F32)
        Wx = sb("o_Wx", [P, P + 2 * HEADS], F32)
        h = sb("o_h", [P, T, P + 2 * HEADS], F32)
        top = sb("o_top", [P, HEADS], F32)
        c = sb("o_c", [P, HEADS], F32)
        z = sb("o_z", [P, T, 2, HEADS], F32)
        e = sb("o_e", [P, 4, T, HEADS], F32)
        negs = sb("o_negs", [P, HEADS, T], F32)
        negsT = sb("o_negsT", [P, HEADS, P], F32)
        QT = T // 4 if T >= 32 else T // 2
        f = sb("o_f", [P, QT, HEADS, 2, HW], F32)
        g = sb("o_g", [P, QT, HEADS * 2 * HW], F32)
        r3 = sb("o_r3", [P, QT, 3, HEADS * 2 * HW], BF16)
        pW = ps("o_pW", [P, 2, SUB], F32)
        pS = ps("o_pS", [P, SUB], F32)
        loaded, w_ok, heads_ok, w_mm, top_ok, c_ok = (sem("o_" + n) for n in
                                                      ("loaded", "w_ok", "heads_ok", "w_mm", "top_ok", "c_ok"))
        dcol = sb("o_dcol", [P, T, HEADS], F32)
        dcol_ok = sem("o_dcol_ok")
        dch, z_ok, e_ok, negs_ok, negs_tr, negs_cp, rows_st, r_ok, r_st, e_st = (
            sem("o_" + n) for n in ("dch", "z_ok", "e_ok", "negs_ok", "negs_tr", "negs_cp", "rows_st",
                                    "r_ok", "r_st", "e_st"))
        blk = block()
        tensor, scalar, vector = project(blk, sem, ps, sb, "o", lambda t: X[:, t], Wx, P + 2 * HEADS, h, (loaded, 16 * 5), (w_ok, 1))
        TH = min(P, HEADS * T)
        NTR = HEADS * T // TH

        @blk.sync
        def _(sp):
            sp.dma_start(X[:], tiles(x)).then_inc(loaded, 16)
            sp.dma_start(ident[:], c_ident).then_inc(loaded, 16)
            sp.dma_start(Wn[:], W0).then_inc(loaded, 16)
            sp.dma_start(sd[:, 0:1], src0.rearrange("a h d -> (h d) a")).then_inc(loaded, 16)
            sp.dma_start(sd[:, 1:2], dst0.rearrange("a h d -> (h d) a")).then_inc(loaded, 16)
            for n in range(T // QT):
                sp.wait_ge(r_ok, n + 1)
                sp.dma_start(rhs0[:, n * QT:(n + 1) * QT], r3[:]).then_inc(r_st, 16)
            sp.wait_ge(dcol_ok, 1)
            sp.wait_ge(e_ok, 4)
            sp.dma_start(ab0, e[:, 0:2]).then_inc(e_st, 16)
            sp.dma_start(d0_cols, dcol[:]).then_inc(e_st, 16)
            sp.wait_ge(negs_cp, NTR)
            rr = rows[0:HEADS].rearrange("h (t p) -> (h t) p", p=P)
            for n in range(NTR):
                sp.dma_start(rr[n * TH:(n + 1) * TH], negsT[:TH, n]).then_inc(rows_st, 16)
            sp.wait_ge(rows_st, 16 * NTR)
            sp.wait_ge(e_st, 32)
            sp.wait_ge(r_st, 16 * (T // QT))

        @blk.gpsimd
        def _(pool):
            pool.wait_ge(top_ok, 1)
            nc.gpsimd.partition_all_reduce(c[:], top[:], P, RMAX).then_inc(c_ok, 1)

        @blk.scalar
        def _(act):
            scalar(act)
            act.wait_ge(z_ok, 1)
            nc.scalar.activation(e[:, 0], z[:, :, 0], ACT.Exp).then_inc(e_ok, 1)
            act.wait_ge(z_ok, 2)
            nc.scalar.activation(e[:, 1], z[:, :, 1], ACT.Exp).then_inc(e_ok, 1)
            act.wait_ge(z_ok, 3)
            nc.scalar.activation(e[:, 2], z[:, :, 0], ACT.Exp).then_inc(e_ok, 1)
            nc.scalar.activation(e[:, 3], z[:, :, 0], ACT.Exp, scale=SLOPE).then_inc(e_ok, 1)

        @blk.vector
        def _(dve):
            link = chain(dve, dch)
            link(nc.vector.memset(heads[:], 0.0))
            dve.wait_ge(loaded, 16 * 5)
            for k in range(2):
                for hd in range(HEADS):
                    q = slice(hd * HD, (hd + 1) * HD)
                    link(nc.vector.tensor_copy(heads[q, k * HEADS + hd:k * HEADS + hd + 1], sd[q, k:k + 1]))
            dve.sem_inc(heads_ok, 1)
            dve.wait_ge(w_mm, 1)
            link(nc.vector.tensor_copy(Wx[:, :P], pW[:, 0, :P]))
            nc.vector.tensor_copy(Wx[:, P:], pW[:, 1, :2 * HEADS]).then_inc(w_ok, 1)
            vector(dve)
            s, d = h[:, :, P:P + HEADS], h[:, :, P + HEADS:]
            nc.vector.tensor_reduce(top[:], d.rearrange("p t h -> p h t"), AX.X, ALU.max).then_inc(top_ok, 1)
            nc.vector.tensor_scalar(negs[:], s.rearrange("p t h -> p h t"), -1.0, None, ALU.mult).then_inc(negs_ok, 1)
            nc.vector.tensor_copy(dcol[:], d).then_inc(dcol_ok, 1)
            dve.wait_ge(c_ok, 1)
            cb = c[:].unsqueeze(1).broadcast_to([P, T, HEADS])
            link(nc.vector.tensor_tensor(z[:, :, 1], s, cb, ALU.add))
            nc.vector.tensor_scalar(z[:, :, 0], z[:, :, 1], 1 - SLOPE, 0.0, ALU.mult, ALU.min).then_inc(z_ok, 1)
            dve.wait_ge(z_ok, 1)
            nc.vector.tensor_scalar(z[:, :, 1], z[:, :, 1], SLOPE - 1, 0.0, ALU.mult, ALU.min).then_inc(z_ok, 1)
            dve.wait_ge(e_ok, 1)
            nc.vector.tensor_tensor(z[:, :, 0], d, cb, ALU.subtract).then_inc(z_ok, 1)
            for n in range(NTR):
                dve.wait_ge(negs_tr, NTR)
                nc.vector.tensor_copy(negsT[:TH, n], pS[:TH, n * P:(n + 1) * P]).then_inc(negs_cp, 1)
            dve.wait_ge(e_ok, 4)
            for n in range(T // QT):
                ts_ = slice(n * QT, (n + 1) * QT)
                for hd in range(HEADS):
                    for k in range(2):
                        w = e[:, 2 + k, ts_, hd:hd + 1]
                        link(nc.vector.tensor_tensor(f[:, :, hd, k, :HD], h[:, ts_, hd * HD:(hd + 1) * HD],
                                                     w.broadcast_to([P, QT, HD]), ALU.mult))
                        link(nc.vector.tensor_copy(f[:, :, hd, k, HD:], w))
                ff = f[:].rearrange("p t h k c -> p t (h k c)")
                if n:
                    dve.wait_ge(r_st, 16 * n)
                link(nc.vector.tensor_copy(r3[:, :, 0], ff))
                link(nc.vector.tensor_tensor(g[:], ff, r3[:, :, 0], ALU.subtract))
                link(nc.vector.tensor_copy(r3[:, :, 1], g[:]))
                link(nc.vector.tensor_tensor(r3[:, :, 2], g[:], r3[:, :, 1], ALU.subtract))
                dve.sem_inc(r_ok, 1)

        @blk.tensor
        def _(pe):
            pe.wait_ge(loaded, 16 * 5)
            pe.wait_ge(heads_ok, 1)
            nc.tensor.transpose(pW[:, 0, :P], Wn[:], ident[:])
            nc.tensor.matmul(pW[:, 1, :2 * HEADS], Wn[:], heads[:], start=True, stop=True).then_inc(w_mm, 1)
            tensor(pe)
            pe.wait_ge(negs_ok, 1)
            nf = negs[:].rearrange("p h t -> p (h t)")
            for n in range(NTR):
                nc.tensor.transpose(pS[:TH, n * P:(n + 1) * P], nf[:, n * TH:(n + 1) * TH],
                                    ident[:]).then_inc(negs_tr, 1)

    phase(operands0)

    def sums0(sb, ps, sem, block):
        W2 = 2 * HEADS * HW
        R = sb("s_R", [P, T, 3, HEADS, 2, HW], BF16)
        hd_cols = sb("s_d", [P, T, HEADS], F32)
        negs = sb("s_negs", [P, HEADS, CW], F32)
        mask = sb("s_mask", [P, 2, CT, 2, P], BF16)
        m1 = sb("s_m1", [P, 2, HEADS, CW], BF16)
        Rb = sb("s_Rb", [P, 2, 3, HEADS, 2, HW], BF16)
        rb_ready = sem("s_rb_ready")
        zero = sb("s_zero", [P, SUB], BF16)
        st = sb("s_st", [P, CT, U0W], F32)
        acc = ps("s_acc", [P, CT, SUB], F32)
        loaded, zero_ok, negs_in, chunk_cmp = (sem("s_" + n) for n in ("loaded", "zero_ok", "negs_in", "chunk_cmp"))
        mask_in = [sem("s_mi0"), sem("s_mi1")]
        mask_used = [sem("s_mu0"), sem("s_mu1")]
        m1_ready, m1_used, acc_done, acc_copied, st_out = (sem("s_" + n) for n in
                                                          ("m1r", "m1u", "accd", "accc", "sto"))
        blk = block()
        NP = T // 4

        @blk.sync
        def _(sp):
            sp.dma_start(R[:], rhs0.rearrange("p t k (h u c) -> p t k h u c", h=HEADS, u=2)).then_inc(loaded, 16)
            sp.dma_start(hd_cols[:], d0_cols).then_inc(loaded, 16)
            with sp.Fori(0, NC) as ch:
                sp.wait_ge(chunk_cmp, ch + 1)
                sp.dma_start(negs[:], rows[0:HEADS, bass.ds(ch * CW, CW)].partition_broadcast(P)).then_inc(negs_in, 16)
                with sp.Fori(0, NP) as i:
                    for b in range(2):
                        sp.wait_ge(mask_used[b], ch * NP + i + 1)
                        sp.dma_start(mask[:, b].rearrange("p t k c -> p t (k c)"),
                                     maskT[bass.ds(ch * CT, CT), :, bass.ds(i * 4 + b * 2, 2), :]
                                     .rearrange("t p b c -> p t (b c)")).then_inc(mask_in[b], 16)

        @blk.vector
        def _(dve):
            nc.vector.memset(zero[:], 0.0).then_inc(zero_ok, 1)
            dve.sem_inc(chunk_cmp, 1)
            dve.wait_ge(loaded, 32)
            with dve.Fori(0, NC) as ch:
                with dve.Fori(0, NP) as i:
                    dve.wait_ge(negs_in, ch * 16 + 16)
                    for b in range(2):
                        dve.wait_ge(mask_in[b], (ch * NP + i + 1) * 16)
                        for k in range(2):
                            dve.wait_ge(m1_used, (ch * NP + i) * 4 + b * 2 + k + 1)
                            for hd in range(HEADS):
                                last = nc.vector.scalar_tensor_tensor(
                                    m1[:, k, hd].rearrange("p (t c) -> p t c", c=P),
                                    negs[:, hd].rearrange("p (t c) -> p t c", c=P),
                                    hd_cols[:, bass.ds(i * 4 + b * 2 + k, 1), hd:hd + 1].rearrange("p a c -> p (a c)"),
                                    mask[:, b, :, k], ALU.is_lt, ALU.mult)
                            last.then_inc(m1_ready, 1)
                dve.wait_ge(m1_ready, (ch + 1) * T)
                dve.sem_inc(chunk_cmp, 1)

        @blk.tensor
        def _(pe):
            pe.sem_inc(m1_used, 2)
            for b in range(2):
                pe.sem_inc(mask_used[b], 1)
            pe.wait_ge(zero_ok, 1)
            pe.wait_ge(loaded, 32)
            with pe.Fori(0, NC) as ch:
                for t in range(CT):
                    pe.wait_ge(acc_copied, ch * CT + t + 1)
                    nc.tensor.matmul(acc[:, t, :U0W], zero[:, :P], zero[:, :U0W], start=True, stop=False)
                with pe.Fori(0, NP) as i:
                    for b in range(2):
                        for k in range(2):
                            pe.wait_ge(m1_ready, (ch * NP + i) * 4 + b * 2 + k + 1)
                            pe.wait_ge(rb_ready, (ch * NP + i) * 4 + b * 2 + k + 1)
                            for t in range(CT):
                                for part in range(3):
                                    nc.tensor.matmul(
                                        acc[:, t, W2:U0W].rearrange("p (h c) -> p h c", c=HW), mask[:, b, t, k],
                                        Rb[:, k, part, :, 1],
                                        start=False, stop=False, skip_group_check=True)
                                for hd in range(HEADS):
                                    for part in range(3):
                                        last = nc.tensor.matmul(
                                            acc[:, t, hd * 2 * HW:(hd + 1) * 2 * HW],
                                            m1[:, k, hd, t * P:(t + 1) * P],
                                            Rb[:, k, part, hd].rearrange("p u c -> p (u c)"),
                                            start=False, stop=False, skip_group_check=True)
                            last.then_inc(m1_used, 1)
                        pe.wait_ge(m1_used, (ch * NP + i) * 4 + b * 2 + 4)
                        pe.sem_inc(mask_used[b], 1)
                for t in range(CT):
                    nc.tensor.matmul(acc[:, t, :U0W], zero[:, :P], zero[:, :U0W], start=False,
                                     stop=True).then_inc(acc_done, 1)

        @blk.scalar
        def _(act):
            act.sem_inc(acc_copied, CT)
            act.sem_inc(st_out, 16)
            with act.Fori(0, NC) as ch:
                with act.Fori(0, T // 2) as i:
                    for k in range(2):
                        act.wait_ge(loaded, 32)
                        act.wait_ge(m1_used, ch * T + i * 2 + k + 1)
                        nc.scalar.copy(Rb[:, k].rearrange("p q h u c -> p (q h u c)"),
                                       R[:, bass.ds(i * 2 + k, 1)].rearrange("p a q h u c -> p (a q h u c)")
                                       ).then_inc(rb_ready, 1)
                act.wait_ge(st_out, ch * 16 + 16)
                for t in range(CT):
                    act.wait_ge(acc_done, ch * CT + t + 1)
                    nc.scalar.copy(st[:, t], acc[:, t, :U0W]).then_inc(acc_copied, 1)
                act.wait_ge(acc_copied, (ch + 2) * CT)
                act.dma_start(sums[bass.ds(ch * CT, CT)].rearrange("t p c -> p t c"), st[:]).then_inc(st_out, 16)
            act.wait_ge(st_out, 16 * NC + 16)

    phase(sums0)

    def normalise(dve, link, X, tmp, stat, var_ok, std_ok):
        wide = lambda a: a.unsqueeze(2).broadcast_to([P, T, P])
        link(nc.vector.tensor_reduce(stat[:, 0], X[:], AX.X, ALU.add))
        link(nc.vector.tensor_scalar(stat[:, 0], stat[:, 0], 1.0 / P, None, ALU.mult))
        link(nc.vector.tensor_tensor(X[:], X[:], wide(stat[:, 0]), ALU.subtract))
        link(nc.vector.tensor_tensor(tmp[:], X[:], X[:], ALU.mult))
        link(nc.vector.tensor_reduce(stat[:, 1], tmp[:], AX.X, ALU.add))
        nc.vector.tensor_scalar(stat[:, 1], stat[:, 1], 1.0 / P, EPS, ALU.mult, ALU.add).then_inc(var_ok, 1)
        dve.wait_ge(std_ok, 1)
        link(nc.vector.reciprocal(stat[:, 0], stat[:, 2]))
        link(nc.vector.tensor_tensor(X[:], X[:], wide(stat[:, 0]), ALU.mult))

    def root(act, stat, var_ok, std_ok):
        act.wait_ge(var_ok, 1)
        nc.scalar.activation(stat[:, 2], stat[:, 1], ACT.Sqrt).then_inc(std_ok, 1)

    def finish0(sb, ps, sem, block):
        X, tmp, stat = sb("f_X", [P, T, P], F32), sb("f_tmp", [P, T, P], F32), sb("f_stat", [P, 3, T], F32)
        U = sb("f_U", [P, T, U0W], F32)
        ab = sb("f_ab", [P, 2, T, HEADS], F32)
        loaded, dch, var_ok, std_ok, x_ok, x_st = (sem("f_" + n) for n in
                                                   ("loaded", "dch", "var_ok", "std_ok", "x_ok", "x_st"))
        blk = block()

        @blk.sync
        def _(sp):
            sp.dma_start(U[:], sums[:, :, :U0W].rearrange("t p c -> p t c")).then_inc(loaded, 16)
            sp.dma_start(ab[:], ab0).then_inc(loaded, 16)
            sp.dma_start(X[:], tiles(x)).then_inc(loaded, 16)
            sp.wait_ge(x_ok, 1)
            sp.dma_start(x_1, X[:]).then_inc(x_st, 16)
            sp.wait_ge(x_st, 16)

        @blk.scalar
        def _(act):
            root(act, stat, var_ok, std_ok)

        @blk.vector
        def _(dve):
            link = chain(dve, dch)
            dve.wait_ge(loaded, 48)
            for hd in range(HEADS):
                u = U[:, :, hd * 2 * HW:hd * 2 * HW + HW]
                v = U[:, :, hd * 2 * HW + HW:(hd + 1) * 2 * HW]
                w = U[:, :, 2 * HEADS * HW + hd * HW:2 * HEADS * HW + (hd + 1) * HW]
                link(nc.vector.tensor_tensor(w, w, v, ALU.subtract))
                link(nc.vector.tensor_tensor(w, w, ab[:, 1, :, hd:hd + 1].broadcast_to([P, T, HW]), ALU.mult))
                link(nc.vector.tensor_tensor(u, u, ab[:, 0, :, hd:hd + 1].broadcast_to([P, T, HW]), ALU.mult))
                link(nc.vector.tensor_tensor(u, u, w, ALU.add))
                link(nc.vector.reciprocal(w[:, :, HD:], u[:, :, HD:]))
                link(nc.vector.tensor_tensor(u[:, :, :HD], u[:, :, :HD], w[:, :, HD:].broadcast_to([P, T, HD]),
                                             ALU.mult))
                xs = X[:, :, hd * HD:(hd + 1) * HD]
                link(nc.vector.tensor_tensor(xs, xs, u[:, :, :HD], ALU.add))
            normalise(dve, link, X, tmp, stat, var_ok, std_ok)
            dve.sem_inc(x_ok, 1)

    phase(finish0)

    def parts1(sb, ps, sem, block):
        xe = sb("xe", [P, NBLK, P], F32)
        none = sb("none", [1, NBLK * P], F32)
        parts = sb("parts", [P, 3, NBLK, P], BF16)
        zeroed, loaded, dch, parts_ok, stored = (sem(n) for n in ("zeroed", "loaded", "dch", "parts_ok", "stored"))
        blk = block()

        @blk.sync
        def _(sp):
            sp.wait_ge(zeroed, 2)
            sp.dma_start(xe[:P - 1, :T], x_1[:P - 1]).then_inc(loaded, 16)
            sp.dma_start(xe[:T, T], x_1[P - 1]).then_inc(loaded, 16)
            sp.dma_start(xe[P - 1:], none[:]).then_inc(loaded, 16)
            sp.wait_ge(parts_ok, 1)
            sp.dma_start(parts_d, parts[:]).then_inc(stored, 16)
            sp.wait_ge(stored, 16)

        @blk.vector
        def _(dve):
            link = chain(dve, dch)
            nc.vector.memset(none[:], NEG).then_inc(zeroed, 1)
            nc.vector.memset(xe[:], 0.0).then_inc(zeroed, 1)
            dve.wait_ge(loaded, 48)
            link(nc.vector.tensor_copy(parts[:, 0], xe[:]))
            link(nc.vector.tensor_tensor(xe[:], xe[:], parts[:, 0], ALU.subtract))
            link(nc.vector.tensor_copy(parts[:, 1], xe[:]))
            link(nc.vector.tensor_tensor(parts[:, 2], xe[:], parts[:, 1], ALU.subtract))
            dve.sem_inc(parts_ok, 1)

    phase(parts1)

    def maxima1(sb, ps, sem, block):
        NSUB = N // SUB
        wide, more = divmod(NSUB, 6)
        width = [wide + (u // 2 < more // 2) for u in range(6)]
        start_ = [sum(width[:u]) for u in range(6)]
        MAXW = width[0]
        assert more % 2 == 0 and wide > 0 and NSUB % 2 == 0
        prew = sb("prew", [P, P], F32)
        pre = sb("pre", [P, P], BF16)
        half = sb("half", [P, 1], F32)
        slot = sb("slot", [P, 2, P + 1], F32)
        first = sb("first", [1, 2, NBLK + 1], I32)
        best = sb("best", [P, N], F32)
        mask = sb("mask", [P, 2, T, P], BF16)
        nothing = sb("nothing", [P, T, P], BF16)
        order = sb("order", [P, 2, N], BF16)
        parts = sb("parts", [P, 3, NBLK, P], BF16)
        hot = sb("hot", [P, N], BF16)
        count = ps("count", [P, 2, SUB], F32)
        rowv = ps("rowv", [P, 2, MAXW, SUB], F32)
        (loaded, pre_ok, best_ok, zero_ok, count_ready, order_ready, block_done, row_ready, row_used,
         best_st) = (sem(n) for n in ("loaded", "pre_ok", "best_ok", "zero_ok", "count_ready", "order_ready",
                                      "block_done", "row_ready", "row_used", "best_st"))
        best_done = sem("best_done")
        hot_ready = [sem(f"hot_ready{g}") for g in range(3)]
        mask_in = [sem("mask_in0"), sem("mask_in1")]
        blk = block()

        @blk.sync
        def _(sp):
            sp.dma_start(prew[:], c_prefix).then_inc(loaded, 16)
            sp.dma_start(half[:], c_half).then_inc(loaded, 16)
            sp.dma_start(slot[:].rearrange("p k n -> p (k n)"), c_slot).then_inc(loaded, 16)
            sp.dma_start(first[:], first_d.rearrange("(a k) n -> a k n", a=1)).then_inc(loaded, 16)
            sp.dma_start(parts[:], parts_d).then_inc(loaded, 16)
            for b in range(2):
                sp.dma_start(mask[:, b], maskT[:, :, b, :].rearrange("t p c -> p t c")).then_inc(mask_in[b], 16)
                sp.sem_inc(mask_in[b], 16)
            with sp.Fori(1, T // 2) as i:
                for b in range(2):
                    sp.wait_ge(count_ready, (i * 2 + b - 1) * NSUB)
                    sp.dma_start(mask[:, b], maskT[:, :, bass.ds(i * 2 + b, 1), :]
                                 .rearrange("t p a c -> p t (a c)")).then_inc(mask_in[b], 32)
            sp.wait_ge(zero_ok, 1)
            sp.wait_ge(count_ready, (T - 1) * NSUB)
            sp.dma_start(mask[:T, 0], maskT[:, P - 1].rearrange("t b c -> b t c")).then_inc(mask_in[0], 16)
            sp.dma_start(mask[T:, 0], nothing[T:]).then_inc(mask_in[0], 16)
            sp.wait_ge(count_ready, T * NSUB)
            sp.dma_start(mask[:, 1], nothing[:]).then_inc(mask_in[1], 32)
            sp.wait_ge(count_ready, (T + 1) * NSUB)
            sp.dma_start(mask[:, 0], nothing[:]).then_inc(mask_in[0], 32)
            sp.wait_ge(best_done, 1)
            sp.dma_start(best_d, best[:]).then_inc(best_st, 16)
            sp.wait_ge(best_st, 16)

        @blk.tensor
        def _(pe):
            def counts(b, k, some):
                for c in some:
                    pe.wait_ge(order_ready, b * NSUB + c + 1)
                    nc.tensor.matmul(count[:, c % 2].rearrange("p (t c) -> p t c", c=P), pre[:],
                                     mask[:, k, c * 4:(c + 1) * 4], start=True, stop=True).then_inc(count_ready, 1)

            def products(n, b, u):
                if u % 2 == 0:
                    pe.wait_ge(hot_ready[u // 2], n + 1)
                pe.wait_ge(row_used, n * 6 + u + 2)
                for part in range(3):
                    for w in range(width[u]):
                        c = (start_[u] + w) * SUB
                        last = nc.tensor.matmul(
                            rowv[:, u % 2, w], parts[:, part, bass.ds(b, 1)].rearrange("p a c -> p (a c)"),
                            hot[:, c:c + SUB], start=part == 0, stop=part == 2)
                last.then_inc(row_ready, 1)

            pe.sem_inc(row_ready, 1)
            pe.wait_ge(pre_ok, 1)
            pe.wait_ge(mask_in[0], 32)
            counts(0, 0, range(NSUB))
            with pe.Fori(0, NBLK // 2) as i:
                for k in range(2):
                    b = i * 2 + k
                    lo = pe.value_load(first[0:1, 0, bass.ds(b, 1)], min_val=0, max_val=NBLK * P)
                    hi = pe.value_load(first[0:1, 0, bass.ds(b + 1, 1)], min_val=2, max_val=NBLK * P)
                    for u in range(6):
                        products(lo, b, u)
                        if u == 0:
                            pe.wait_ge(mask_in[1 - k], (i + 1 + k) * 32)
                        counts(b + 1, 1 - k, range(start_[u], start_[u] + width[u]))
                    with pe.Fori(lo + 1, hi) as n:
                        for u in range(6):
                            products(n, b, u)

        @blk.scalar
        def _(act):
            def orders(b, k):
                for c in range(NSUB):
                    act.wait_ge(count_ready, b * NSUB + c + 1)
                    nc.scalar.activation(order[:, k, c * SUB:(c + 1) * SUB], count[:, c % 2], ACT.Identity,
                                         bias=half[:]).then_inc(order_ready, 1)

            act.sem_inc(order_ready, 2)
            act.wait_ge(loaded, 80)
            orders(0, 0)
            with act.Fori(0, NBLK // 2) as i:
                for k in range(2):
                    act.wait_ge(block_done, i * 2 + k + 1)
                    orders(i * 2 + k + 1, 1 - k)

        @blk.vector
        def _(dve):
            dve.wait_ge(loaded, 80)
            nc.vector.memset(nothing[:], 0.0).then_inc(zero_ok, 1)
            nc.vector.tensor_copy(pre[:], prew[:]).then_inc(pre_ok, 1)
            nc.vector.memset(best[:], NEG).then_inc(best_ok, 1)
            dve.wait_ge(best_ok, 1)
            dve.sem_inc(row_used, 3)
            dve.sem_inc(block_done, 1)

            def pick(g, k, turn):
                c = slice(start_[2 * g] * SUB, (start_[2 * g + 1] + width[2 * g + 1]) * SUB)
                nc.vector.tensor_scalar(hot[:, c], order[:, k, c], slot[:, 0, bass.ds(turn, 1)],
                                        slot[:, 1, bass.ds(turn, 1)], ALU.max,
                                        ALU.is_equal).then_inc(hot_ready[g], 1)

            def take(unit, u):
                dve.wait_ge(row_ready, unit)
                dve.wait_ge(row_used, unit)
                c = slice(start_[u] * SUB, (start_[u] + width[u]) * SUB)
                cols_ = best[:, c].rearrange("p (s c) -> p s c", c=SUB)
                nc.vector.tensor_tensor(cols_, rowv[:, u % 2, :width[u]], cols_, ALU.max).then_inc(row_used, 1)

            def most(n, k, turn):
                pick(1, k, turn)
                take(n * 6 + 2, 0)
                take(n * 6 + 3, 1)
                pick(2, k, turn)
                take(n * 6 + 4, 2)
                take(n * 6 + 5, 3)

            def rest(after):
                take(after * 6, 4)
                take(after * 6 + 1, 5)

            dve.wait_ge(order_ready, NSUB + 2)
            pick(0, 0, 0)
            with dve.Fori(0, NBLK // 2) as i:
                for k in range(2):
                    b = i * 2 + k
                    lo = dve.value_load(first[0:1, 0, bass.ds(b, 1)], min_val=0, max_val=NBLK * P)
                    turns = dve.value_load(first[0:1, 1, bass.ds(b, 1)], min_val=2, max_val=P)
                    most(lo, k, 0)
                    with dve.Fori(1, turns) as turn:
                        pick(0, k, turn)
                        rest(lo + turn)
                        most(lo + turn, k, turn)
                    dve.wait_ge(hot_ready[2], lo + turns)
                    dve.sem_inc(block_done, 1)
                    dve.wait_ge(order_ready, (b + 2) * NSUB + 2)
                    pick(0, 1 - k, 0)
                    rest(lo + turns)
            total = dve.value_load(first[0:1, 0, NBLK:NBLK + 1], min_val=0, max_val=NBLK * P)
            dve.wait_ge(row_used, total * 6 + 3)
            dve.sem_inc(best_done, 1)

    phase(maxima1)

    def write_rows(pe_in, ident, sb, ps, sem, tag, count):
        flat = sb(tag + "_flat", [P, count, P], F32)
        pF = ps(tag + "_pF", [P, count, SUB], F32)
        tr, cp, st = sem(tag + "_rtr"), sem(tag + "_rcp"), sem(tag + "_rst")

        def tensor(pe):
            for n in range(count):
                nc.tensor.transpose(pF[:T, n, :P], pe_in(n), ident[:]).then_inc(tr, 1)

        def scalar(act):
            for n in range(count):
                act.wait_ge(tr, n + 1)
                nc.scalar.copy(flat[:T, n], pF[:T, n, :P]).then_inc(cp, 1)

        def sync(sp, first_row):
            for n in range(count):
                sp.wait_ge(cp, n + 1)
                sp.dma_start(rows[first_row + n].rearrange("(t p) -> t p", p=P), flat[:T, n]).then_inc(st, 16)
            sp.wait_ge(st, 16 * count)

        return tensor, scalar, sync

    def finish1(sb, ps, sem, block):
        X, tmp, stat = sb("g_X", [P, T, P], F32), sb("g_tmp", [P, T, P], F32), sb("g_stat", [P, 3, T], F32)
        ident = sb("g_ident", [P, P], F32)
        best = sb("g_best", [P, N], F32)
        at = sb("g_at", [P, 2, P], F32)
        sc = sb("g_sc", [P, 5, T], F32)
        y = ps("g_y", [P, 4, SUB], F32)
        loaded, dch, var_ok, std_ok, x_ok, x_st, best_ok, tr, tr_used, sc_ok = (
            sem("g_" + n) for n in ("loaded", "dch", "var_ok", "std_ok", "x_ok", "x_st", "best_ok", "tr", "tr_used",
                                    "sc_ok"))
        rt, ra, rs = write_rows(lambda n: sc[:, 1], ident, sb, ps, sem, "g", 1)
        blk = block()

        @blk.sync
        def _(sp):
            sp.dma_start(best[:], best_d).then_inc(loaded, 16)
            sp.dma_start(ident[:], c_ident).then_inc(loaded, 16)
            sp.dma_start(X[:], x_1).then_inc(loaded, 16)
            sp.dma_start(at[:], attn2.rearrange("(k c) a -> a k c", k=2).partition_broadcast(P)
                         .rearrange("q a k c -> q (a k) c")).then_inc(loaded, 16)
            sp.wait_ge(x_ok, 1)
            sp.dma_start(x_2, X[:]).then_inc(x_st, 16)
            sp.wait_ge(sc_ok, 1)
            sp.dma_start(cols[:, :4], sc[:, :4]).then_inc(x_st, 16)
            rs(sp, 4)
            sp.wait_ge(x_st, 32)

        @blk.scalar
        def _(act):
            root(act, stat, var_ok, std_ok)
            ra(act)

        @blk.tensor
        def _(pe):
            pe.wait_ge(loaded, 64)
            pe.wait_ge(best_ok, 1)
            for t in range(T):
                if t >= 4:
                    pe.wait_ge(tr_used, t - 3)
                nc.tensor.transpose(y[:, t % 4, :P], best[:, t * P:(t + 1) * P], ident[:]).then_inc(tr, 1)
            pe.wait_ge(sc_ok, 1)
            rt(pe)

        @blk.vector
        def _(dve):
            link = chain(dve, dch)
            dve.wait_ge(loaded, 64)
            link(nc.vector.scalar_tensor_tensor(best[:], best[:], NEG / 2, best[:], ALU.is_gt, ALU.mult))
            dve.sem_inc(best_ok, 1)
            for t in range(T):
                dve.wait_ge(tr, t + 1)
                nc.vector.tensor_tensor(X[:, t], y[:, t % 4, :P], X[:, t], ALU.add).then_inc(tr_used, 1)
            dve.wait_ge(tr_used, T)
            normalise(dve, link, X, tmp, stat, var_ok, std_ok)
            dve.sem_inc(x_ok, 1)
            for k in range(2):
                link(nc.vector.tensor_tensor(tmp[:], X[:], at[:, k].unsqueeze(1).broadcast_to([P, T, P]), ALU.mult))
                link(nc.vector.tensor_reduce(sc[:, k], tmp[:], AX.X, ALU.add))
            link(nc.vector.tensor_scalar(sc[:, 2], sc[:, 1], SLOPE, None, ALU.mult))
            link(nc.vector.memset(sc[:, 3], 1.0))
            dve.sem_inc(sc_ok, 1)

    phase(finish1)

    def guard(tag, with_sum):
        def body(sb, ps, sem, block):
            ident = sb("ident", [P, P], F32)
            sc = sb("sc", [P, 5, T], F32)
            dall = sb("dall", [P, N], F32)
            neg = sb("neg", [P, 2, N], BF16)
            v = sb("v", [P, 2, N], F32)
            dn = sb("dn", [P, T], F32)
            zt = sb("zt", [P, 2, T], F32)
            m = sb("m", [P, T], F32)
            tot = sb("tot", [P, T], F32)
            gate = sb("gate", [P, T], F32)
            s12 = sb("s12", [P, 2, T], F32)
            tick = sb("tick", [P, 1], F32)
            dmax = sb("dmax", [P, 2], F32)
            dn_ok, off_ready, exp_ready, tot_ok, sum_ok = (
                sem(n) for n in ("dn_ok", "off_ready", "exp_ready", "tot_ok", "sum_ok"))
            total = sb("total", [P, 2], F32)
            off = sb("off", [P, 2, T], F32)
            up = sb("up", [P, 2, N if with_sum else 1], F32)
            loaded, dch, v_used, ln_in, ln_ok, s_ok, gate_st, step = (
                sem(n) for n in ("loaded", "dch", "v_used", "ln_in", "ln_ok", "s_ok", "gate_st", "step"))
            neg_in = [sem("neg_in0"), sem("neg_in1")]
            neg_used = [sem("neg_used0"), sem("neg_used1")]
            rt, ra, rs = write_rows(lambda n: s12[:, n], ident, sb, ps, sem, "w", 2)
            blk = block()

            @blk.sync
            def _(sp):
                sp.dma_start(ident[:], c_ident).then_inc(loaded, 16)
                sp.dma_start(sc[:, :4], cols[:, :4]).then_inc(loaded, 16)
                sp.dma_start(dall[:], rows[4].partition_broadcast(P)).then_inc(loaded, 16)
                with sp.Fori(0, T // 2) as i:
                    for b in range(2):
                        sp.wait_ge(neg_used[b], i + 1)
                        sp.dma_start(neg[:, b], negn[bass.ds(i * 2 + b, 1)].rearrange("a p n -> p (a n)")
                                     ).then_inc(neg_in[b], 16)
                rs(sp, 5)
                if with_sum:
                    sp.dma_start(cols[:, 4], gate[:]).then_inc(gate_st, 16)
                    sp.wait_ge(gate_st, 16)

            @blk.vector
            def _(dve):
                link = chain(dve, dch)
                for b in range(2):
                    dve.sem_inc(neg_used[b], 1)
                dve.wait_ge(loaded, 48)

                def largest(t, i, b):
                    one = bass.ds(t, 1)
                    dve.wait_ge(neg_in[b], i * 16 + 16)
                    if with_sum:
                        dve.wait_ge(v_used, t + 1)
                    nc.vector.memset(tick[:], 0.0)
                    nc.vector.tensor_tensor_reduce(out=v[:, b], in0=dall[:], in1=neg[:, b], scale=1.0,
                                                   scalar=4 * NEG, op0=ALU.add, op1=ALU.max,
                                                   accum_out=dmax[:, b:b + 1]).then_inc(neg_used[b], 1)
                    dve.wait_ge(neg_used[b], i + 2)
                    nc.vector.tensor_copy(dn[:, one], dmax[:, b:b + 1]).then_inc(dn_ok, 1)
                    if with_sum:
                        nc.vector.tensor_tensor(zt[:, 0, one], sc[:, 0, one], dmax[:, b:b + 1],
                                                ALU.add).then_inc(step, 1)
                        dve.wait_ge(step, t * 3 + 1)
                        nc.vector.tensor_scalar(zt[:, 1, one], zt[:, 0, one], SLOPE, None,
                                                ALU.mult).then_inc(step, 1)
                        dve.wait_ge(step, t * 3 + 2)
                        nc.vector.tensor_tensor(m[:, one], zt[:, 0, one], zt[:, 1, one],
                                                ALU.max).then_inc(step, 1)
                        dve.wait_ge(step, t * 3 + 3)
                        nc.vector.tensor_tensor(off[:, 0, one], sc[:, 0, one], m[:, one],
                                                ALU.subtract).then_inc(off_ready, 1)
                        nc.vector.scalar_tensor_tensor(off[:, 1, one], sc[:, 0, one], SLOPE, m[:, one], ALU.mult,
                                                       ALU.subtract).then_inc(off_ready, 1)

                def add_up(t, b):
                    dve.wait_ge(exp_ready, t * 2 + 2)
                    nc.vector.scalar_tensor_tensor(up[:, b], up[:, b], 0.0, v[:, b], ALU.max, ALU.max,
                                                   accum_out=total[:, b:b + 1]).then_inc(v_used, 1)
                    dve.wait_ge(v_used, t + 3)
                    nc.vector.tensor_copy(tot[:, bass.ds(t, 1)], total[:, b:b + 1]).then_inc(tot_ok, 1)

                def steps(i, first):
                    for b in range(2):
                        largest(i * 2 + b, i, b)
                        if with_sum and not (first and b == 0):
                            add_up(i * 2 + b - 1, 1 - b)

                if with_sum:
                    dve.sem_inc(v_used, 2)
                steps(0, True)
                with dve.Fori(1, T // 2) as i:
                    steps(i, False)
                if with_sum:
                    add_up(T - 1, 1)
                    dve.wait_ge(tot_ok, T)
                    dve.sem_inc(sum_ok, 1)
                dve.wait_ge(dn_ok, T)
                link(nc.vector.tensor_tensor(zt[:, 0], sc[:, 0], dn[:], ALU.add))
                link(nc.vector.tensor_scalar(zt[:, 1], zt[:, 0], SLOPE, None, ALU.mult))
                link(nc.vector.tensor_tensor(m[:], zt[:, 0], zt[:, 1], ALU.max))
                if with_sum:
                    dve.wait_ge(ln_ok, 1)
                    link(nc.vector.tensor_tensor(m[:], m[:], tot[:], ALU.add))
                link(nc.vector.tensor_tensor(s12[:, 0], sc[:, 0], m[:], ALU.subtract))
                link(nc.vector.scalar_tensor_tensor(s12[:, 1], sc[:, 0], SLOPE, m[:], ALU.mult, ALU.subtract))
                dve.sem_inc(s_ok, 1)

            @blk.tensor
            def _(pe):
                pe.wait_ge(loaded, 48)
                pe.wait_ge(s_ok, 1)
                rt(pe)

            @blk.scalar
            def _(act):
                if with_sum:
                    with act.Fori(0, T // 2) as i:
                        for b in range(2):
                            t = i * 2 + b
                            one = bass.ds(t, 1)
                            act.wait_ge(off_ready, t * 2 + 2)
                            act.wait_ge(v_used, t + 1)
                            nc.scalar.activation(up[:, b], v[:, b], ACT.Exp, bias=off[:, 0, one]).then_inc(
                                exp_ready, 1)
                            nc.scalar.activation(v[:, b], v[:, b], ACT.Exp, bias=off[:, 1, one],
                                                 scale=SLOPE).then_inc(exp_ready, 1)
                    act.wait_ge(sum_ok, 1)
                    nc.scalar.activation(tot[:], tot[:], ACT.Ln).then_inc(ln_in, 1)
                    act.wait_ge(ln_in, 1)
                    nc.scalar.activation(gate[:], tot[:], ACT.Exp, scale=-1.0).then_inc(ln_ok, 1)
                    act.wait_ge(ln_ok, 1)
                ra(act)

        phase(body)

    def attend(tag, values, width, threshold):
        def body(sb, ps, sem, block):
            NP = T // 4
            vals = sb("vals", [P, T, P], F32)
            rhs = sb("rhs", [P, T, P + 1], F32)
            sc = sb("sc", [P, 5, T], F32)
            s12 = sb("s12", [P, 2, CW], F32)
            mask = sb("mask", [P, 2, CT, 2, P], BF16)
            low = sb("low", [P, 2, CW], F32)
            arg = sb("arg", [P, 2, CW], F32)
            prob = sb("prob", [P, 2, CW], F32)
            wts = sb("wts", [P, 2, CW], F32)
            kept = sb("kept", [P, 2, CW], F32)
            maskv = sb("maskv", [P, T, 1], BF16)
            zero = sb("zero", [P, SUB], BF16)
            st = sb("st", [P, CT, P + 1], F32)
            acc = ps("acc", [P, CT, SUB], F32)
            loaded, rhs_ok, s_in, s_used, low_ready, arg_ready, prob_ready, w_ready, k_ready, k_used = (
                sem(n) for n in ("loaded", "rhs_ok", "s_in", "s_used", "low_ready", "arg_ready", "prob_ready",
                                 "w_ready", "k_ready", "k_used"))
            acc_done, acc_copied, st_out = sem("acc_done"), sem("acc_copied"), sem("st_out")
            mask_in = [sem("mask_in0"), sem("mask_in1")]
            mask_used = [sem("mask_used0"), sem("mask_used1")]
            blk = block()
            units = [(b, k) for b in range(2) for k in range(2)]

            @blk.sync
            def _(sp):
                sp.dma_start(vals[:], values).then_inc(loaded, 16)
                sp.dma_start(sc[:, :4], cols[:, :4]).then_inc(loaded, 16)
                with sp.Fori(0, NC) as ch:
                    sp.wait_ge(s_used, ch + 1)
                    sp.dma_start(s12[:], rows[5:7, bass.ds(ch * CW, CW)].partition_broadcast(P)).then_inc(s_in, 16)
                    with sp.Fori(0, NP) as i:
                        for b in range(2):
                            sp.wait_ge(mask_used[b], ch * NP + i + 1)
                            sp.dma_start(mask[:, b].rearrange("p t k c -> p t (k c)"),
                                         maskT[bass.ds(ch * CT, CT), :, bass.ds(i * 4 + b * 2, 2), :]
                                         .rearrange("t p b c -> p t (b c)")).then_inc(mask_in[b], 16)

            def chunks(eng, before, first_step, second_step, after):
                with eng.Fori(0, NC) as ch:
                    before(ch)

                    def steps(i, first):
                        for u in range(4):
                            n = (ch * NP + i) * 4 + u
                            first_step(n, i * 4 + u, u)
                            if not (first and u == 0):
                                second_step(n - 1, (u - 1) % 4)
                    steps(0, True)
                    with eng.Fori(1, NP) as i:
                        steps(i, False)
                    second_step((ch + 1) * T - 1, 3)
                    after(ch)

            @blk.scalar
            def _(act):
                act.sem_inc(acc_copied, CT)
                act.sem_inc(st_out, 16)
                act.sem_inc(prob_ready, 2)
                act.wait_ge(loaded, 32)

                def lower(n, j, u):
                    act.wait_ge(arg_ready, n + 1)
                    nc.scalar.activation(low[:, u % 2], s12[:, 1], ACT.Identity,
                                         bias=sc[:, 2, bass.ds(j, 1)]).then_inc(low_ready, 1)

                def exps(n, u):
                    act.wait_ge(arg_ready, n + 3)
                    act.wait_ge(w_ready, n + 1)
                    nc.scalar.activation(prob[:, u % 2], arg[:, u % 2], ACT.Exp).then_inc(prob_ready, 1)

                def copy_out(ch):
                    act.wait_ge(st_out, ch * 16 + 16)
                    for t in range(CT):
                        act.wait_ge(acc_done, ch * CT + t + 1)
                        nc.scalar.copy(st[:, t], acc[:, t, :P + 1]).then_inc(acc_copied, 1)
                    act.wait_ge(acc_copied, (ch + 2) * CT)
                    act.dma_start(sums[bass.ds(ch * CT, CT), :, :P + 1].rearrange("t p c -> p t c"),
                                  st[:]).then_inc(st_out, 16)

                chunks(act, lambda ch: act.wait_ge(s_in, ch * 16 + 16), lower, exps, copy_out)
                act.wait_ge(st_out, 16 * NC + 16)

            @blk.vector
            def _(dve):
                dve.wait_ge(loaded, 32)
                nc.vector.memset(zero[:], 0.0)
                nc.vector.tensor_copy(rhs[:, :, :P], vals[:])
                nc.vector.tensor_copy(maskv[:], sc[:, 3].unsqueeze(2))
                nc.vector.memset(rhs[:, :, P:], 1.0).then_inc(rhs_ok, 1)
                dve.sem_inc(s_used, 1)
                dve.sem_inc(arg_ready, 2)
                dve.sem_inc(w_ready, 2)

                def larger(n, j, u):
                    dve.wait_ge(low_ready, n + 1)
                    dve.wait_ge(prob_ready, n + 1)
                    nc.vector.scalar_tensor_tensor(arg[:, u % 2], s12[:, 0],
                                                   sc[:, 1, bass.ds(j, 1)], low[:, u % 2],
                                                   ALU.add, ALU.max).then_inc(arg_ready, 1)

                def masked(n, u):
                    b, k = units[u]
                    dve.wait_ge(prob_ready, n + 3)
                    if u % 2 == 0:
                        dve.wait_ge(mask_in[b], (n - u + 4) * 4)
                    dve.wait_ge(k_used, n + 1)
                    out_, ready = (wts, w_ready)
                    nc.vector.scalar_tensor_tensor(out_[:, u % 2].rearrange("p (t c) -> p t c", c=P),
                                                   prob[:, u % 2].rearrange("p (t c) -> p t c", c=P), 2.0,
                                                   mask[:, b, :, k], ALU.min, ALU.mult).then_inc(w_ready, 1)
                    if threshold is not None:
                        dve.wait_ge(w_ready, n + 3)
                        nc.vector.scalar_tensor_tensor(kept[:, u % 2], wts[:, u % 2], threshold, wts[:, u % 2],
                                                       ALU.is_ge, ALU.mult).then_inc(k_ready, 1)

                def done(ch):
                    dve.sem_inc(s_used, 1)

                chunks(dve, lambda ch: dve.wait_ge(s_in, ch * 16 + 16), larger, masked, done)

            @blk.tensor
            def _(pe):
                pe.sem_inc(k_used, 2)
                for b in range(2):
                    pe.sem_inc(mask_used[b], 1)
                pe.wait_ge(rhs_ok, 1)
                src = wts if threshold is None else kept
                with pe.Fori(0, NC) as ch:
                    for t in range(CT):
                        pe.wait_ge(acc_copied, ch * CT + t + 1)
                        nc.tensor.matmul(acc[:, t, :P + 1], zero[:, :P], zero[:, :P + 1], start=True, stop=False)
                    with pe.Fori(0, NP) as i:
                        for u, (b, k) in enumerate(units):
                            n = (ch * NP + i) * 4 + u
                            if threshold is not None:
                                pe.wait_ge(mask_in[b], (n - u + 4) * 4)
                            if threshold is not None:
                                for t in range(CT):
                                    nc.tensor.matmul(acc[:, t, P:P + 1], mask[:, b, t, k],
                                                     maskv[:, bass.ds(i * 4 + u, 1)].rearrange("p a c -> p (a c)"),
                                                     start=False, stop=False, skip_group_check=True)
                            if threshold is None:
                                pe.wait_ge(w_ready, n + 3)
                            else:
                                pe.wait_ge(k_ready, n + 1)
                            for t in range(CT):
                                last = nc.tensor.matmul(
                                    acc[:, t, :width], src[:, u % 2, t * P:(t + 1) * P],
                                    rhs[:, bass.ds(i * 4 + u, 1), :width].rearrange("p a c -> p (a c)"),
                                    start=False, stop=False, skip_group_check=True)
                            last.then_inc(k_used, 1)
                            if k == 1:
                                pe.wait_ge(k_used, n + 3)
                                pe.sem_inc(mask_used[b], 1)
                    for t in range(CT):
                        nc.tensor.matmul(acc[:, t, :P + 1], zero[:, :P], zero[:, :P + 1], start=False,
                                         stop=True).then_inc(acc_done, 1)

        phase(body)

    guard("g2", False)
    attend("t2", x_2, P + 1, None)

    def finish2(sb, ps, sem, block):
        ident = ident_of["h"] = sb("h_ident", [P, P], F32)
        X, tmp, stat = sb("h_X", [P, T, P], F32), sb("h_tmp", [P, T, P], F32), sb("h_stat", [P, 3, T], F32)
        U = sb("h_U", [P, T, P + 1], F32)
        W = sb("h_W", [P, P], F32)
        h = sb("h_h", [P, T, P], F32)
        at = sb("h_at", [P, 2, P], F32)
        sc = sb("h_sc", [P, 5, T], F32)
        loaded, dch, var_ok, std_ok, x_ok, x_st, sc_ok = (
            sem("h_" + n) for n in ("loaded", "dch", "var_ok", "std_ok", "x_ok", "x_st", "sc_ok"))
        rt, ra, rs = write_rows(lambda n: sc[:, 1], ident, sb, ps, sem, "h", 1)
        tensor, scalar, vector = project(None, sem, ps, sb, "h", lambda t: X[:, t], W, P, h, (loaded, 80), (x_ok, 1))
        blk = block()

        @blk.sync
        def _(sp):
            sp.dma_start(U[:], sums[:, :, :P + 1].rearrange("t p c -> p t c")).then_inc(loaded, 16)
            sp.dma_start(ident[:], c_ident).then_inc(loaded, 16)
            sp.dma_start(X[:], x_2).then_inc(loaded, 16)
            sp.dma_start(W[:], W3).then_inc(loaded, 16)
            sp.dma_start(at[:], a3.rearrange("(k c) a -> a k c", k=2).partition_broadcast(P)
                         .rearrange("q a k c -> q (a k) c")).then_inc(loaded, 16)
            sp.wait_ge(x_ok, 1)
            sp.dma_start(x_3, X[:]).then_inc(x_st, 16)
            sp.wait_ge(sc_ok, 1)
            sp.dma_start(cols[:, :4], sc[:, :4]).then_inc(x_st, 16)
            sp.dma_start(h_3, h[:]).then_inc(x_st, 16)
            rs(sp, 4)
            sp.wait_ge(x_st, 48)

        @blk.scalar
        def _(act):
            root(act, stat, var_ok, std_ok)
            scalar(act)
            ra(act)

        @blk.tensor
        def _(pe):
            tensor(pe)
            pe.wait_ge(sc_ok, 1)
            rt(pe)

        @blk.vector
        def _(dve):
            link = chain(dve, dch)
            dve.wait_ge(loaded, 80)
            link(nc.vector.reciprocal(stat[:, 0], U[:, :, P]))
            link(nc.vector.tensor_tensor(tmp[:], U[:, :, :P], stat[:, 0].unsqueeze(2).broadcast_to([P, T, P]),
                                         ALU.mult))
            link(nc.vector.tensor_tensor(X[:], X[:], tmp[:], ALU.add))
            normalise(dve, link, X, tmp, stat, var_ok, std_ok)
            dve.sem_inc(x_ok, 1)
            vector(dve)
            for k in range(2):
                link(nc.vector.tensor_tensor(tmp[:], h[:], at[:, k].unsqueeze(1).broadcast_to([P, T, P]), ALU.mult))
                link(nc.vector.tensor_reduce(sc[:, k], tmp[:], AX.X, ALU.add))
            link(nc.vector.tensor_reduce(stat[:, 0], h[:], AX.X, ALU.add))
            link(nc.vector.tensor_scalar(sc[:, 3], stat[:, 0], 0.0, None, ALU.not_equal))
            link(nc.vector.tensor_scalar(stat[:, 1], sc[:, 3], 1.0, -NEG, ALU.subtract, ALU.mult))
            link(nc.vector.tensor_tensor(sc[:, 1], sc[:, 1], stat[:, 1], ALU.add))
            link(nc.vector.tensor_scalar(sc[:, 2], sc[:, 1], SLOPE, None, ALU.mult))
            dve.sem_inc(sc_ok, 1)

    phase(finish2)
    guard("g3", True)
    attend("t3", h_3, P, THR)

    def finish3(sb, ps, sem, block):
        X, tmp, stat = sb("X", [P, T, P], F32), sb("tmp", [P, T, P], F32), sb("stat", [P, 3, T], F32)
        U = sb("U", [P, T, P + 1], F32)
        h = sb("h", [P, T, P], F32)
        sc = sb("sc", [P, 5, T], F32)
        loaded, dch, var_ok, std_ok, x_ok, x_st, low_ok, exp_ok = (
            sem(n) for n in ("loaded", "dch", "var_ok", "std_ok", "x_ok", "x_st", "low_ok", "exp_ok"))
        blk = block()

        @blk.sync
        def _(sp):
            sp.dma_start(U[:], sums[:, :, :P + 1].rearrange("t p c -> p t c")).then_inc(loaded, 16)
            sp.dma_start(X[:], x_3).then_inc(loaded, 16)
            sp.dma_start(h[:], h_3).then_inc(loaded, 16)
            sp.dma_start(sc[:, :5], cols[:, :5]).then_inc(loaded, 16)
            sp.wait_ge(x_ok, 1)
            sp.dma_start(tiles(out), X[:]).then_inc(x_st, 16)
            sp.wait_ge(x_st, 16)

        @blk.scalar
        def _(act):
            act.wait_ge(low_ok, 1)
            nc.scalar.activation(tmp[:], tmp[:], ACT.Exp).then_inc(exp_ok, 1)
            root(act, stat, var_ok, std_ok)

        @blk.vector
        def _(dve):
            link = chain(dve, dch)
            dve.wait_ge(loaded, 64)
            link(nc.vector.scalar_tensor_tensor(stat[:, 0], sc[:, 4], THR, U[:, :, P], ALU.is_gt, ALU.mult))
            link(nc.vector.tensor_tensor(U[:, :, :P], U[:, :, :P], stat[:, 0].unsqueeze(2).broadcast_to([P, T, P]),
                                         ALU.mult))
            link(nc.vector.tensor_tensor(h[:], h[:], U[:, :, :P], ALU.add))
            link(nc.vector.tensor_scalar(tmp[:], h[:], 0.0, None, ALU.min))
            dve.sem_inc(low_ok, 1)
            link(nc.vector.tensor_scalar(h[:], h[:], 0.0, -1.0, ALU.max, ALU.add))
            link(nc.vector.tensor_tensor(X[:], X[:], h[:], ALU.add))
            dve.wait_ge(exp_ok, 1)
            link(nc.vector.tensor_tensor(X[:], X[:], tmp[:], ALU.add))
            normalise(dve, link, X, tmp, stat, var_ok, std_ok)
            dve.sem_inc(x_ok, 1)

    phase(finish3)


_INS = ["x", "adj", "L0_gnn_W", "L0_gnn_attn_src", "L0_gnn_attn_dst", "L2_gnn_attn", "L3_gnn_W", "L3_gnn_a"]


def kernel(**inputs):
    import concourse.bacc as bacc
    from concourse.bass_utils import run_bass_kernel_spmd

    nc = bacc.Bacc("TRN2", target_bir_lowering=False, num_devices=1)
    arrays, args = {}, []
    for name, a in [(n, inputs[n]) for n in _INS] + sorted(constants().items()):
        a = np.ascontiguousarray(a)
        arrays[f"in_{name}"] = a
        args.append(nc.dram_tensor(f"in_{name}", a.shape, mybir.dt.from_np(a.dtype), kind="ExternalInput").ap())
    n = inputs["x"].shape[0]
    out = nc.dram_tensor("out", (n, P), F32, kind="ExternalOutput").ap()
    by_name = dict(zip(_INS + sorted(constants()), args))
    build(nc, *(by_name[k] for k in _INS), by_name["c_half"], by_name["c_ident"],
          by_name["c_prefix"], by_name["c_slot"], out)
    r = run_bass_kernel_spmd(nc, [arrays], core_ids=[0])
    return r.results[0]["out"]
```
